# Optimizing a Trainium2 kernel written in Bass

```python
import numpy as np
import jax
import jax.numpy as jnp

def _softmax(x, axis=-1):
    return jax.nn.softmax(x, axis=axis)

def _gelu(x):
    return jax.nn.gelu(x, approximate=True)

def _silu(x):
    return jax.nn.silu(x)

def _sigmoid(x):
    return jax.nn.sigmoid(x)

def _layernorm(x, axis=-1, eps=1e-05):
    m = jnp.mean(x, axis=axis, keepdims=True)
    v = jnp.var(x, axis=axis, keepdims=True)
    return (x - m) / jnp.sqrt(v + eps)

def _scatter_add(tgt, idx, src, axis=0):
    return tgt.at[idx].add(src)

def _segment_sum(src, seg, n):
    return jax.ops.segment_sum(src, seg, n)
kernel_name = 'mk_recurrent_d2_jaxref_r8_3df33e'

def setup_inputs(seed: int=0):
    np.random.seed(seed)
    _w = jnp.asarray

    def _L0_attn_setup():
        import jax, jax.numpy as jnp
        import numpy as np
        N_HEAD = 16
        key = jax.random.key(seed)
        k1, k2, k3, k4, k5 = jax.random.split(key, 5)
        B, T, C = (8, 256, 128)
        hs = C // N_HEAD
        return {'ids': jax.random.normal(k1, (B, T, C), dtype=jnp.float32), 'qkv_w': jax.random.normal(k2, (3 * hs, C), dtype=jnp.float32) * C ** (-0.5), 'qkv_b': jax.random.normal(k3, (3 * hs,), dtype=jnp.float32) * 0.02, 'proj_w': jax.random.normal(k4, (C, C), dtype=jnp.float32) * C ** (-0.5), 'proj_b': jax.random.normal(k5, (C,), dtype=jnp.float32) * 0.02}
    _L0_attn_in = _L0_attn_setup()

    def _L0_ffn_setup():
        import jax, jax.numpy as jnp
        import numpy as np
        D_MODEL = 128
        HIDDEN = 128
        NUM_EXPERTS = 8
        TOP_K = 2
        key = jax.random.key(seed)
        ks = jax.random.split(key, 10)
        s = 0.02
        return {'x': jax.random.normal(ks[0], (2, 256, D_MODEL), dtype=jnp.float32), 'gate_w': jax.random.normal(ks[1], (NUM_EXPERTS, D_MODEL), dtype=jnp.float32) * s, 'up_w': jax.random.normal(ks[2], (NUM_EXPERTS, D_MODEL, HIDDEN), dtype=jnp.float32) * s, 'up_b': jnp.zeros((NUM_EXPERTS, HIDDEN), dtype=jnp.float32), 'down_w': jax.random.normal(ks[3], (NUM_EXPERTS, HIDDEN, D_MODEL), dtype=jnp.float32) * s, 'down_b': jnp.zeros((NUM_EXPERTS, D_MODEL), dtype=jnp.float32), 'sh_up_w': jax.random.normal(ks[4], (D_MODEL, HIDDEN), dtype=jnp.float32) * s, 'sh_up_b': jnp.zeros((HIDDEN,), dtype=jnp.float32), 'sh_down_w': jax.random.normal(ks[5], (HIDDEN, D_MODEL), dtype=jnp.float32) * s, 'sh_down_b': jnp.zeros((D_MODEL,), dtype=jnp.float32)}
    _L0_ffn_in = _L0_ffn_setup()

    def _L1_attn_setup():
        import jax, jax.numpy as jnp
        import numpy as np
        N_HEAD = 16
        key = jax.random.key(seed)
        ks = jax.random.split(key, 10)
        C = 128
        B, T = (4, 1024)
        s = 1.0 / np.sqrt(C)
        return {'x': jax.random.normal(ks[0], (B, T, C), dtype=jnp.float32), 'Wq': jax.random.normal(ks[1], (C, C), dtype=jnp.float32) * s, 'bq': jax.random.normal(ks[2], (C,), dtype=jnp.float32) * s, 'Wk': jax.random.normal(ks[3], (C, C), dtype=jnp.float32) * s, 'bk': jax.random.normal(ks[4], (C,), dtype=jnp.float32) * s, 'Wv': jax.random.normal(ks[5], (C, C), dtype=jnp.float32) * s, 'bv': jax.random.normal(ks[6], (C,), dtype=jnp.float32) * s, 'Wp': jax.random.normal(ks[7], (C, C), dtype=jnp.float32) * s, 'bp': jax.random.normal(ks[8], (C,), dtype=jnp.float32) * s}
    _L1_attn_in = _L1_attn_setup()

    def _L1_ffn_setup():
        import jax, jax.numpy as jnp
        import numpy as np
        B, S, H, E = (8, 512, 128, 8)
        TEMPERATURE = 1.0
        key = jax.random.key(seed)
        ks = jax.random.split(key, 7)
        s_h = 1.0 / np.sqrt(H).astype(np.float32)
        s_h2 = 1.0 / np.sqrt(H // 2).astype(np.float32)
        return {'hidden_states': jax.random.normal(ks[0], (B, S, H), jnp.float32), 'W1': jax.random.normal(ks[1], (H, H // 2), jnp.float32) * s_h, 'b1': jnp.zeros((H // 2,), jnp.float32), 'W2': jax.random.normal(ks[2], (H // 2, E), jnp.float32) * s_h2, 'b2': jnp.zeros((E,), jnp.float32), 'expert_W': jax.random.normal(ks[3], (E, H, H), jnp.float32) * s_h, 'expert_b': jax.random.normal(ks[4], (E, H), jnp.float32)}
    _L1_ffn_in = _L1_ffn_setup()
    _d = {'L0_attn_ids': _L0_attn_in['ids'], 'L0_attn_qkv_w': _L0_attn_in['qkv_w'], 'L0_attn_qkv_b': _L0_attn_in['qkv_b'], 'L0_attn_proj_w': _L0_attn_in['proj_w'], 'L0_attn_proj_b': _L0_attn_in['proj_b'], 'L0_ffn_gate_w': _L0_ffn_in['gate_w'], 'L0_ffn_up_w': _L0_ffn_in['up_w'], 'L0_ffn_up_b': _L0_ffn_in['up_b'], 'L0_ffn_down_w': _L0_ffn_in['down_w'], 'L0_ffn_down_b': _L0_ffn_in['down_b'], 'L0_ffn_sh_up_w': _L0_ffn_in['sh_up_w'], 'L0_ffn_sh_up_b': _L0_ffn_in['sh_up_b'], 'L0_ffn_sh_down_w': _L0_ffn_in['sh_down_w'], 'L0_ffn_sh_down_b': _L0_ffn_in['sh_down_b'], 'L1_attn_Wq': _L1_attn_in['Wq'], 'L1_attn_bq': _L1_attn_in['bq'], 'L1_attn_Wk': _L1_attn_in['Wk'], 'L1_attn_bk': _L1_attn_in['bk'], 'L1_attn_Wv': _L1_attn_in['Wv'], 'L1_attn_bv': _L1_attn_in['bv'], 'L1_attn_Wp': _L1_attn_in['Wp'], 'L1_attn_bp': _L1_attn_in['bp'], 'L1_ffn_W1': _L1_ffn_in['W1'], 'L1_ffn_b1': _L1_ffn_in['b1'], 'L1_ffn_W2': _L1_ffn_in['W2'], 'L1_ffn_b2': _L1_ffn_in['b2'], 'L1_ffn_expert_W': _L1_ffn_in['expert_W'], 'L1_ffn_expert_b': _L1_ffn_in['expert_b']}
    _x0 = _d['L0_attn_ids']
    _d['L0_attn_ids'] = jax.random.normal(jax.random.fold_in(jax.random.key(seed), 1), (8, 512, 128), dtype=_x0.dtype)
    del _x0
    return _d

def reference(L0_attn_ids, L0_attn_qkv_w, L0_attn_qkv_b, L0_attn_proj_w, L0_attn_proj_b, L0_ffn_gate_w, L0_ffn_up_w, L0_ffn_up_b, L0_ffn_down_w, L0_ffn_down_b, L0_ffn_sh_up_w, L0_ffn_sh_up_b, L0_ffn_sh_down_w, L0_ffn_sh_down_b, L1_attn_Wq, L1_attn_bq, L1_attn_Wk, L1_attn_bk, L1_attn_Wv, L1_attn_bv, L1_attn_Wp, L1_attn_bp, L1_ffn_W1, L1_ffn_b1, L1_ffn_W2, L1_ffn_b2, L1_ffn_expert_W, L1_ffn_expert_b):

    def _L0_attn_ref(ids, qkv_w, qkv_b, proj_w, proj_b):
        import jax, jax.numpy as jnp
        import numpy as np
        N_HEAD = 16
        B, T, C = ids.shape
        hs = qkv_w.shape[0] // 3
        qkv = ids @ qkv_w.T + qkv_b
        q, k, v = jnp.split(qkv, 3, axis=-1)
        wei = jnp.einsum('btd,bsd->bts', q, k)
        tril = jnp.tril(jnp.ones((T, T), dtype=bool))
        wei = jnp.where(tril, wei, jnp.float32(0.0))
        out_h = jnp.einsum('bts,bsd->btd', wei, v)
        out = jnp.tile(out_h, (1, 1, N_HEAD))
        return out @ proj_w.T + proj_b

    def _L0_ffn_ref(x, gate_w, up_w, up_b, down_w, down_b, sh_up_w, sh_up_b, sh_down_w, sh_down_b):
        import jax, jax.numpy as jnp
        import numpy as np
        D_MODEL = 128
        HIDDEN = 128
        NUM_EXPERTS = 8
        TOP_K = 2
        b, s, d = x.shape
        xf = x.reshape(-1, d)
        shared = jax.nn.silu(x @ sh_up_w + sh_up_b) @ sh_down_w + sh_down_b
        logits = xf @ gate_w.T
        scores = jax.nn.softmax(logits, axis=-1)
        topk_w, topk_i = jax.lax.top_k(scores, TOP_K)
        topk_w = topk_w / (topk_w.sum(axis=-1, keepdims=True) + 1e-20)
        comb = (jax.nn.one_hot(topk_i, NUM_EXPERTS, dtype=xf.dtype) * topk_w[..., None]).sum(axis=1)
        h = jnp.einsum('nd,edh->neh', xf, up_w) + up_b
        h = jax.nn.silu(h)
        ye = jnp.einsum('neh,ehd->ned', h, down_w) + down_b
        y = jnp.einsum('ned,ne->nd', ye, comb).reshape(b, s, d)
        return y + shared

    def _L1_attn_ref(x, Wq, bq, Wk, bk, Wv, bv, Wp, bp):
        import jax, jax.numpy as jnp
        import numpy as np
        N_HEAD = 16
        B, T, C = x.shape
        H = N_HEAD
        d = C // H

        def proj_heads(W, b):
            h = x @ W.T + b
            return h.reshape(B, T, H, d).transpose(0, 2, 1, 3)
        q = proj_heads(Wq, bq)
        k = proj_heads(Wk, bk)
        v = proj_heads(Wv, bv)
        q = jax.nn.softmax(q, axis=-1)
        k = jax.nn.softmax(k, axis=-1)
        k_sum = k.sum(axis=-2, keepdims=True)
        D_inv = 1.0 / (q * k_sum).sum(axis=-1, keepdims=True)
        context = jnp.einsum('bhnd,bhnv->bhdv', k, v)
        out = jnp.einsum('bhqd,bhdv->bhqv', q, context)
        out = out * D_inv + q
        out = out.transpose(0, 2, 1, 3).reshape(B, T, C)
        return out @ Wp.T + bp

    def _L1_ffn_ref(hidden_states, W1, b1, W2, b2, expert_W, expert_b):
        import jax, jax.numpy as jnp
        import numpy as np
        B, S, H, E = (8, 512, 128, 8)
        TEMPERATURE = 1.0
        h = jax.nn.relu(jnp.einsum('bsh,hf->bsf', hidden_states, W1) + b1)
        logits = jnp.einsum('bsf,fe->bse', h, W2) + b2
        probs = jax.nn.softmax(logits / TEMPERATURE, axis=-1)
        sel = jnp.argmax(probs, axis=-1)
        out = jnp.zeros_like(hidden_states)
        for e in range(E):
            mask = (sel == e)[..., None].astype(hidden_states.dtype)
            xe = hidden_states * mask
            ye = jnp.einsum('bsh,hd->bsd', xe, expert_W[e]) + expert_b[e]
            out = out + ye * mask
        return out
    x = L0_attn_ids
    xn = _layernorm(x, axis=-1)
    s = _L0_attn_ref(xn, L0_attn_qkv_w, L0_attn_qkv_b, L0_attn_proj_w, L0_attn_proj_b)
    g = _silu(_L0_ffn_ref(xn, L0_ffn_gate_w, L0_ffn_up_w, L0_ffn_up_b, L0_ffn_down_w, L0_ffn_down_b, L0_ffn_sh_up_w, L0_ffn_sh_up_b, L0_ffn_sh_down_w, L0_ffn_sh_down_b))
    x = x + s * g
    xn = _layernorm(x, axis=-1)
    s = _L1_attn_ref(xn, L1_attn_Wq, L1_attn_bq, L1_attn_Wk, L1_attn_bk, L1_attn_Wv, L1_attn_bv, L1_attn_Wp, L1_attn_bp)
    g = _silu(_L1_ffn_ref(xn, L1_ffn_W1, L1_ffn_b1, L1_ffn_W2, L1_ffn_b2, L1_ffn_expert_W, L1_ffn_expert_b))
    x = x + s * g
    return x

_drawn_inputs = setup_inputs


def setup_inputs(seed=0):
    import zlib

    import numpy as np

    out = dict(_drawn_inputs(seed))
    spreads = {'L0_ffn_up_b': (0.0, 0.1),
     'L0_ffn_down_b': (0.0, 0.1),
     'L0_ffn_sh_up_b': (0.0, 0.1),
     'L0_ffn_sh_down_b': (0.0, 0.1),
     'L1_ffn_b1': (0.0, 0.8),
     'L1_ffn_b2': (0.0, 0.728)}
    factors = {'L0_attn_proj_b': 200.0,
     'L1_attn_Wq': 3.107,
     'L1_attn_bq': 30.649,
     'L1_attn_Wk': 5.339,
     'L1_attn_bk': 64.0,
     'L1_attn_bv': 4.993,
     'L1_attn_bp': 4.728}
    for name, (base, spread) in spreads.items():
        noise = np.random.default_rng([zlib.crc32(name.encode()), seed]).standard_normal(out[name].shape)
        drawn = base * np.exp(spread * noise) if base else spread * noise
        out[name] = jnp.asarray(drawn.astype(out[name].dtype))
    for name, factor in factors.items():
        out[name] = (out[name] * factor).astype(out[name].dtype)
    return out
```

```python
from contextlib import ExitStack

import numpy as np

import concourse.bass as bass
from concourse import mybir

ALU = mybir.AluOpType
ACT = mybir.ActivationFunctionType
AX_X = mybir.AxisListType.X
F32 = mybir.dt.float32
FR = mybir.dt.float32r
U32 = mybir.dt.uint32

P = 128
C = 128
B, T = 8, 512
NT = T // P
E = 8
EX = E + 1
HS = 8
NH = C // HS
F1 = C // 2
EPS = 1e-5
TINY = 1e-20

Q_ROW, K_ROW, V_ROW, G_ROW = 0, 32, 64, 96
PR = G_ROW + E
KVG = PR - K_ROW
K_COL, V_COL, G_COL = 0, V_ROW - K_ROW, G_ROW - K_ROW

C_ID, C_TRI, C_BLK, C_IND, C_FOLD, C_IOTA, C_M2, C_M24, C_ONE = 0, 128, 256, 384, 400, 408, 416, 417, 418
C_SEL = 546
NCONST = C_SEL + E * C
V_UP, V_PR, V_PROJ, V_SHD, V_B1 = 0, EX, EX + 1, EX + 2, EX + 3
NVEC = EX + 4
R_QKV, R_EXP, R_PROJ = 0, 3 * C, 3 * C + E * C
NROW = R_PROJ + NT * C


def build_program(nc, x, consts, w_pr, w_up, w_dn, w_pj, b_dn, vecs, rows, w_qkv, w_ex, w_p1, w_r1, w_r2, out):
    with ExitStack() as ctx:
        def sb(name, shape, dt=F32):
            return ctx.enter_context(nc.sbuf_tensor(name, shape, dt))

        def sem(name):
            return ctx.enter_context(nc.semaphore(name))

        cst = sb("cst", [P, NCONST])
        vec = sb("vec", [P, NVEC])
        row = sb("row", [2, NROW])
        row_r = sb("row_r", [2, NROW], FR)
        row_s = sb("row_s", [2, NROW], FR)
        bdn = sb("bdn", [3 * E, C])
        bdn_r = sb("bdn_r", [3 * E, C], FR)
        bdn_s = sb("bdn_s", [3 * E, C], FR)
        ones_s = sb("ones_s", [2, P], FR)
        sel_s = sb("sel_s", [2 * E, E * C], FR)
        wpr, wpr_h, wpr_l = sb("wpr", [P, PR]), sb("wpr_h", [P, PR], FR), sb("wpr_l", [P, PR], FR)
        wup, wup_h, wup_l = sb("wup", [P, EX * C]), sb("wup_h", [P, EX * C], FR), sb("wup_l", [P, EX * C], FR)
        wdn, wdn_h, wdn_l = sb("wdn", [P, EX * C]), sb("wdn_h", [P, EX * C], FR), sb("wdn_l", [P, EX * C], FR)
        wqkv, wqkv_h, wqkv_l = sb("wqkv", [P, 3 * C]), sb("wqkv_h", [P, 3 * C], FR), sb("wqkv_l", [P, 3 * C], FR)
        wex, wex_h, wex_l = sb("wex", [P, E * C]), sb("wex_h", [P, E * C], FR), sb("wex_l", [P, E * C], FR)
        wr1, wr1_h, wr1_l = sb("wr1", [P, F1]), sb("wr1_h", [P, F1], FR), sb("wr1_l", [P, F1], FR)
        wpj, wsum = sb("wpj", [P, C]), sb("wsum", [HS, C])
        wp1 = sb("wp1", [P, C])
        wr2 = sb("wr2", [F1 + 1, E])
        mhalf = sb("mhalf", [P, NT])

        xs = sb("xs", [P, B, NT, C])
        st0, mv0, ve0, rs0 = sb("st0", [P, NT, 6]), sb("mv0", [P, NT, 2]), sb("ve0", [P, NT]), sb("rs0", [P, NT])
        xn0 = sb("xn0", [P, NT, C])
        xh0, xl0 = sb("xh0", [P, T], FR), sb("xl0", [P, T], FR)
        prj, kT = sb("prj", [PR, T]), sb("kT", [HS, T])
        kvg = sb("kvg", [P, NT, KVG])
        wm = sb("wm", [P, T])
        st_sum = sb("st_sum", [HS, (NT - 1) * HS])
        ohT = sb("ohT", [HS, T])
        sTb = sb("sTb", [P, T])
        top8, topi = sb("top8", [P, NT, E]), sb("topi", [P, NT, E], U32)
        topf = sb("topf", [P, NT, 2])
        lsh, esh = sb("lsh", [P, NT, E]), sb("esh", [P, NT, E])
        onehot = sb("onehot", [P, NT, 2, E])
        tot, e12, den, rden = sb("tot", [P, NT]), sb("e12", [P, NT]), sb("den", [P, NT]), sb("rden", [P, NT])
        w12 = sb("w12", [P, NT, 2])
        ohw = sb("ohw", [P, NT, 2, E])
        comb = sb("comb", [P, NT, E])
        comb3 = sb("comb3", [P, NT, 3 * E], FR)
        combT = sb("combT", [3 * E, T], FR)
        act_s = [sb(f"act_s{i}", [P, T]) for i in range(2)]
        act_c = [sb(f"act_c{i}", [P, T]) for i in range(2)]
        act_h = [sb(f"act_h{i}", [P, T], FR) for i in range(4)]
        act_l = [sb(f"act_l{i}", [P, T], FR) for i in range(4)]
        g0T, pT = sb("g0T", [P, T]), sb("pT", [P, T])
        st1, mv1, ve1, rs1 = sb("st1", [P, NT, 6]), sb("mv1", [P, NT, 2]), sb("ve1", [P, NT]), sb("rs1", [P, NT])
        xn1 = sb("xn1", [P, NT, C])
        xh1, xl1 = sb("xh1", [P, T], FR), sb("xl1", [P, T], FR)
        qk_max = sb("qk_max", [P, NT, 2 * NH])
        qk = sb("qk", [P, NT, 2 * C])
        vv = sb("vv", [P, NT, C + 1])
        qk_sum, qk_rs = sb("qk_sum", [P, NT * 2 * NH]), sb("qk_rs", [P, NT * 2 * NH])
        ctxn = sb("ctxn", [P, C + NH])
        qT = sb("qT", [P, T])
        dinv = sb("dinv", [P, NT, NH])
        att = sb("att", [P, NT, C])
        attT = sb("attT", [P, T])
        hT = sb("hT", [F1 + 1, T])
        top8b, topib = sb("top8b", [P, NT, E]), sb("topib", [P, NT, E], U32)
        topfb = sb("topfb", [P, NT])
        mask = sb("mask", [P, NT, E])
        prod = [sb(f"prod{i}", [P, 2, NT, C]) for i in range(2)]
        sum4 = [sb(f"sum4{i}", [P, NT, C]) for i in range(2)]
        sum2 = [sb(f"sum2{i}", [P, 2, C]) for i in range(2)]
        sel1 = sb("sel1", [P, NT, C])
        g1, sg = sb("g1", [P, NT, C]), sb("sg", [P, NT, C])

        ps = [ctx.enter_context(nc.psum_tensor(f"bank{i}", [P, 512], F32)) for i in range(8)]
        UP = ps[0:2]
        CB, Y = ps[2], ps[3]
        Z0, Z1, Z2, Z3 = ps[4:8]

        ident = cst[:, C_ID:C_ID + P]
        tri = cst[:, C_TRI:C_TRI + P]
        ones2 = cst[0:2, C_ONE:C_ONE + P]

        s_dve_passed = sem("s_dve_passed")
        s_pool_passed = sem("s_pool_passed")
        s_early_in = sem("s_early_in")
        s_late_in = sem("s_late_in")
        s_x0_in = sem("s_x0_in")
        s_x_in = sem("s_x_in")
        s_out_done = sem("s_out_done")
        s_w_split = sem("s_w_split")
        s_fold_done = sem("s_fold_done")
        s_consts_ready = sem("s_consts_ready")
        s_memset_ready = sem("s_memset_ready")
        s_bn0 = sem("s_bn0")
        s_stats0 = sem("s_stats0")
        s_ve0 = sem("s_ve0")
        s_rstd0 = sem("s_rstd0")
        s_xn0 = sem("s_xn0")
        s_xT0 = sem("s_xT0")
        s_xh0 = sem("s_xh0")
        s_xl0 = sem("s_xl0")
        s_prj0 = sem("s_prj0")
        s_prj_sb = sem("s_prj_sb")
        s_kvg_ps = sem("s_kvg_ps")
        s_kvg_sb = sem("s_kvg_sb")
        s_wei = sem("s_wei")
        s_wm = sem("s_wm")
        s_stp = sem("s_stp")
        s_st_sb = sem("s_st_sb")
        s_oh_ps = sem("s_oh_ps")
        s_oh_sb = sem("s_oh_sb")
        s_sT_ps = sem("s_sT_ps")
        s_sT_sb = sem("s_sT_sb")
        s_top8 = sem("s_top8")
        s_topi = sem("s_topi")
        s_topf = sem("s_topf")
        s_lsh = sem("s_lsh")
        s_esh = sem("s_esh")
        s_onehot = sem("s_onehot")
        s_tot = sem("s_tot")
        s_e12 = sem("s_e12")
        s_den = sem("s_den")
        s_rden = sem("s_rden")
        s_w12 = sem("s_w12")
        s_ohw = sem("s_ohw")
        s_comb = sem("s_comb")
        s_combh = sem("s_combh")
        s_comb3 = sem("s_comb3")
        s_combT_ps = sem("s_combT_ps")
        s_combT = sem("s_combT")
        s_up = sem("s_up")
        s_silu = sem("s_silu")
        s_cbc = sem("s_cbc")
        s_scaled = sem("s_scaled")
        s_act_h = sem("s_act_h")
        s_act_l = sem("s_act_l")
        s_down = sem("s_down")
        s_g0 = sem("s_g0")
        s_pT = sem("s_pT")
        s_pTT = sem("s_pTT")
        s_x1 = sem("s_x1")
        s_bn1 = sem("s_bn1")
        s_stats1 = sem("s_stats1")
        s_ve1 = sem("s_ve1")
        s_rstd1 = sem("s_rstd1")
        s_xn1 = sem("s_xn1")
        s_xT1 = sem("s_xT1")
        s_xh1 = sem("s_xh1")
        s_xl1 = sem("s_xl1")
        s_qkv = sem("s_qkv")
        s_v_sb = sem("s_v_sb")
        s_qk_max = sem("s_qk_max")
        s_qk_sub = sem("s_qk_sub")
        s_qk_exp = sem("s_qk_exp")
        s_qk_sum = sem("s_qk_sum")
        s_qk_rs = sem("s_qk_rs")
        s_qk_sm = sem("s_qk_sm")
        s_ctx = sem("s_ctx")
        s_ctx_sb = sem("s_ctx_sb")
        s_qT_ps = sem("s_qT_ps")
        s_qT = sem("s_qT")
        s_nd = sem("s_nd")
        s_dinv = sem("s_dinv")
        s_att_m = sem("s_att_m")
        s_att = sem("s_att")
        s_attT_ps = sem("s_attT_ps")
        s_attT = sem("s_attT")
        s_s1 = sem("s_s1")
        s_hT_ps = sem("s_hT_ps")
        s_hT = sem("s_hT")
        s_lg = sem("s_lg")
        s_top8b = sem("s_top8b")
        s_topib = sem("s_topib")
        s_topfb = sem("s_topfb")
        s_mask = sem("s_mask")
        s_ex = sem("s_ex")
        s_prod = sem("s_prod")
        s_sum4 = sem("s_sum4")
        s_sum2 = sem("s_sum2")
        s_sel1 = sem("s_sel1")
        s_g1 = sem("s_g1")
        s_sg = sem("s_sg")
        s_fin = sem("s_fin")

        block = ctx.enter_context(nc.Block())

        def positive(n):
            return not isinstance(n, int) or n > 0

        def upto_next(c):
            return min(c + 2, B) if isinstance(c, int) else c + 2

        def schedule(eng, first, iteration):
            first()
            iteration(0, True, False, True)
            iteration(1, True, True, True)
            with eng.Fori(2, B - 1) as i:
                iteration(i, True, True, True)
            iteration(B - 1, True, True, False)
            iteration(B, False, True, False)

        @block.sync
        def _(sp):
            def x_dram(a, c, n=1):
                return a[c:c + n].rearrange("b (t p) d -> p (b t) d", p=P)

            sp.dma_start(xs[:, 0], x_dram(x, 0)).then_inc(s_x0_in, 16)
            for dst, src in ((cst, consts), (vec, vecs), (wpr, w_pr), (row, rows), (bdn, b_dn), (wpj, w_pj), (wup, w_up)):
                sp.dma_start(dst[:, :], src).then_inc(s_early_in, 16)
            sp.dma_start(xs[:, 1:B].rearrange("p b t d -> p (b t) d"), x_dram(x, 1, B - 1)).then_inc(s_x_in, 16)
            sp.dma_start(wdn[:, :], w_dn).then_inc(s_early_in, 16)
            for dst, src in ((wqkv, w_qkv), (wex, w_ex), (wp1, w_p1), (wr1, w_r1), (wr2, w_r2)):
                sp.dma_start(dst[:, :], src).then_inc(s_late_in, 16)

            def store(c):
                sp.wait_ge(s_fin, c + 1)
                sp.dma_start(out[bass.ds(c, 1)].rearrange("b (t p) d -> p (b t) d", p=P),
                             xs[:, bass.ds(c, 1)].rearrange("p b t d -> p (b t) d")).then_inc(s_out_done, 16)

            with sp.Fori(0, B) as c:
                store(c)
            sp.wait_ge(s_out_done, 16 * B)

        @block.tensor
        def _(pe):

            def mm(o, l, r, start=True, stop=True):
                return nc.tensor.matmul(o, l, r, start=start, stop=stop, skip_group_check=True)

            def mm3(o, lh, ll, rh, rl, start=True, stop=True):
                mm(o, lh, rh, start, False)
                mm(o, lh, rl, False, False)
                return mm(o, ll, rh, False, stop)

            def transpose_tiles(o, src, w, n):
                for t in range(NT):
                    last = nc.tensor.transpose(o(t), src(t), ident[0:n, 0:n])
                return last

            def a_xT(c):
                pe.wait_ge(s_xn0, c + 1)
                if positive(c):
                    pe.wait_ge(s_combT, c)
                transpose_tiles(lambda t: Z0[:, t * P:(t + 1) * P], lambda t: xn0[:, t, :], P, P).then_inc(s_xT0, 1)

            def a_prj(c):
                pe.wait_ge(s_xl0, c + 1)
                if positive(c):
                    pe.wait_ge(s_sT_sb, c)
                mm3(Z1[0:PR, :], wpr_h[:, :], wpr_l[:, :], xh0[:, :], xl0[:, :]).then_inc(s_prj0, 1)

            def a_kvg(c):
                pe.wait_ge(s_prj_sb, c + 1)
                if positive(c):
                    pe.wait_ge(s_oh_sb, c)
                transpose_tiles(lambda t: Z2[:, t * PR:(t + 1) * PR], lambda t: prj[:, t * P:(t + 1) * P],
                                PR, PR).then_inc(s_kvg_ps, 1)

            def a_wei(c):
                pe.wait_ge(s_xl0, c + 1)
                for t in range(NT):
                    s = slice(t * P, (t + 1) * P)
                    last = mm(Z0[:, s], kT[:, s], prj[Q_ROW:Q_ROW + HS, s])
                last.then_inc(s_wei, 1)

            def a_state(c):
                pe.wait_ge(s_kvg_sb, c + 1)
                for t in range(NT - 1):
                    n = NT - 1 - t
                    v = kvg[:, t, V_COL:V_COL + HS].rearrange("p (o d) -> p o d", o=1).broadcast_to([P, n, HS])
                    last = mm(Z1[0:HS, t * HS:(NT - 1) * HS].rearrange("p (j d) -> p j d", d=HS),
                              kvg[:, t, K_COL:K_COL + HS], v, start=(t == 0), stop=(t == NT - 2))
                last.then_inc(s_stp, 1)

            def a_out(c):
                pe.wait_ge(s_wm, c + 1)
                pe.wait_ge(s_st_sb, c + 1)
                for t in range(NT):
                    s = slice(t * P, (t + 1) * P)
                    last = mm(Z2[0:HS, s], kvg[:, t, V_COL:V_COL + HS], wm[:, s], stop=(t == 0))
                    if t:
                        last = mm(Z2[0:HS, s], st_sum[:, (t - 1) * HS:t * HS], prj[Q_ROW:Q_ROW + HS, s], start=False)
                last.then_inc(s_oh_ps, 1)

            def a_sT(c):
                pe.wait_ge(s_oh_sb, c + 1)
                mm(Z1[:, :], wsum[:, :], ohT[:, :]).then_inc(s_sT_ps, 1)

            def a_comb(c):
                pe.wait_ge(s_comb3, c + 1)
                pe.wait_ge(s_wm, c + 1)
                transpose_tiles(lambda t: Z0[0:3 * E, t * P:(t + 1) * P], lambda t: comb3[:, t, :].bitcast(F32),
                                3 * E, P).then_inc(s_combT_ps, 1)

            def which(k):
                return E if k == 0 else k - 1

            def m_up(c, k):
                if k >= 2:
                    if positive(c * EX + k - 1):
                        pe.wait_ge(s_silu, c * EX + k - 1)
                else:
                    if positive(c * EX):
                        pe.wait_ge(s_silu, c * EX)
                if k == 0:
                    if not isinstance(c, int) or c >= 1:
                        if positive(c * 2 * NT - 2 * NT):
                            pe.wait_ge(s_prod, c * 2 * NT - 2 * NT)
                e = which(k)
                mm3(UP[k % 2][:, :], wup_h[:, e * C:(e + 1) * C], wup_l[:, e * C:(e + 1) * C],
                    xh0[:, :], xl0[:, :]).then_inc(s_up, 1)

            def m_bcast(c, k):
                if positive(c * E + k - 1):
                    pe.wait_ge(s_scaled, c * E + k - 1)
                if k == 1:
                    if not isinstance(c, int) or c >= 2:
                        if positive(c - 1):
                            pe.wait_ge(s_sg, c - 1)
                    pe.wait_ge(s_combT, c + 1)
                mm(CB[:, :], sel_s[:, (k - 1) * C:k * C], combT[0:2 * E, :]).then_inc(s_cbc, 1)

            def m_down(c, k):
                if k == 0:
                    if positive(c):
                        pe.wait_ge(s_g0, c)
                    pe.wait_ge(s_combT, c + 1)
                    mm(Y[:, :], bdn_s[:, :], combT[:, :], stop=False)
                pe.wait_ge(s_act_h, c * EX + k + 1)
                pe.wait_ge(s_act_l, c * EX + k + 1)
                e = which(k)
                mm3(Y[:, :], wdn_h[:, e * C:(e + 1) * C], wdn_l[:, e * C:(e + 1) * C],
                    act_h[k % 4][:, :], act_l[k % 4][:, :], start=False, stop=(k == E)).then_inc(s_down, 1)

            def m_pT(c):
                pe.wait_ge(s_pT, c + 1)
                pe.wait_ge(s_g0, c + 1)
                transpose_tiles(lambda t: Y[:, t * P:(t + 1) * P], lambda t: pT[:, t * P:(t + 1) * P],
                                P, P).then_inc(s_pTT, 1)

            def b_xT(c):
                pe.wait_ge(s_xn1, c + 1)
                pe.wait_ge(s_combT, upto_next(c))
                transpose_tiles(lambda t: Z0[:, t * P:(t + 1) * P], lambda t: xn1[:, t, :], P, P).then_inc(s_xT1, 1)

            QB = [Z2, Z3]

            def b_qkv(c, t):
                if t == 0:
                    pe.wait_ge(s_xl1, c + 1)
                    pe.wait_ge(s_oh_sb, upto_next(c))
                if t >= 2:
                    if positive(c * NT + t - 1):
                        pe.wait_ge(s_v_sb, c * NT + t - 1)
                    if positive(c * NT + t - 1):
                        pe.wait_ge(s_qk_sub, c * NT + t - 1)
                s = slice(t * P, (t + 1) * P)
                o = QB[t % 2][:, 0:3 * C]
                mm(o, ones_s[:, :], row_s[:, R_QKV:R_QKV + 3 * C], stop=False)
                mm(o, xh1[:, s], wqkv_h[:, :], False, False)
                mm(o, xl1[:, s], wqkv_h[:, :], False, False)
                mm(o, xh1[:, s], wqkv_l[:, :], False, True).then_inc(s_qkv, 1)

            def b_hid(c):
                pe.wait_ge(s_xl1, c + 1)
                mm3(Z0[0:F1, :], wr1_h[:, :], wr1_l[:, :], xh1[:, :], xl1[:, :]).then_inc(s_hT_ps, 1)

            def b_logits(c):
                pe.wait_ge(s_hT, c + 1)
                pe.wait_ge(s_sT_sb, upto_next(c))
                for t in range(NT):
                    last = mm(Z1[:, t * E:(t + 1) * E], hT[:, t * P:(t + 1) * P], wr2[:, :])
                last.then_inc(s_lg, 1)

            def b_ctx(c):
                pe.wait_ge(s_qk_sm, c + 1)
                pe.wait_ge(s_v_sb, c * NT + NT)
                pe.wait_ge(s_hT, c + 1)
                for t in range(NT):
                    last = mm(Z0[:, 0:C + 1], qk[:, t, C:2 * C], vv[:, t, :], start=(t == 0), stop=(t == NT - 1))
                last.then_inc(s_ctx, 1)

            def b_qT(c):
                pe.wait_ge(s_topib, c + 1)
                transpose_tiles(lambda t: Z1[:, t * P:(t + 1) * P], lambda t: qk[:, t, 0:C], P, P).then_inc(s_qT_ps, 1)

            def b_nd(c):
                pe.wait_ge(s_qT, c + 1)
                pe.wait_ge(s_ctx_sb, c + 1)
                pe.wait_ge(s_qk_sub, c * NT + NT)
                for t in range(NT):
                    o = QB[t // 2][:, (t % 2) * (C + NH):(t % 2 + 1) * (C + NH)]
                    last = mm(o, qT[:, t * P:(t + 1) * P], ctxn[:, :])
                last.then_inc(s_nd, 1)

            def b_attT(c):
                pe.wait_ge(s_att, c + 1)
                pe.wait_ge(s_qT, c + 1)
                transpose_tiles(lambda t: Z1[:, t * P:(t + 1) * P], lambda t: att[:, t, :], P, P).then_inc(s_attT_ps, 1)

            def e_expert(c, n):
                t, half = n // 2, n % 2
                if n == 0:
                    if c_has_next:
                        pe.wait_ge(s_silu, (c + 2) * EX)
                    else:
                        if positive(B * EX):
                            pe.wait_ge(s_silu, B * EX)
                else:
                    if n >= 2:
                        if positive(c * 2 * NT + n - 1):
                            pe.wait_ge(s_prod, c * 2 * NT + n - 1)
                s = slice(t * P, (t + 1) * P)
                h = slice(half * 4 * C, (half + 1) * 4 * C)
                o = UP[n % 2][:, :]
                mm(o, ones_s[:, :], row_s[:, R_EXP + half * 4 * C:R_EXP + (half + 1) * 4 * C], stop=False)
                mm(o, xh1[:, s], wex_h[:, h], False, False)
                mm(o, xl1[:, s], wex_h[:, h], False, False)
                mm(o, xh1[:, s], wex_l[:, h], False, True).then_inc(s_ex, 1)

            def e_proj(c):
                pe.wait_ge(s_attT, c + 1)
                if c_has_next:
                    pe.wait_ge(s_scaled, (c + 2) * E)
                mm(CB[:, :], ones_s[:, :], row_s[:, R_PROJ:R_PROJ + T], stop=False)
                for t in range(NT):
                    s = slice(t * P, (t + 1) * P)
                    last = mm(CB[:, s], attT[:, s], wp1[:, :], start=False, stop=(t == NT - 1))
                last.then_inc(s_s1, 1)

            def first():
                pe.wait_ge(s_consts_ready, 1)
                mm(Z1[0:HS, 0:C], cst[:, C_FOLD:C_FOLD + HS], wpj[:, :]).then_inc(s_fold_done, 1)
                pe.wait_ge(s_sT_sb, 0)
                stage_a(0)

            def stage_a(c):
                for f in (a_xT, a_prj, a_kvg, a_wei, a_state, a_out, a_sT, a_comb):
                    f(c)

            def iteration(i, has_m, has_l1, has_next):
                nonlocal c_has_next
                c_has_next = has_m
                j = i - 1
                LAG = 3
                beside = {0: [b_xT], 1: [], 2: [lambda c: b_qkv(c, 0)], 3: [lambda c: b_qkv(c, 1), b_hid],
                          4: [lambda c: b_qkv(c, 2)], 5: [lambda c: b_qkv(c, 3), b_logits], 8: [b_ctx, b_qT],
                          10: [b_nd], 11: [b_attT]}
                for k in range(EX + LAG):
                    if has_m:
                        if k < EX:
                            m_up(i, k)
                        if 1 <= k < EX:
                            m_bcast(i, k)
                        if k >= LAG:
                            m_down(i, k - LAG)
                    if has_l1:
                        for f in beside.get(k, []):
                            f(j)
                after = {1: [a_xT], 2: [a_prj], 3: [a_kvg, a_wei], 4: [a_state], 5: [a_out], 6: [a_sT], 7: [a_comb]}
                for n in range(2 * NT):
                    if has_l1:
                        e_expert(j, n)
                        if n == 4:
                            e_proj(j)
                    if has_m and n == 3:
                        m_pT(i)
                    if has_next:
                        for f in after.get(n, []):
                            f(i + 1)

            c_has_next = True
            schedule(pe, first, iteration)

        @block.scalar
        def _(act):

            def identity(o, i, **kw):
                return nc.scalar.activation(o, i, ACT.Identity, **kw)

            def a_xh(c):
                act.wait_ge(s_xT0, c + 1)
                if positive(c * EX):
                    act.wait_ge(s_up, c * EX)
                identity(xh0[:, :], Z0[:, :]).then_inc(s_xh0, 1)

            def a_prj(c):
                act.wait_ge(s_prj0, c + 1)
                if positive(c):
                    act.wait_ge(s_oh_ps, c)
                identity(prj[:, :], Z1[0:PR, :], bias=vec[0:PR, V_PR:V_PR + 1])
                identity(kT[:, :], Z1[K_ROW:K_ROW + HS, :], bias=vec[K_ROW:K_ROW + HS, V_PR:V_PR + 1]).then_inc(s_prj_sb, 1)

            def a_state(c):
                act.wait_ge(s_stp, c + 1)
                identity(st_sum[:, :], Z1[0:HS, 0:(NT - 1) * HS]).then_inc(s_st_sb, 1)

            def a_exp(c):
                act.wait_ge(s_lsh, c + 1)
                if positive(c):
                    act.wait_ge(s_w12, c)
                nc.scalar.activation(esh[:, :, :], lsh[:, :, :], ACT.Exp).then_inc(s_esh, 1)

            def a_oh(c):
                act.wait_ge(s_oh_ps, c + 1)
                if positive(c):
                    act.wait_ge(s_sT_ps, c)
                identity(ohT[:, :], Z2[0:HS, :]).then_inc(s_oh_sb, 1)

            def a_sTb(c):
                act.wait_ge(s_sT_ps, c + 1)
                if positive(c):
                    act.wait_ge(s_pT, c)
                identity(sTb[:, :], Z1[:, :], bias=vec[:, V_PROJ:V_PROJ + 1]).then_inc(s_sT_sb, 1)

            def a_combT(c):
                act.wait_ge(s_combT_ps, c + 1)
                if positive(c * EX):
                    act.wait_ge(s_down, c * EX)
                identity(combT[:, :], Z0[0:3 * E, :]).then_inc(s_combT, 1)

            def m_silu(c, k):
                e = E if k == 0 else k - 1
                act.wait_ge(s_up, c * EX + k + 1)
                dst = act_s[k % 2]
                if k == 0:
                    if positive(c * E):
                        act.wait_ge(s_scaled, c * E)
                elif k >= 3:
                    if positive(c * E + k - 2):
                        act.wait_ge(s_scaled, c * E + k - 2)
                elif k == 2:
                    act.wait_ge(s_act_l, c * EX + 1)
                    act.wait_ge(s_act_h, c * EX + 1)
                nc.scalar.activation(dst[:, :], UP[k % 2][:, :], ACT.Silu, bias=vec[:, V_UP + e:V_UP + e + 1]).then_inc(s_silu, 1)

            def m_high(c, k):
                if k == 0:
                    act.wait_ge(s_silu, c * EX + 1)
                    src = act_s[0]
                else:
                    if positive(c * E + k):
                        act.wait_ge(s_scaled, c * E + k)
                    src = act_c[k % 2]
                if k >= 4:
                    if positive(c * EX + k - 3):
                        act.wait_ge(s_down, c * EX + k - 3)
                else:
                    if positive(c * EX):
                        act.wait_ge(s_down, c * EX)
                identity(act_h[k % 4][:, :], src[:, :]).then_inc(s_act_h, 1)

            def m_gate(c):
                act.wait_ge(s_down, c * EX + EX)
                if positive(c):
                    act.wait_ge(s_pT, c)
                nc.scalar.activation(g0T[:, :], Y[:, :], ACT.Silu, bias=vec[:, V_SHD:V_SHD + 1]).then_inc(s_g0, 1)

            def b_xh(c):
                act.wait_ge(s_xT1, c + 1)
                if positive(c * 2 * NT):
                    act.wait_ge(s_ex, c * 2 * NT)
                identity(xh1[:, :], Z0[:, :]).then_inc(s_xh1, 1)

            def b_v(c, t):
                act.wait_ge(s_qkv, c * NT + t + 1)
                if t == 0:
                    if positive(c):
                        act.wait_ge(s_ctx, c)
                identity(vv[:, t, 0:C], [Z2, Z3][t % 2][:, 2 * C:3 * C]).then_inc(s_v_sb, 1)

            def b_exp(c, t):
                act.wait_ge(s_qk_sub, c * NT + t + 1)
                nc.scalar.activation(qk[:, t, :], qk[:, t, :], ACT.Exp).then_inc(s_qk_exp, 1)

            def b_relu(c):
                act.wait_ge(s_hT_ps, c + 1)
                if positive(c):
                    act.wait_ge(s_lg, c)
                nc.scalar.activation(hT[0:F1, :], Z0[0:F1, :], ACT.Relu, bias=vec[0:F1, V_B1:V_B1 + 1]).then_inc(s_hT, 1)

            def b_qT(c):
                act.wait_ge(s_qT_ps, c + 1)
                if positive(c):
                    act.wait_ge(s_nd, c)
                identity(qT[:, :], Z1[:, :]).then_inc(s_qT, 1)

            def b_attT(c):
                act.wait_ge(s_attT_ps, c + 1)
                if positive(c):
                    act.wait_ge(s_s1, c)
                identity(attT[:, :], Z1[:, :]).then_inc(s_attT, 1)

            def e_gate(c):
                act.wait_ge(s_sel1, c * NT + NT)
                if positive(c):
                    act.wait_ge(s_sg, c)
                nc.scalar.activation(g1[:, :, :], sel1[:, :, :], ACT.Silu).then_inc(s_g1, 1)

            def first():
                act.wait_ge(s_early_in, 16 * 8)
                identity(sel_s[:, :], cst[0:2 * E, C_SEL:C_SEL + E * C])
                identity(ones_s[:, :], ones2).then_inc(s_consts_ready, 1)
                act.wait_ge(s_fold_done, 1)
                identity(wsum[:, :], Z1[0:HS, 0:C]).then_inc(s_consts_ready, 1)
                for f in (a_xh, a_prj, a_state, a_exp, a_oh, a_sTb, a_combT):
                    f(0)

            def iteration(i, has_m, has_l1, has_next):
                j = i - 1
                beside = {0: [b_xh], 2: [lambda c: b_v(c, 0)], 3: [lambda c: b_v(c, 1), b_relu], 4: [lambda c: b_v(c, 2)],
                          5: [lambda c: b_v(c, 3)] + [lambda c, t=t: b_exp(c, t) for t in range(NT)],
                          9: [b_qT], 11: [b_attT]}
                for k in range(EX + 3):
                    if has_m:
                        if k < EX:
                            m_silu(i, k)
                        if 1 <= k <= EX:
                            m_high(i, k - 1)
                    if has_l1:
                        for f in beside.get(k, []):
                            f(j)
                if has_m:
                    m_gate(i)
                if has_next:
                    for f in (a_xh, a_prj, a_state, a_exp, a_oh, a_sTb, a_combT):
                        f(i + 1)
                if has_l1:
                    e_gate(j)

            schedule(act, first, iteration)

        @block.vector
        def _(dve):
            v = nc.vector


            def passed():
                dve.sem_inc(s_dve_passed, 1)

            def stats(c, s_bn, s_stats, st, mv, src):
                passed()
                for t in range(NT):
                    last = v.bn_stats(st[:, t, :], src(t))
                last.then_inc(s_bn, 1)
                dve.wait_ge(s_bn, c + 1)
                passed()
                for t in range(NT):
                    last = v.bn_aggr(mv[:, t, :], st[:, t, :])
                last.then_inc(s_stats, 1)

            def normalise(c, s_rstd, s_xT, s_xn, xn, src, mv, rs):
                dve.wait_ge(s_rstd, c + 1)
                if positive(c):
                    dve.wait_ge(s_xT, c)
                for t in range(NT):
                    last = v.tensor_scalar(xn[:, t, :], src(t), mv[:, t, 0:1], rs[:, t:t + 1], ALU.subtract, ALU.mult)
                last.then_inc(s_xn, 1)

            def x_of(c):
                if isinstance(c, int):
                    return lambda t: xs[:, c, t, :]
                return lambda t: xs[:, bass.ds(c, 1), t, :].rearrange("p o d -> p (o d)")

            def a_stats(c):
                if positive(c):
                    dve.wait_ge(s_rstd0, c)
                stats(c, s_bn0, s_stats0, st0, mv0, x_of(c))

            def a_norm(c):
                normalise(c, s_rstd0, s_xT0, s_xn0, xn0, x_of(c), mv0, rs0)

            def a_xl(c):
                dve.wait_ge(s_xh0, c + 1)
                if positive(c * EX):
                    dve.wait_ge(s_up, c * EX)
                v.tensor_tensor(xl0[:, :], Z0[:, :], xh0[:, :].bitcast(F32), ALU.subtract).then_inc(s_xl0, 1)

            def a_kvg(c):
                dve.wait_ge(s_kvg_ps, c + 1)
                if positive(c):
                    dve.wait_ge(s_oh_ps, c)
                v.tensor_copy(kvg[:, :, :], Z2[:, 0:NT * PR].rearrange("p (t n) -> p t n", t=NT)[:, :, K_ROW:PR]).then_inc(s_kvg_sb, 1)

            def a_wm(c):
                dve.wait_ge(s_wei, c + 1)
                v.tensor_tensor(wm[:, :].rearrange("p (t n) -> p t n", t=NT), Z0[:, :].rearrange("p (t n) -> p t n", t=NT),
                                tri.rearrange("p (o n) -> p o n", o=1).broadcast_to([P, NT, P]), ALU.mult).then_inc(s_wm, 1)

            def a_top(c):
                dve.wait_ge(s_kvg_sb, c + 1)
                if positive(c):
                    dve.wait_ge(s_lsh, c)
                passed()
                for t in range(NT):
                    last = v.max(top8[:, t, :], kvg[:, t, G_COL:G_COL + E])
                last.then_inc(s_top8, 1)
                dve.wait_ge(s_top8, c + 1)
                passed()
                for t in range(NT):
                    last = v.max_index(topi[:, t, :], top8[:, t, :], kvg[:, t, G_COL:G_COL + E])
                last.then_inc(s_topi, 1)
                dve.wait_ge(s_topi, c + 1)
                v.tensor_copy(topf[:, :, :], topi[:, :, 0:2]).then_inc(s_topf, 1)
                dve.wait_ge(s_topf, c + 1)
                if positive(c):
                    dve.wait_ge(s_ohw, c)
                v.tensor_tensor(onehot[:, :, :, :].rearrange("p t k e -> p (t k) e"),
                                cst[:, C_IOTA:C_IOTA + E].rearrange("p (o e) -> p o e", o=1).broadcast_to([P, NT * 2, E]),
                                topf[:, :, :].rearrange("p t (k o) -> p (t k) o", o=1).broadcast_to([P, NT * 2, E]),
                                ALU.is_equal).then_inc(s_onehot, 1)

            def a_den(c):
                dve.wait_ge(s_esh, c + 1)
                v.tensor_reduce(tot[:, :], esh[:, :, :], AX_X, ALU.add).then_inc(s_tot, 1)
                dve.wait_ge(s_e12, c + 1)
                dve.wait_ge(s_tot, c + 1)
                v.scalar_tensor_tensor(den[:, :], tot[:, :], TINY, e12[:, :], ALU.mult, ALU.add).then_inc(s_den, 1)
                dve.wait_ge(s_den, c + 1)
                if positive(c):
                    dve.wait_ge(s_w12, c)
                v.reciprocal(rden[:, :], den[:, :]).then_inc(s_rden, 1)

            def m_scale(c, k):
                dve.wait_ge(s_silu, c * EX + k + 1)
                if positive(c * E + k):
                    dve.wait_ge(s_cbc, c * E + k)
                if k >= 3:
                    if positive(c * EX + k - 1):
                        dve.wait_ge(s_act_l, c * EX + k - 1)
                else:
                    if positive(c * EX):
                        dve.wait_ge(s_act_l, c * EX)
                if k >= 3:
                    if positive(c * EX + k - 1):
                        dve.wait_ge(s_act_h, c * EX + k - 1)
                else:
                    if positive(c * EX):
                        dve.wait_ge(s_act_h, c * EX)
                v.tensor_tensor(act_c[k % 2][:, :], act_s[k % 2][:, :], CB[:, :], ALU.mult).then_inc(s_scaled, 1)

            def m_pT(c):
                dve.wait_ge(s_g0, c + 1)
                dve.wait_ge(s_sT_sb, c + 1)
                if positive(c):
                    dve.wait_ge(s_pTT, c)
                v.tensor_tensor(pT[:, :], g0T[:, :], sTb[:, :], ALU.mult).then_inc(s_pT, 1)

            def m_x1(c):
                dve.wait_ge(s_pTT, c + 1)
                x_c = xs[:, c] if isinstance(c, int) else xs[:, bass.ds(c, 1)].rearrange("p o t d -> p (o t) d")
                v.tensor_tensor(x_c, Y[:, :].rearrange("p (t d) -> p t d", t=NT), x_c, ALU.add).then_inc(s_x1, 1)

            def l_stats(c):
                dve.wait_ge(s_x1, c + 1)
                if positive(c):
                    dve.wait_ge(s_rstd1, c)
                stats(c, s_bn1, s_stats1, st1, mv1, x_of(c))

            def l_norm(c):
                normalise(c, s_rstd1, s_xT1, s_xn1, xn1, x_of(c), mv1, rs1)

            def b_xl(c):
                dve.wait_ge(s_xh1, c + 1)
                v.tensor_tensor(xl1[:, :], Z0[:, :], xh1[:, :].bitcast(F32), ALU.subtract).then_inc(s_xl1, 1)

            def b_max(c, t):
                dve.wait_ge(s_v_sb, c * NT + t + 1)
                z = [Z2, Z3][t % 2][:, 0:2 * C].rearrange("p (h d) -> p h d", d=HS)
                if t == 0:
                    if positive(c):
                        dve.wait_ge(s_qT_ps, c)
                    if positive(c):
                        dve.wait_ge(s_att, c)
                v.tensor_reduce(qk_max[:, t, :], z, AX_X, ALU.max).then_inc(s_qk_max, 1)
                dve.wait_ge(s_qk_max, c * NT + t + 1)
                v.tensor_tensor(qk[:, t, :].rearrange("p (h d) -> p h d", d=HS), z,
                                qk_max[:, t, :].rearrange("p (h o) -> p h o", o=1).broadcast_to([P, 2 * NH, HS]),
                                ALU.subtract).then_inc(s_qk_sub, 1)

            def b_soft(c):
                dve.wait_ge(s_qk_exp, c * NT + NT)
                a = qk[:, :, :].rearrange("p t (h d) -> p (t h) d", d=HS)
                v.tensor_reduce(qk_sum[:, :], a, AX_X, ALU.add).then_inc(s_qk_sum, 1)
                dve.wait_ge(s_qk_sum, c + 1)
                v.reciprocal(qk_rs[:, :], qk_sum[:, :]).then_inc(s_qk_rs, 1)
                dve.wait_ge(s_qk_rs, c + 1)
                v.tensor_tensor(a, a, qk_rs[:, :].rearrange("p (h o) -> p h o", o=1).broadcast_to([P, NT * 2 * NH, HS]),
                                ALU.mult).then_inc(s_qk_sm, 1)

            def b_ctx(c):
                dve.wait_ge(s_ctx, c + 1)
                if positive(c):
                    dve.wait_ge(s_nd, c)
                v.tensor_tensor(ctxn[:, 0:C], Z0[:, 0:C], cst[:, C_BLK:C_BLK + C], ALU.mult)
                v.tensor_scalar(ctxn[:, C:C + NH], cst[:, C_IND:C_IND + NH], Z0[:, C:C + 1], None, ALU.mult).then_inc(s_ctx_sb, 1)

            def b_att(c):
                dve.wait_ge(s_nd, c + 1)
                if positive(c):
                    dve.wait_ge(s_attT_ps, c)
                for b, z in enumerate((Z2, Z3)):
                    zz = z[:, 0:2 * (C + NH)].rearrange("p (t n) -> p t n", t=2)
                    last = v.reciprocal(dinv[:, 2 * b:2 * b + 2, :], zz[:, :, C:C + NH])
                last.then_inc(s_dinv, 1)
                dve.wait_ge(s_dinv, c + 1)
                for b, z in enumerate((Z2, Z3)):
                    for u in range(2):
                        t = 2 * b + u
                        o = u * (C + NH)
                        last = v.tensor_tensor(att[:, t, :].rearrange("p (h d) -> p h d", d=HS),
                                               z[:, o:o + C].rearrange("p (h d) -> p h d", d=HS),
                                               dinv[:, t, :].rearrange("p (h o) -> p h o", o=1).broadcast_to([P, NH, HS]), ALU.mult)
                last.then_inc(s_att_m, 1)
                dve.wait_ge(s_att_m, c + 1)
                v.tensor_tensor(att[:, :, :], att[:, :, :], qk[:, :, 0:C], ALU.add).then_inc(s_att, 1)

            def b_top(c):
                dve.wait_ge(s_lg, c + 1)
                passed()
                for t in range(NT):
                    last = v.max(top8b[:, t, :], Z1[:, t * E:(t + 1) * E])
                last.then_inc(s_top8b, 1)
                dve.wait_ge(s_top8b, c + 1)
                passed()
                for t in range(NT):
                    last = v.max_index(topib[:, t, :], top8b[:, t, :], Z1[:, t * E:(t + 1) * E])
                last.then_inc(s_topib, 1)
                dve.wait_ge(s_topib, c + 1)
                v.tensor_copy(topfb[:, :], topib[:, :, 0]).then_inc(s_topfb, 1)
                dve.wait_ge(s_topfb, c + 1)
                v.tensor_tensor(mask[:, :, :], cst[:, C_IOTA:C_IOTA + E].rearrange("p (o e) -> p o e", o=1).broadcast_to([P, NT, E]),
                                topfb[:, :].rearrange("p (t o) -> p t o", o=1).broadcast_to([P, NT, E]), ALU.is_equal).then_inc(s_mask, 1)

            def e_prod(c, n):
                t, half = n // 2, n % 2
                dve.wait_ge(s_ex, c * 2 * NT + n + 1)
                if n == 0:
                    dve.wait_ge(s_mask, c + 1)
                if half == 0:
                    if t >= 2:
                        if positive(c * NT + t - 1):
                            dve.wait_ge(s_sum4, c * NT + t - 1)
                    else:
                        if positive(c * NT):
                            dve.wait_ge(s_sum4, c * NT)
                v.tensor_tensor(prod[t % 2][:, half], UP[n % 2][:, :].rearrange("p (e d) -> p e d", d=C),
                                mask[:, t, half * 4:half * 4 + 4].rearrange("p (e o) -> p e o", o=1).broadcast_to([P, 4, C]),
                                ALU.mult).then_inc(s_prod, 1)

            def e_sg(c):
                dve.wait_ge(s_s1, c + 1)
                dve.wait_ge(s_g1, c + 1)
                if positive(c):
                    dve.wait_ge(s_fin, c)
                v.tensor_tensor(sg[:, :, :], CB[:, :].rearrange("p (t d) -> p t d", t=NT), g1[:, :, :], ALU.mult).then_inc(s_sg, 1)

            def split(h, l, w):
                v.tensor_copy(h[:, :], w[:, :]).then_inc(s_w_split, 1)
                nsplit[0] += 1
                dve.wait_ge(s_w_split, nsplit[0])
                v.tensor_tensor(l[:, :], w[:, :], h[:, :].bitcast(F32), ALU.subtract).then_inc(s_w_split, 1)
                nsplit[0] += 1

            def stack(s, r, w, m):
                v.tensor_scalar(r[:, :], w[:, :], m, None, ALU.mult).then_inc(s_w_split, 1)
                nsplit[0] += 1
                dve.wait_ge(s_w_split, nsplit[0])
                v.tensor_tensor(s[:, :], w[:, :], r[:, :].bitcast(F32), ALU.subtract).then_inc(s_w_split, 1)
                nsplit[0] += 1

            nsplit = [0]

            def first():
                dve.wait_ge(s_x0_in, 16)
                a_stats(0)
                dve.wait_ge(s_early_in, 16 * 8)
                split(wpr_h, wpr_l, wpr)
                a_norm(0)
                split(wup_h, wup_l, wup)
                stack(bdn_s, bdn_r, bdn, cst[0:3 * E, C_M24:C_M24 + 1])
                a_xl(0)
                a_kvg(0)
                a_wm(0)
                a_top(0)
                a_den(0)
                split(wdn_h, wdn_l, wdn)
                stack(row_s, row_r, row, cst[0:2, C_M2:C_M2 + 1])
                dve.wait_ge(s_late_in, 16 * 5)
                split(wqkv_h, wqkv_l, wqkv)
                split(wex_h, wex_l, wex)
                split(wr1_h, wr1_l, wr1)
                v.memset(vv[:, :, C:C + 1], 1.0)
                v.memset(hT[F1:F1 + 1, :], 1.0).then_inc(s_memset_ready, 1)
                dve.wait_ge(s_x_in, 16)

            def iteration(i, has_m, has_l1, has_next):
                j = i - 1
                beside = {0: [l_norm, b_xl], 2: [lambda c: b_max(c, 0)], 3: [lambda c: b_max(c, 1)], 4: [lambda c: b_max(c, 2)],
                          5: [lambda c: b_max(c, 3), b_top], 7: [b_soft], 9: [b_ctx], 10: [b_att]}
                for k in range(EX + 3):
                    if has_m and 1 <= k < EX:
                        m_scale(i, k)
                    if has_l1:
                        for f in beside.get(k, []):
                            f(j)
                after = {0: [a_stats], 1: [a_norm, a_xl], 4: [a_kvg, a_wm, a_top], 6: [a_den]}
                for n in range(2 * NT):
                    if has_l1:
                        e_prod(j, n)
                    if has_m and n == 2:
                        m_pT(i)
                    if has_m and n == 4:
                        m_x1(i)
                        l_stats(i)
                    if has_next:
                        for f in after.get(n, []):
                            f(i + 1)
                if has_l1:
                    e_sg(j)

            schedule(dve, first, iteration)

        @block.gpsimd
        def _(pool):
            g = nc.gpsimd


            def passed():
                pool.sem_inc(s_pool_passed, 1)

            def rstd(c, s_stats, s_ve, s_xn, s_rstd, mv, ve, rs):
                pool.wait_ge(s_stats, c + 1)
                passed()
                g.tensor_scalar(ve[:, :], mv[:, :, 1], EPS, 1.0, ALU.add, ALU.mult).then_inc(s_ve, 1)
                pool.wait_ge(s_ve, c + 1)
                if positive(c):
                    pool.wait_ge(s_xn, c)
                g.tensor_tensor(rs[:, :], ve[:, :], mhalf[:, :], ALU.pow).then_inc(s_rstd, 1)

            def a_rstd(c):
                rstd(c, s_stats0, s_ve0, s_xn0, s_rstd0, mv0, ve0, rs0)

            def l_rstd(c):
                rstd(c, s_stats1, s_ve1, s_xn1, s_rstd1, mv1, ve1, rs1)

            def a_lsh(c):
                pool.wait_ge(s_top8, c + 1)
                if positive(c):
                    pool.wait_ge(s_esh, c)
                g.tensor_tensor(lsh[:, :, :], top8[:, :, :], top8[:, :, 0:1].broadcast_to([P, NT, E]), ALU.subtract).then_inc(s_lsh, 1)

            def a_comb(c):
                pool.wait_ge(s_esh, c + 1)
                if positive(c):
                    pool.wait_ge(s_den, c)
                g.tensor_tensor(e12[:, :], esh[:, :, 0], esh[:, :, 1], ALU.add).then_inc(s_e12, 1)
                pool.wait_ge(s_rden, c + 1)
                g.tensor_tensor(w12[:, :, :], esh[:, :, 0:2], rden[:, :].rearrange("p (t o) -> p t o", o=1).broadcast_to([P, NT, 2]),
                                ALU.mult).then_inc(s_w12, 1)
                pool.wait_ge(s_w12, c + 1)
                pool.wait_ge(s_onehot, c + 1)
                g.tensor_tensor(ohw[:, :, :, :].rearrange("p t k e -> p (t k) e"), onehot[:, :, :, :].rearrange("p t k e -> p (t k) e"),
                                w12[:, :, :].rearrange("p t (k o) -> p (t k) o", o=1).broadcast_to([P, NT * 2, E]),
                                ALU.mult).then_inc(s_ohw, 1)
                pool.wait_ge(s_ohw, c + 1)
                g.tensor_tensor(comb[:, :, :], ohw[:, :, 0, :], ohw[:, :, 1, :], ALU.add).then_inc(s_comb, 1)
                pool.wait_ge(s_comb, c + 1)
                if positive(c):
                    pool.wait_ge(s_combT_ps, c)
                passed()
                g.tensor_copy(comb3[:, :, 0:E], comb[:, :, :])
                g.tensor_copy(comb3[:, :, 2 * E:3 * E], comb[:, :, :]).then_inc(s_combh, 1)
                pool.wait_ge(s_combh, c + 1)
                g.tensor_tensor(comb3[:, :, E:2 * E], comb[:, :, :], comb3[:, :, 0:E].bitcast(F32), ALU.subtract).then_inc(s_comb3, 1)

            def m_low(c, k):
                pool.wait_ge(s_act_h, c * EX + k + 1)
                if k >= 4:
                    if positive(c * EX + k - 3):
                        pool.wait_ge(s_down, c * EX + k - 3)
                else:
                    if positive(c * EX):
                        pool.wait_ge(s_down, c * EX)
                src = act_s[0] if k == 0 else act_c[k % 2]
                g.tensor_tensor(act_l[k % 4][:, :], src[:, :], act_h[k % 4][:, :].bitcast(F32), ALU.subtract).then_inc(s_act_l, 1)

            def e_sum(c, t):
                pool.wait_ge(s_prod, c * 2 * NT + 2 * t + 2)
                b = t % 2
                if t >= 1:
                    if positive(c * NT + t - 1):
                        pool.wait_ge(s_sum2, c * NT + t - 1)
                g.tensor_tensor(sum4[b][:, :, :], prod[b][:, 0], prod[b][:, 1], ALU.add).then_inc(s_sum4, 1)
                pool.wait_ge(s_sum4, c * NT + t + 1)
                if t >= 1:
                    if positive(c * NT + t - 1):
                        pool.wait_ge(s_sel1, c * NT + t - 1)
                g.tensor_tensor(sum2[b][:, :, :], sum4[b][:, 0:2, :], sum4[b][:, 2:4, :], ALU.add).then_inc(s_sum2, 1)
                pool.wait_ge(s_sum2, c * NT + t + 1)
                if t == 0:
                    if positive(c):
                        pool.wait_ge(s_g1, c)
                g.tensor_tensor(sel1[:, t, :], sum2[b][:, 0, :], sum2[b][:, 1, :], ALU.add).then_inc(s_sel1, 1)

            def e_fin(c):
                pool.wait_ge(s_sg, c + 1)
                x_c = xs[:, c] if isinstance(c, int) else xs[:, bass.ds(c, 1)].rearrange("p o t d -> p (o t) d")
                g.tensor_tensor(x_c, x_c, sg[:, :, :], ALU.add).then_inc(s_fin, 1)

            def first():
                g.memset(mhalf[:, :], -0.5).then_inc(s_memset_ready, 1)
                pool.wait_ge(s_memset_ready, 1)
                a_rstd(0)
                a_lsh(0)
                a_comb(0)

            def iteration(i, has_m, has_l1, has_next):
                j = i - 1
                if has_m:
                    for k in range(EX):
                        m_low(i, k)
                if has_next:
                    a_rstd(i + 1)
                if has_l1:
                    e_sum(j, 0)
                    e_sum(j, 1)
                if has_m:
                    l_rstd(i)
                if has_next:
                    a_lsh(i + 1)
                if has_l1:
                    e_sum(j, 2)
                if has_next:
                    a_comb(i + 1)
                if has_l1:
                    e_sum(j, 3)
                    e_fin(j)

            schedule(pool, first, iteration)


def constants():
    c = np.zeros((P, NCONST), np.float32)
    r = np.arange(P)
    c[:, C_ID:C_ID + P] = np.eye(P)
    c[:, C_TRI:C_TRI + P] = r[:, None] <= r[None, :]
    c[:, C_BLK:C_BLK + C] = r[:, None] // HS == r[None, :] // HS
    c[:, C_IND:C_IND + NH] = r[:, None] // HS == np.arange(NH)[None, :]
    c[:, C_FOLD:C_FOLD + HS] = r[:, None] % HS == np.arange(HS)[None, :]
    c[:, C_IOTA:C_IOTA + E] = np.arange(E)[None, :]
    c[0, C_M2] = 0.0
    c[1, C_M2] = 1.0
    c[2 * E:3 * E, C_M24] = 1.0
    c[:, C_ONE:C_ONE + P] = 1.0
    for e in range(E):
        c[[e, E + e], C_SEL + e * C:C_SEL + (e + 1) * C] = 1.0
    return c


def kernel(**inputs):
    import concourse.bacc as bacc
    from concourse.bass_utils import run_bass_kernel_spmd

    a = {k: np.asarray(v) for k, v in inputs.items()}
    z = lambda *s: np.zeros(s, np.float32)

    w_pr, b_pr = z(C, PR), z(P)
    for i, at in enumerate((Q_ROW, K_ROW, V_ROW)):
        w_pr[:, at:at + HS] = a["L0_attn_qkv_w"][i * HS:(i + 1) * HS].T
        b_pr[at:at + HS] = a["L0_attn_qkv_b"][i * HS:(i + 1) * HS]
    w_pr[:, G_ROW:G_ROW + E] = a["L0_ffn_gate_w"].T

    def side_by_side(stack, shared):
        return np.concatenate([stack.transpose(1, 0, 2).reshape(C, -1), shared], axis=1)

    vecs = z(P, NVEC)
    vecs[:, V_UP:V_UP + E] = a["L0_ffn_up_b"].T
    vecs[:, V_UP + E] = a["L0_ffn_sh_up_b"]
    vecs[:, V_PR] = b_pr
    vecs[:, V_PROJ] = a["L0_attn_proj_b"]
    vecs[:, V_SHD] = a["L0_ffn_sh_down_b"]
    vecs[0:F1, V_B1] = a["L1_ffn_b1"]
    rows1 = np.concatenate([a["L1_attn_bq"], a["L1_attn_bk"], a["L1_attn_bv"], a["L1_ffn_expert_b"].reshape(-1)]
                           + [a["L1_attn_bp"]] * NT)
    arrays = {
        "x": a["L0_attn_ids"], "consts": constants(), "w_pr": w_pr,
        "w_up": side_by_side(a["L0_ffn_up_w"], a["L0_ffn_sh_up_w"]),
        "w_dn": side_by_side(a["L0_ffn_down_w"], a["L0_ffn_sh_down_w"]),
        "w_pj": a["L0_attn_proj_w"].T, "b_dn": np.concatenate([a["L0_ffn_down_b"]] * 3),
        "vecs": vecs, "rows": np.stack([rows1, rows1]),
        "w_qkv": np.concatenate([a["L1_attn_Wq"].T, a["L1_attn_Wk"].T, a["L1_attn_Wv"].T], axis=1),
        "w_ex": a["L1_ffn_expert_W"].transpose(1, 0, 2).reshape(C, -1),
        "w_p1": a["L1_attn_Wp"].T, "w_r1": a["L1_ffn_W1"],
        "w_r2": np.concatenate([a["L1_ffn_W2"], a["L1_ffn_b2"][None]]),
    }
    arrays = {k: np.ascontiguousarray(v) for k, v in arrays.items()}
    nc = bacc.Bacc("TRN2", target_bir_lowering=False, num_devices=1)
    aps = {k: nc.dram_tensor(k, v.shape, mybir.dt.from_np(v.dtype), kind="ExternalInput").ap() for k, v in arrays.items()}
    out = nc.dram_tensor("out", (B, T, C), F32, kind="ExternalOutput").ap()
    build_program(nc, out=out, **aps)
    r = run_bass_kernel_spmd(nc, [arrays], core_ids=[0])
    return r.results[0]["out"]
```

```python
from contextlib import ExitStack

import numpy as np

import concourse.bass as bass
from concourse import mybir

ALU = mybir.AluOpType
ACT = mybir.ActivationFunctionType
AX_X = mybir.AxisListType.X
F32 = mybir.dt.float32
FR = mybir.dt.float32r
U32 = mybir.dt.uint32

P = 128
C = 128
B, T = 8, 512
NT = T // P
E = 8
EX = E + 1
HS = 8
V3 = 3 * HS
NH = C // HS
F1 = C // 2
EPS = 1e-5
TINY = 1e-20

Q_ROW, K_ROW, V_ROW, G_ROW = 0, 32, 64, 96
PR = G_ROW + E
KVG = PR - K_ROW
K_COL, V_COL, G_COL = 0, V_ROW - K_ROW, G_ROW - K_ROW

C_ID, C_TRI, C_BLK, C_IND, C_FOLD, C_IOTA, C_M2, C_M24, C_MW, C_ONE = 0, 128, 256, 384, 400, 424, 432, 433, 434, 435
C_SEL = C_ONE + 128
NCONST = C_SEL + E * C
V_UP, V_PR, V_PROJ, V_SHD, V_B1 = 0, EX, EX + 1, EX + 2, EX + 3
NVEC = EX + 4
R_QKV, R_EXP, R_PROJ = 0, 3 * C, 3 * C + E * C
NROW = R_PROJ + NT * C


def build_program(nc, x, consts, w_pr, w_up, w_dn, w_pj, b_dn, vecs, rows, w_qkv, w_ex, w_p1, w_r1, w_r2, out):
    with ExitStack() as ctx:
        def sb(name, shape, dt=F32):
            return ctx.enter_context(nc.sbuf_tensor(name, shape, dt))

        def sem(name):
            return ctx.enter_context(nc.semaphore(name))

        cst = sb("cst", [P, NCONST])
        vec = sb("vec", [P, NVEC])
        row = sb("row", [2, NROW])
        row_r = sb("row_r", [2, NROW], FR)
        row_s = sb("row_s", [2, NROW], FR)
        bdn = sb("bdn", [3 * E, C])
        bdn_r = sb("bdn_r", [3 * E, C], FR)
        bdn_s = sb("bdn_s", [3 * E, C], FR)
        ones_s = sb("ones_s", [2, P], FR)
        sel_s = sb("sel_s", [2 * E, E * C], FR)
        wpr, wpr_h, wpr_l = sb("wpr", [P, PR]), sb("wpr_h", [P, PR], FR), sb("wpr_l", [P, PR], FR)
        wup, wup_h, wup_l = sb("wup", [P, EX * C]), sb("wup_h", [P, EX * C], FR), sb("wup_l", [P, EX * C], FR)
        wdn, wdn_h, wdn_l = sb("wdn", [P, EX * C]), sb("wdn_h", [P, EX * C], FR), sb("wdn_l", [P, EX * C], FR)
        wqkv, wqkv_h, wqkv_l = sb("wqkv", [P, 3 * C]), sb("wqkv_h", [P, 3 * C], FR), sb("wqkv_l", [P, 3 * C], FR)
        wex, wex_h, wex_l = sb("wex", [P, E * C]), sb("wex_h", [P, E * C], FR), sb("wex_l", [P, E * C], FR)
        wr1, wr1_h, wr1_l = sb("wr1", [P, F1]), sb("wr1_h", [P, F1], FR), sb("wr1_l", [P, F1], FR)
        wpj = sb("wpj", [P, C])
        wsum, wsum_r, wsum_s = sb("wsum", [V3, C]), sb("wsum_r", [V3, C], FR), sb("wsum_s", [V3, C], FR)
        ident_r = sb("ident_r", [P, P], FR)
        wp1 = sb("wp1", [P, C])
        wr2 = sb("wr2", [F1 + 1, E])
        mhalf = sb("mhalf", [P, NT])

        xs = sb("xs", [P, B, NT, C])
        st0, mv0, ve0, rs0 = sb("st0", [P, NT, 6]), sb("mv0", [P, NT, 2]), sb("ve0", [P, NT]), sb("rs0", [P, NT])
        xn0 = sb("xn0", [P, NT, C])
        xh0, xl0 = sb("xh0", [P, T], FR), sb("xl0", [P, T], FR)
        prj, kT = sb("prj", [PR, T]), sb("kT", [HS, T])
        kvg = sb("kvg", [P, NT, KVG])
        wm = sb("wm", [P, T])
        st_sum = sb("st_sum", [HS, (NT - 1) * V3])
        oh_r, oh_s = sb("oh_r", [V3, T], FR), sb("oh_s", [V3, T], FR)
        sTb = sb("sTb", [P, T])
        top8, topi = sb("top8", [P, NT, E]), sb("topi", [P, NT, E], U32)
        topf = sb("topf", [P, NT, 2])
        lsh, esh = sb("lsh", [P, NT, E]), sb("esh", [P, NT, E])
        onehot = sb("onehot", [P, NT, 2, E])
        tot, e12, den, rden = sb("tot", [P, NT]), sb("e12", [P, NT]), sb("den", [P, NT]), sb("rden", [P, NT])
        w12 = sb("w12", [P, NT, 2])
        ohw = sb("ohw", [P, NT, 2, E])
        comb = sb("comb", [P, NT, E])
        comb3 = sb("comb3", [P, NT, 3 * E], FR)
        combT = sb("combT", [3 * E, T], FR)
        act_s = [sb(f"act_s{i}", [P, T]) for i in range(2)]
        act_c = [sb(f"act_c{i}", [P, T]) for i in range(2)]
        act_h = [sb(f"act_h{i}", [P, T], FR) for i in range(4)]
        act_l = [sb(f"act_l{i}", [P, T], FR) for i in range(4)]
        g0T, pT = sb("g0T", [P, T]), sb("pT", [P, T])
        st1, mv1, ve1, rs1 = sb("st1", [P, NT, 6]), sb("mv1", [P, NT, 2]), sb("ve1", [P, NT]), sb("rs1", [P, NT])
        xn1 = sb("xn1", [P, NT, C])
        xh1, xl1 = sb("xh1", [P, T], FR), sb("xl1", [P, T], FR)
        qk_max = sb("qk_max", [P, NT, 2 * NH])
        qk = sb("qk", [P, NT, 2 * C])
        vv = sb("vv", [P, NT, C + 1])
        qk_sum, qk_rs = sb("qk_sum", [P, NT * 2 * NH]), sb("qk_rs", [P, NT * 2 * NH])
        ctxn = sb("ctxn", [P, C + NH])
        qT = sb("qT", [P, T])
        dinv = sb("dinv", [P, NT, NH])
        att = sb("att", [P, NT, C])
        attT = sb("attT", [P, T])
        hT = sb("hT", [F1 + 1, T])
        top8b, topib = sb("top8b", [P, NT, E]), sb("topib", [P, NT, E], U32)
        topfb = sb("topfb", [P, NT])
        mask = sb("mask", [P, NT, E])
        prod = [sb(f"prod{i}", [P, 2, NT, C]) for i in range(2)]
        sum4 = [sb(f"sum4{i}", [P, NT, C]) for i in range(2)]
        sum2 = [sb(f"sum2{i}", [P, 2, C]) for i in range(2)]
        sel1 = sb("sel1", [P, NT, C])
        g1, sg = sb("g1", [P, NT, C]), sb("sg", [P, NT, C])

        ps = [ctx.enter_context(nc.psum_tensor(f"bank{i}", [P, 512], F32)) for i in range(8)]
        UP = ps[0:2]
        CB, Y = ps[2], ps[3]
        A0, A1 = ps[4:6]
        L0, L1 = ps[6:8]

        ident = cst[:, C_ID:C_ID + P]
        tri = cst[:, C_TRI:C_TRI + P]
        ones2 = cst[0:2, C_ONE:C_ONE + P]

        s_dve_passed = sem("s_dve_passed")
        s_pool_passed = sem("s_pool_passed")
        s_early_in = sem("s_early_in")
        s_late_in = sem("s_late_in")
        s_x0_in = sem("s_x0_in")
        s_x_in = sem("s_x_in")
        s_out_done = sem("s_out_done")
        s_w_split = sem("s_w_split")
        s_fold_done = sem("s_fold_done")
        s_wdn_ready = sem("s_wdn_ready")
        s_l1_ready = sem("s_l1_ready")
        s_consts_ready = sem("s_consts_ready")
        s_memset_ready = sem("s_memset_ready")
        s_bn0 = sem("s_bn0")
        s_stats0 = sem("s_stats0")
        s_ve0 = sem("s_ve0")
        s_rstd0 = sem("s_rstd0")
        s_xn0 = sem("s_xn0")
        s_xT0 = sem("s_xT0")
        s_xh0 = sem("s_xh0")
        s_xl0 = sem("s_xl0")
        s_prj0 = sem("s_prj0")
        s_prj_sb = sem("s_prj_sb")
        s_kvg_ps = sem("s_kvg_ps")
        s_kvg_sb = sem("s_kvg_sb")
        s_wei = sem("s_wei")
        s_wm = sem("s_wm")
        s_stp = sem("s_stp")
        s_st_sb = sem("s_st_sb")
        s_oh_ps = sem("s_oh_ps")
        s_oh_r = sem("s_oh_r")
        s_oh_s = sem("s_oh_s")
        s_sT_ps = sem("s_sT_ps")
        s_sT_sb = sem("s_sT_sb")
        s_top8 = sem("s_top8")
        s_topi = sem("s_topi")
        s_topf = sem("s_topf")
        s_lsh = sem("s_lsh")
        s_esh = sem("s_esh")
        s_onehot = sem("s_onehot")
        s_tot = sem("s_tot")
        s_e12 = sem("s_e12")
        s_den = sem("s_den")
        s_rden = sem("s_rden")
        s_w12 = sem("s_w12")
        s_ohw = sem("s_ohw")
        s_comb = sem("s_comb")
        s_combh = sem("s_combh")
        s_comb3 = sem("s_comb3")
        s_combT_ps = sem("s_combT_ps")
        s_combT = sem("s_combT")
        s_up = sem("s_up")
        s_silu = sem("s_silu")
        s_cbc = sem("s_cbc")
        s_scaled = sem("s_scaled")
        s_act_h = sem("s_act_h")
        s_act_l = sem("s_act_l")
        s_down = sem("s_down")
        s_g0 = sem("s_g0")
        s_pT = sem("s_pT")
        s_pTT = sem("s_pTT")
        s_x1 = sem("s_x1")
        s_bn1 = sem("s_bn1")
        s_stats1 = sem("s_stats1")
        s_ve1 = sem("s_ve1")
        s_rstd1 = sem("s_rstd1")
        s_xn1 = sem("s_xn1")
        s_xT1 = sem("s_xT1")
        s_xh1 = sem("s_xh1")
        s_xl1 = sem("s_xl1")
        s_qkv = sem("s_qkv")
        s_v_sb = sem("s_v_sb")
        s_qk_max = sem("s_qk_max")
        s_qk_sub = sem("s_qk_sub")
        s_qk_exp = sem("s_qk_exp")
        s_qk_sum = sem("s_qk_sum")
        s_qk_rs = sem("s_qk_rs")
        s_qk_sm = sem("s_qk_sm")
        s_ctx = sem("s_ctx")
        s_ctx_sb = sem("s_ctx_sb")
        s_qT_ps = sem("s_qT_ps")
        s_qT = sem("s_qT")
        s_nd = sem("s_nd")
        s_dinv = sem("s_dinv")
        s_att_m = sem("s_att_m")
        s_att = sem("s_att")
        s_attT_ps = sem("s_attT_ps")
        s_attT = sem("s_attT")
        s_s1 = sem("s_s1")
        s_hT_ps = sem("s_hT_ps")
        s_hT = sem("s_hT")
        s_lg = sem("s_lg")
        s_top8b = sem("s_top8b")
        s_topib = sem("s_topib")
        s_topfb = sem("s_topfb")
        s_mask = sem("s_mask")
        s_ex = sem("s_ex")
        s_prod = sem("s_prod")
        s_sum4 = sem("s_sum4")
        s_sum2 = sem("s_sum2")
        s_sel1 = sem("s_sel1")
        s_g1 = sem("s_g1")
        s_sg = sem("s_sg")
        s_fin = sem("s_fin")

        block = ctx.enter_context(nc.Block())

        def positive(n):
            return not isinstance(n, int) or n > 0

        def schedule(eng, first, iteration):
            first()
            iteration(0, True, False, True)
            iteration(1, True, True, True)
            with eng.Fori(2, B - 1) as i:
                iteration(i, True, True, True)
            iteration(B - 1, True, True, False)
            iteration(B, False, True, False)

        @block.sync
        def _(sp):
            def x_dram(a, c, n=1):
                return a[c:c + n].rearrange("b (t p) d -> p (b t) d", p=P)

            sp.dma_start(xs[:, 0], x_dram(x, 0)).then_inc(s_x0_in, 16)
            for dst, src in ((cst, consts), (vec, vecs), (wpr, w_pr), (row, rows), (bdn, b_dn), (wpj, w_pj), (wup, w_up)):
                sp.dma_start(dst[:, :], src).then_inc(s_early_in, 16)
            sp.dma_start(xs[:, 1:B].rearrange("p b t d -> p (b t) d"), x_dram(x, 1, B - 1)).then_inc(s_x_in, 16)
            sp.dma_start(wdn[:, :], w_dn).then_inc(s_early_in, 16)
            for dst, src in ((wqkv, w_qkv), (wex, w_ex), (wp1, w_p1), (wr1, w_r1), (wr2, w_r2)):
                sp.dma_start(dst[:, :], src).then_inc(s_late_in, 16)

            def store(c):
                sp.wait_ge(s_fin, c + 1)
                sp.dma_start(out[bass.ds(c, 1)].rearrange("b (t p) d -> p (b t) d", p=P),
                             xs[:, bass.ds(c, 1)].rearrange("p b t d -> p (b t) d")).then_inc(s_out_done, 16)

            with sp.Fori(0, B) as c:
                store(c)
            sp.wait_ge(s_out_done, 16 * B)

        @block.tensor
        def _(pe):

            def mm(o, l, r, start=True, stop=True):
                return nc.tensor.matmul(o, l, r, start=start, stop=stop, skip_group_check=True)

            def mm3(o, lh, ll, rh, rl, start=True, stop=True):
                mm(o, lh, rh, start, False)
                mm(o, lh, rl, False, False)
                return mm(o, ll, rh, False, stop)

            def transpose_tiles(o, src, w, n):
                for t in range(NT):
                    last = nc.tensor.transpose(o(t), src(t), ident[0:n, 0:n])
                return last

            def a_xT(c):
                pe.wait_ge(s_xn0, c + 1)
                if positive(c):
                    pe.wait_ge(s_combT, c)
                transpose_tiles(lambda t: A0[:, t * P:(t + 1) * P], lambda t: xn0[:, t, :], P, P).then_inc(s_xT0, 1)

            def a_prj(c):
                pe.wait_ge(s_xl0, c + 1)
                if positive(c):
                    pe.wait_ge(s_sT_sb, c)
                mm3(A1[0:PR, :], wpr_h[:, :], wpr_l[:, :], xh0[:, :], xl0[:, :]).then_inc(s_prj0, 1)

            def a_kvg(c):
                pe.wait_ge(s_prj_sb, c + 1)
                transpose_tiles(lambda t: A0[:, t * PR:(t + 1) * PR], lambda t: prj[:, t * P:(t + 1) * P],
                                PR, PR).then_inc(s_kvg_ps, 1)

            def a_wei(c):
                pe.wait_ge(s_prj_sb, c + 1)
                for t in range(NT):
                    s = slice(t * P, (t + 1) * P)
                    last = mm(A1[:, s], kT[:, s], prj[Q_ROW:Q_ROW + HS, s])
                last.then_inc(s_wei, 1)

            def a_state(c):
                pe.wait_ge(s_kvg_sb, c + 1)
                for t in range(NT - 1):
                    n = NT - 1 - t
                    v = kvg[:, t, V_COL:V_COL + V3].rearrange("p (o d) -> p o d", o=1).broadcast_to([P, n, V3])
                    last = mm(A0[0:HS, t * V3:(NT - 1) * V3].rearrange("p (j d) -> p j d", d=V3),
                              kvg[:, t, K_COL:K_COL + HS], v, start=(t == 0), stop=(t == NT - 2))
                last.then_inc(s_stp, 1)

            def a_out(c):
                pe.wait_ge(s_wm, c + 1)
                pe.wait_ge(s_st_sb, c + 1)
                for t in range(NT):
                    s = slice(t * P, (t + 1) * P)
                    last = mm(A0[0:V3, s], kvg[:, t, V_COL:V_COL + V3], wm[:, s], stop=(t == 0))
                    if t:
                        last = mm(A0[0:V3, s], st_sum[:, (t - 1) * V3:t * V3], prj[Q_ROW:Q_ROW + HS, s], start=False)
                last.then_inc(s_oh_ps, 1)

            def a_sT(c):
                pe.wait_ge(s_oh_s, c + 1)
                mm(A1[:, :], wsum_s[:, :], oh_s[:, :]).then_inc(s_sT_ps, 1)

            def a_comb(c):
                pe.wait_ge(s_comb3, c + 1)
                pe.wait_ge(s_oh_s, c + 1)
                for t in range(NT):
                    last = nc.tensor.transpose(A0[0:3 * E, t * P:(t + 1) * P].bitcast(FR), comb3[:, t, :], ident_r[:, :])
                last.then_inc(s_combT_ps, 1)

            def which(k):
                return E if k == 0 else k - 1

            def m_up(c, k):
                if k >= 2:
                    pe.wait_ge(s_silu, c * EX + k - 1)
                else:
                    if positive(c):
                        pe.wait_ge(s_silu, c * EX)
                if k == 0:
                    pe.wait_ge(s_xl0, c + 1)
                e = which(k)
                mm3(UP[k % 2][:, :], wup_h[:, e * C:(e + 1) * C], wup_l[:, e * C:(e + 1) * C],
                    xh0[:, :], xl0[:, :]).then_inc(s_up, 1)

            def m_bcast(c, k):
                if positive(c * E + k - 1):
                    pe.wait_ge(s_scaled, c * E + k - 1)
                if k == 1:
                    pe.wait_ge(s_combT, c + 1)
                mm(CB[:, :], sel_s[:, (k - 1) * C:k * C], combT[0:2 * E, :]).then_inc(s_cbc, 1)

            def m_down(c, k):
                if k == 0:
                    if positive(c):
                        pe.wait_ge(s_x1, c)
                    pe.wait_ge(s_combT, c + 1)
                    pe.wait_ge(s_wdn_ready, 1)
                    mm(Y[:, :], bdn_s[:, :], combT[:, :], stop=False)
                pe.wait_ge(s_act_h, c * EX + k + 1)
                pe.wait_ge(s_act_l, c * EX + k + 1)
                e = which(k)
                mm3(Y[:, :], wdn_h[:, e * C:(e + 1) * C], wdn_l[:, e * C:(e + 1) * C],
                    act_h[k % 4][:, :], act_l[k % 4][:, :], start=False, stop=(k == E)).then_inc(s_down, 1)

            def m_pT(c):
                pe.wait_ge(s_pT, c + 1)
                pe.wait_ge(s_g0, c + 1)
                transpose_tiles(lambda t: Y[:, t * P:(t + 1) * P], lambda t: pT[:, t * P:(t + 1) * P],
                                P, P).then_inc(s_pTT, 1)

            def l_xT(c):
                pe.wait_ge(s_xn1, c + 1)
                if positive(c):
                    pe.wait_ge(s_prod, c * 2 * NT)
                transpose_tiles(lambda t: L0[:, t * P:(t + 1) * P], lambda t: xn1[:, t, :], P, P).then_inc(s_xT1, 1)

            def l_hid(c):
                pe.wait_ge(s_l1_ready, 1)
                pe.wait_ge(s_xl1, c + 1)
                if positive(c):
                    pe.wait_ge(s_sg, c)
                mm3(L1[0:F1, :], wr1_h[:, :], wr1_l[:, :], xh1[:, :], xl1[:, :]).then_inc(s_hT_ps, 1)

            QB = [L0, L1]

            def l_qkv(c, t):
                if t == 0:
                    pe.wait_ge(s_xl1, c + 1)
                if t == 1:
                    pe.wait_ge(s_topib, c + 1)
                if t >= 2:
                    pe.wait_ge(s_qk_sub, c * NT + t - 1)
                s = slice(t * P, (t + 1) * P)
                o = QB[t % 2][:, 0:3 * C]
                mm(o, ones_s[:, :], row_s[:, R_QKV:R_QKV + 3 * C], stop=False)
                mm(o, xh1[:, s], wqkv_h[:, :], False, False)
                mm(o, xl1[:, s], wqkv_h[:, :], False, False)
                mm(o, xh1[:, s], wqkv_l[:, :], False, True).then_inc(s_qkv, 1)

            def l_logits(c):
                pe.wait_ge(s_hT, c + 1)
                for t in range(NT):
                    last = mm(L1[:, t * E:(t + 1) * E], hT[:, t * P:(t + 1) * P], wr2[:, :])
                last.then_inc(s_lg, 1)

            def l_ctx(c):
                pe.wait_ge(s_qk_sm, c + 1)
                pe.wait_ge(s_v_sb, c * NT + NT)
                for t in range(NT):
                    last = mm(L0[:, 0:C + 1], qk[:, t, C:2 * C], vv[:, t, :], start=(t == 0), stop=(t == NT - 1))
                last.then_inc(s_ctx, 1)

            def l_qT(c):
                pe.wait_ge(s_qk_sm, c + 1)
                transpose_tiles(lambda t: L1[:, t * P:(t + 1) * P], lambda t: qk[:, t, 0:C], P, P).then_inc(s_qT_ps, 1)

            def l_nd(c):
                pe.wait_ge(s_qT, c + 1)
                pe.wait_ge(s_ctx_sb, c + 1)
                for t in range(NT):
                    o = QB[t // 2][:, (t % 2) * (C + NH):(t % 2 + 1) * (C + NH)]
                    last = mm(o, qT[:, t * P:(t + 1) * P], ctxn[:, :])
                last.then_inc(s_nd, 1)

            def l_attT(c):
                pe.wait_ge(s_att, c + 1)
                transpose_tiles(lambda t: L1[:, t * P:(t + 1) * P], lambda t: att[:, t, :], P, P).then_inc(s_attT_ps, 1)

            def l_expert(c, n):
                t, half = n // 2, n % 2
                if n == 0:
                    pe.wait_ge(s_att, c + 1)
                elif n == 1:
                    pe.wait_ge(s_attT, c + 1)
                else:
                    pe.wait_ge(s_prod, c * 2 * NT + n - 1)
                s = slice(t * P, (t + 1) * P)
                h = slice(half * 4 * C, (half + 1) * 4 * C)
                o = QB[n % 2][:, :]
                mm(o, ones_s[:, :], row_s[:, R_EXP + half * 4 * C:R_EXP + (half + 1) * 4 * C], stop=False)
                mm(o, xh1[:, s], wex_h[:, h], False, False)
                mm(o, xl1[:, s], wex_h[:, h], False, False)
                mm(o, xh1[:, s], wex_l[:, h], False, True).then_inc(s_ex, 1)

            def l_proj(c):
                pe.wait_ge(s_attT, c + 1)
                pe.wait_ge(s_prod, (c + 1) * 2 * NT)
                mm(L1[:, :], ones_s[:, :], row_s[:, R_PROJ:R_PROJ + T], stop=False)
                for t in range(NT):
                    s = slice(t * P, (t + 1) * P)
                    last = mm(L1[:, s], attT[:, s], wp1[:, :], start=False, stop=(t == NT - 1))
                last.then_inc(s_s1, 1)

            def first():
                pe.wait_ge(s_consts_ready, 1)
                mm(A1[0:V3, 0:C], cst[:, C_FOLD:C_FOLD + V3], wpj[:, :]).then_inc(s_fold_done, 1)
                a_xT(0)
                pe.wait_ge(s_consts_ready, 2)
                a_prj(0)
                a_kvg(0)
                a_wei(0)
                a_state(0)
                a_out(0)
                a_sT(0)
                a_comb(0)

            def iteration(i, has_m, has_l1, has_next):
                if has_m:
                    m_up(i, 0)
                    m_up(i, 1)
                if has_l1:
                    l_hid(i - 1)
                if has_m:
                    m_bcast(i, 1)
                if has_l1:
                    l_qkv(i - 1, 0)
                if has_m:
                    m_up(i, 2)
                    m_bcast(i, 2)
                if has_l1:
                    l_logits(i - 1)
                if has_m:
                    m_up(i, 3)
                    m_bcast(i, 3)
                    m_down(i, 0)
                    m_up(i, 4)
                    m_bcast(i, 4)
                    m_down(i, 1)
                    m_up(i, 5)
                    m_bcast(i, 5)
                    m_down(i, 2)
                    m_up(i, 6)
                    m_bcast(i, 6)
                    m_down(i, 3)
                    m_up(i, 7)
                    m_bcast(i, 7)
                    m_down(i, 4)
                    m_up(i, 8)
                if has_l1:
                    l_qkv(i - 1, 1)
                if has_next:
                    a_xT(i + 1)
                if has_m:
                    m_bcast(i, 8)
                if has_l1:
                    l_qkv(i - 1, 2)
                    l_qkv(i - 1, 3)
                if has_m:
                    m_down(i, 5)
                    m_down(i, 6)
                if has_next:
                    a_prj(i + 1)
                if has_m:
                    m_down(i, 7)
                    m_down(i, 8)
                if has_next:
                    a_kvg(i + 1)
                if has_l1:
                    l_qT(i - 1)
                    l_ctx(i - 1)
                    l_nd(i - 1)
                if has_m:
                    m_pT(i)
                if has_next:
                    a_wei(i + 1)
                    a_state(i + 1)
                if has_l1:
                    l_attT(i - 1)
                    l_expert(i - 1, 0)
                    l_expert(i - 1, 1)
                    l_expert(i - 1, 2)
                    l_expert(i - 1, 3)
                    l_expert(i - 1, 4)
                    l_expert(i - 1, 5)
                    l_expert(i - 1, 6)
                if has_next:
                    a_out(i + 1)
                if has_l1:
                    l_expert(i - 1, 7)
                if has_next:
                    a_sT(i + 1)
                if has_m:
                    l_xT(i)
                if has_l1:
                    l_proj(i - 1)
                if has_next:
                    a_comb(i + 1)

            schedule(pe, first, iteration)

        @block.scalar
        def _(act):

            def identity(o, i, **kw):
                return nc.scalar.activation(o, i, ACT.Identity, **kw)

            def a_xh(c):
                act.wait_ge(s_xT0, c + 1)
                if positive(c * EX):
                    act.wait_ge(s_up, c * EX)
                identity(xh0[:, :], A0[:, :]).then_inc(s_xh0, 1)

            def a_prj(c):
                act.wait_ge(s_prj0, c + 1)
                if positive(c):
                    act.wait_ge(s_oh_ps, c)
                identity(prj[:, :], A1[0:PR, :], bias=vec[0:PR, V_PR:V_PR + 1])
                identity(kT[:, :], A1[K_ROW:K_ROW + HS, :], bias=vec[K_ROW:K_ROW + HS, V_PR:V_PR + 1]).then_inc(s_prj_sb, 1)

            def a_state(c):
                act.wait_ge(s_stp, c + 1)
                identity(st_sum[:, :], A0[0:HS, 0:(NT - 1) * V3]).then_inc(s_st_sb, 1)

            def a_exp(c):
                act.wait_ge(s_lsh, c + 1)
                if positive(c):
                    act.wait_ge(s_w12, c)
                nc.scalar.activation(esh[:, :, :], lsh[:, :, :], ACT.Exp).then_inc(s_esh, 1)

            def a_oh(c):
                act.wait_ge(s_oh_ps, c + 1)
                if positive(c):
                    act.wait_ge(s_oh_s, c)
                identity(oh_r[:, :], A0[0:V3, :]).then_inc(s_oh_r, 1)

            def a_sTb(c):
                act.wait_ge(s_sT_ps, c + 1)
                if positive(c):
                    act.wait_ge(s_pT, c)
                identity(sTb[:, :], A1[:, :], bias=vec[:, V_PROJ:V_PROJ + 1]).then_inc(s_sT_sb, 1)

            def a_combT(c):
                act.wait_ge(s_combT_ps, c + 1)
                if positive(c * EX):
                    act.wait_ge(s_down, c * EX)
                identity(combT[:, :], A0[0:3 * E, :]).then_inc(s_combT, 1)

            def m_silu(c, k):
                e = E if k == 0 else k - 1
                act.wait_ge(s_up, c * EX + k + 1)
                dst = act_s[k % 2]
                if k == 0:
                    if positive(c * E):
                        act.wait_ge(s_scaled, c * E)
                elif k >= 3:
                    if positive(c * E + k - 2):
                        act.wait_ge(s_scaled, c * E + k - 2)
                elif k == 2:
                    act.wait_ge(s_act_l, c * EX + 1)
                    act.wait_ge(s_act_h, c * EX + 1)
                nc.scalar.activation(dst[:, :], UP[k % 2][:, :], ACT.Silu, bias=vec[:, V_UP + e:V_UP + e + 1]).then_inc(s_silu, 1)

            def m_high(c, k):
                if k == 0:
                    act.wait_ge(s_silu, c * EX + 1)
                    src = act_s[0]
                else:
                    if positive(c * E + k):
                        act.wait_ge(s_scaled, c * E + k)
                    src = act_c[k % 2]
                if k >= 4:
                    if positive(c * EX + k - 3):
                        act.wait_ge(s_down, c * EX + k - 3)
                else:
                    if positive(c * EX):
                        act.wait_ge(s_down, c * EX)
                identity(act_h[k % 4][:, :], src[:, :]).then_inc(s_act_h, 1)

            def m_gate(c):
                act.wait_ge(s_down, c * EX + EX)
                if positive(c):
                    act.wait_ge(s_pT, c)
                nc.scalar.activation(g0T[:, :], Y[:, :], ACT.Silu, bias=vec[:, V_SHD:V_SHD + 1]).then_inc(s_g0, 1)

            def l_xh(c):
                act.wait_ge(s_xT1, c + 1)
                if positive(c * 2 * NT):
                    act.wait_ge(s_ex, c * 2 * NT)
                identity(xh1[:, :], L0[:, :]).then_inc(s_xh1, 1)

            def l_v(c, t):
                act.wait_ge(s_qkv, c * NT + t + 1)
                if t == 0:
                    if positive(c):
                        act.wait_ge(s_ctx, c)
                identity(vv[:, t, 0:C], [L0, L1][t % 2][:, 2 * C:3 * C]).then_inc(s_v_sb, 1)

            def l_exp(c, t):
                act.wait_ge(s_qk_sub, c * NT + t + 1)
                nc.scalar.activation(qk[:, t, :], qk[:, t, :], ACT.Exp).then_inc(s_qk_exp, 1)

            def l_relu(c):
                act.wait_ge(s_hT_ps, c + 1)
                if positive(c):
                    act.wait_ge(s_lg, c)
                nc.scalar.activation(hT[0:F1, :], L1[0:F1, :], ACT.Relu, bias=vec[0:F1, V_B1:V_B1 + 1]).then_inc(s_hT, 1)

            def l_qT(c):
                act.wait_ge(s_qT_ps, c + 1)
                if positive(c):
                    act.wait_ge(s_nd, c)
                identity(qT[:, :], L1[:, :]).then_inc(s_qT, 1)

            def l_attT(c):
                act.wait_ge(s_attT_ps, c + 1)
                if positive(c):
                    act.wait_ge(s_s1, c)
                identity(attT[:, :], L1[:, :]).then_inc(s_attT, 1)

            def l_gate(c):
                act.wait_ge(s_sel1, c * NT + NT)
                if positive(c):
                    act.wait_ge(s_sg, c)
                nc.scalar.activation(g1[:, :, :], sel1[:, :, :], ACT.Silu).then_inc(s_g1, 1)

            def first():
                act.wait_ge(s_early_in, 16 * 8)
                identity(sel_s[:, :], cst[0:2 * E, C_SEL:C_SEL + E * C])
                identity(ident_r[:, :], ident)
                identity(ones_s[:, :], ones2).then_inc(s_consts_ready, 1)
                act.wait_ge(s_fold_done, 1)
                identity(wsum[:, :], A1[0:V3, 0:C]).then_inc(s_consts_ready, 1)
                a_xh(0)
                a_prj(0)
                a_state(0)
                a_exp(0)
                a_oh(0)
                a_sTb(0)
                a_combT(0)

            def iteration(i, has_m, has_l1, has_next):
                if has_m:
                    m_silu(i, 0)
                    m_silu(i, 1)
                    m_high(i, 0)
                if has_l1:
                    l_relu(i - 1)
                if has_m:
                    m_silu(i, 2)
                    m_high(i, 1)
                    m_silu(i, 3)
                    m_high(i, 2)
                    m_silu(i, 4)
                    m_high(i, 3)
                if has_l1:
                    l_v(i - 1, 0)
                if has_m:
                    m_silu(i, 5)
                    m_high(i, 4)
                    m_silu(i, 6)
                    m_high(i, 5)
                    m_silu(i, 7)
                    m_high(i, 6)
                    m_silu(i, 8)
                if has_l1:
                    l_v(i - 1, 1)
                    l_exp(i - 1, 0)
                    l_v(i - 1, 2)
                    l_exp(i - 1, 1)
                    l_v(i - 1, 3)
                if has_m:
                    m_high(i, 7)
                if has_next:
                    a_xh(i + 1)
                if has_l1:
                    l_exp(i - 1, 2)
                    l_exp(i - 1, 3)
                if has_m:
                    m_high(i, 8)
                if has_next:
                    a_prj(i + 1)
                if has_m:
                    m_gate(i)
                if has_l1:
                    l_qT(i - 1)
                    l_attT(i - 1)
                if has_next:
                    a_state(i + 1)
                    a_exp(i + 1)
                    a_oh(i + 1)
                    a_sTb(i + 1)
                if has_m:
                    l_xh(i)
                if has_l1:
                    l_gate(i - 1)
                if has_next:
                    a_combT(i + 1)

            schedule(act, first, iteration)

        @block.vector
        def _(dve):
            v = nc.vector


            def passed():
                dve.sem_inc(s_dve_passed, 1)

            def stats(st, src):
                for t in range(NT):
                    last = v.bn_stats(st[:, t, :], src(t))
                return last

            def aggregate(mv, st):
                for t in range(NT):
                    last = v.bn_aggr(mv[:, t, :], st[:, t, :])
                return last

            def normalise(c, s_rstd, s_xT, s_xn, xn, src, mv, rs):
                dve.wait_ge(s_rstd, c + 1)
                if positive(c):
                    dve.wait_ge(s_xT, c)
                for t in range(NT):
                    last = v.tensor_scalar(xn[:, t, :], src(t), mv[:, t, 0:1], rs[:, t:t + 1], ALU.subtract, ALU.mult)
                last.then_inc(s_xn, 1)

            def x_of(c):
                if isinstance(c, int):
                    return lambda t: xs[:, c, t, :]
                return lambda t: xs[:, bass.ds(c, 1), t, :].rearrange("p o d -> p (o d)")

            def a_stats(c):
                passed()
                stats(st0, x_of(c)).then_inc(s_bn0, 1)

            def a_aggr(c):
                dve.wait_ge(s_bn0, c + 1)
                if positive(c):
                    dve.wait_ge(s_rstd0, c)
                    dve.wait_ge(s_xn0, c)
                passed()
                aggregate(mv0, st0).then_inc(s_stats0, 1)

            def a_norm(c):
                normalise(c, s_rstd0, s_xT0, s_xn0, xn0, x_of(c), mv0, rs0)

            def a_xl(c):
                dve.wait_ge(s_xh0, c + 1)
                if positive(c * EX):
                    dve.wait_ge(s_up, c * EX)
                v.tensor_tensor(xl0[:, :], A0[:, :], xh0[:, :].bitcast(F32), ALU.subtract).then_inc(s_xl0, 1)

            def a_kvg(c):
                dve.wait_ge(s_kvg_ps, c + 1)
                if positive(c):
                    dve.wait_ge(s_oh_ps, c)
                v.tensor_copy(kvg[:, :, :], A0[:, 0:NT * PR].rearrange("p (t n) -> p t n", t=NT)[:, :, K_ROW:PR]).then_inc(s_kvg_sb, 1)

            def a_wm(c):
                dve.wait_ge(s_wei, c + 1)
                v.tensor_tensor(wm[:, :].rearrange("p (t n) -> p t n", t=NT), A1[:, :].rearrange("p (t n) -> p t n", t=NT),
                                tri.rearrange("p (o n) -> p o n", o=1).broadcast_to([P, NT, P]), ALU.mult).then_inc(s_wm, 1)

            def a_top8(c):
                dve.wait_ge(s_kvg_sb, c + 1)
                if positive(c):
                    dve.wait_ge(s_lsh, c)
                passed()
                for t in range(NT):
                    last = v.max(top8[:, t, :], kvg[:, t, G_COL:G_COL + E])
                last.then_inc(s_top8, 1)

            def a_topi(c):
                dve.wait_ge(s_top8, c + 1)
                if positive(c):
                    dve.wait_ge(s_topf, c)
                passed()
                for t in range(NT):
                    last = v.max_index(topi[:, t, :], top8[:, t, :], kvg[:, t, G_COL:G_COL + E])
                last.then_inc(s_topi, 1)

            def a_onehot(c):
                dve.wait_ge(s_topi, c + 1)
                v.tensor_copy(topf[:, :, :], topi[:, :, 0:2]).then_inc(s_topf, 1)
                dve.wait_ge(s_topf, c + 1)
                if positive(c):
                    dve.wait_ge(s_ohw, c)
                v.tensor_tensor(onehot[:, :, :, :].rearrange("p t k e -> p (t k) e"),
                                cst[:, C_IOTA:C_IOTA + E].rearrange("p (o e) -> p o e", o=1).broadcast_to([P, NT * 2, E]),
                                topf[:, :, :].rearrange("p t (k o) -> p (t k) o", o=1).broadcast_to([P, NT * 2, E]),
                                ALU.is_equal).then_inc(s_onehot, 1)

            def a_tot(c):
                dve.wait_ge(s_esh, c + 1)
                v.tensor_reduce(tot[:, :], esh[:, :, :], AX_X, ALU.add).then_inc(s_tot, 1)

            def a_den(c):
                dve.wait_ge(s_e12, c + 1)
                dve.wait_ge(s_tot, c + 1)
                v.scalar_tensor_tensor(den[:, :], tot[:, :], TINY, e12[:, :], ALU.mult, ALU.add).then_inc(s_den, 1)
                dve.wait_ge(s_den, c + 1)
                if positive(c):
                    dve.wait_ge(s_w12, c)
                v.reciprocal(rden[:, :], den[:, :]).then_inc(s_rden, 1)

            def a_ohs(c):
                dve.wait_ge(s_oh_r, c + 1)
                if positive(c):
                    dve.wait_ge(s_sT_ps, c)
                v.scalar_tensor_tensor(oh_s[:, :], oh_r[:, :].bitcast(F32), cst[0:V3, C_M24:C_M24 + 1], A0[0:V3, :],
                                       ALU.mult, ALU.add).then_inc(s_oh_s, 1)

            def m_scale(c, k):
                dve.wait_ge(s_silu, c * EX + k + 1)
                if positive(c * E + k):
                    dve.wait_ge(s_cbc, c * E + k)
                if k >= 3:
                    if positive(c * EX + k - 1):
                        dve.wait_ge(s_act_l, c * EX + k - 1)
                else:
                    if positive(c * EX):
                        dve.wait_ge(s_act_l, c * EX)
                if k >= 3:
                    if positive(c * EX + k - 1):
                        dve.wait_ge(s_act_h, c * EX + k - 1)
                else:
                    if positive(c * EX):
                        dve.wait_ge(s_act_h, c * EX)
                v.tensor_tensor(act_c[k % 2][:, :], act_s[k % 2][:, :], CB[:, :], ALU.mult).then_inc(s_scaled, 1)

            def m_pT(c):
                dve.wait_ge(s_g0, c + 1)
                dve.wait_ge(s_sT_sb, c + 1)
                if positive(c):
                    dve.wait_ge(s_pTT, c)
                v.tensor_tensor(pT[:, :], g0T[:, :], sTb[:, :], ALU.mult).then_inc(s_pT, 1)

            def m_x1(c):
                dve.wait_ge(s_pTT, c + 1)
                x_c = xs[:, c] if isinstance(c, int) else xs[:, bass.ds(c, 1)].rearrange("p o t d -> p (o t) d")
                v.tensor_tensor(x_c, Y[:, :].rearrange("p (t d) -> p t d", t=NT), x_c, ALU.add).then_inc(s_x1, 1)

            def l_stats(c):
                dve.wait_ge(s_x1, c + 1)
                passed()
                stats(st1, x_of(c)).then_inc(s_bn1, 1)

            def l_aggr(c):
                dve.wait_ge(s_bn1, c + 1)
                if positive(c):
                    dve.wait_ge(s_rstd1, c)
                    dve.wait_ge(s_xn1, c)
                passed()
                aggregate(mv1, st1).then_inc(s_stats1, 1)

            def l_norm(c):
                normalise(c, s_rstd1, s_xT1, s_xn1, xn1, x_of(c), mv1, rs1)

            def l_xl(c):
                dve.wait_ge(s_xh1, c + 1)
                v.tensor_tensor(xl1[:, :], L0[:, :], xh1[:, :].bitcast(F32), ALU.subtract).then_inc(s_xl1, 1)

            def l_max(c, t):
                dve.wait_ge(s_v_sb, c * NT + t + 1)
                z = [L0, L1][t % 2][:, 0:2 * C].rearrange("p (h d) -> p h d", d=HS)
                if t == 0:
                    if positive(c):
                        dve.wait_ge(s_qT_ps, c)
                    if positive(c):
                        dve.wait_ge(s_att, c)
                v.tensor_reduce(qk_max[:, t, :], z, AX_X, ALU.max).then_inc(s_qk_max, 1)

            def l_subtract(c, t):
                z = [L0, L1][t % 2][:, 0:2 * C].rearrange("p (h d) -> p h d", d=HS)
                dve.wait_ge(s_qk_max, c * NT + t + 1)
                v.tensor_tensor(qk[:, t, :].rearrange("p (h d) -> p h d", d=HS), z,
                                qk_max[:, t, :].rearrange("p (h o) -> p h o", o=1).broadcast_to([P, 2 * NH, HS]),
                                ALU.subtract).then_inc(s_qk_sub, 1)

            def l_total(c):
                dve.wait_ge(s_qk_exp, c * NT + NT)
                a = qk[:, :, :].rearrange("p t (h d) -> p (t h) d", d=HS)
                v.tensor_reduce(qk_sum[:, :], a, AX_X, ALU.add).then_inc(s_qk_sum, 1)

            def l_recip(c):
                dve.wait_ge(s_qk_sum, c + 1)
                v.reciprocal(qk_rs[:, :], qk_sum[:, :]).then_inc(s_qk_rs, 1)

            def l_softmax(c):
                a = qk[:, :, :].rearrange("p t (h d) -> p (t h) d", d=HS)
                dve.wait_ge(s_qk_rs, c + 1)
                v.tensor_tensor(a, a, qk_rs[:, :].rearrange("p (h o) -> p h o", o=1).broadcast_to([P, NT * 2 * NH, HS]),
                                ALU.mult).then_inc(s_qk_sm, 1)

            def l_ctx(c):
                dve.wait_ge(s_ctx, c + 1)
                if positive(c):
                    dve.wait_ge(s_nd, c)
                v.tensor_tensor(ctxn[:, 0:C], L0[:, 0:C], cst[:, C_BLK:C_BLK + C], ALU.mult)
                v.tensor_scalar(ctxn[:, C:C + NH], cst[:, C_IND:C_IND + NH], L0[:, C:C + 1], None, ALU.mult).then_inc(s_ctx_sb, 1)

            def l_dinv(c):
                dve.wait_ge(s_nd, c + 1)
                if positive(c):
                    dve.wait_ge(s_attT_ps, c)
                for b, z in enumerate((L0, L1)):
                    zz = z[:, 0:2 * (C + NH)].rearrange("p (t n) -> p t n", t=2)
                    last = v.reciprocal(dinv[:, 2 * b:2 * b + 2, :], zz[:, :, C:C + NH])
                last.then_inc(s_dinv, 1)

            def l_attm(c):
                dve.wait_ge(s_dinv, c + 1)
                for b, z in enumerate((L0, L1)):
                    for u in range(2):
                        t = 2 * b + u
                        o = u * (C + NH)
                        last = v.tensor_tensor(att[:, t, :].rearrange("p (h d) -> p h d", d=HS),
                                               z[:, o:o + C].rearrange("p (h d) -> p h d", d=HS),
                                               dinv[:, t, :].rearrange("p (h o) -> p h o", o=1).broadcast_to([P, NH, HS]), ALU.mult)
                last.then_inc(s_att_m, 1)

            def l_addq(c):
                dve.wait_ge(s_att_m, c + 1)
                v.tensor_tensor(att[:, :, :], att[:, :, :], qk[:, :, 0:C], ALU.add).then_inc(s_att, 1)

            def l_top8(c):
                dve.wait_ge(s_lg, c + 1)
                passed()
                for t in range(NT):
                    last = v.max(top8b[:, t, :], L1[:, t * E:(t + 1) * E])
                last.then_inc(s_top8b, 1)

            def l_topi(c):
                dve.wait_ge(s_top8b, c + 1)
                passed()
                for t in range(NT):
                    last = v.max_index(topib[:, t, :], top8b[:, t, :], L1[:, t * E:(t + 1) * E])
                last.then_inc(s_topib, 1)

            def l_mask(c):
                dve.wait_ge(s_topib, c + 1)
                if positive(c):
                    dve.wait_ge(s_mask, c)
                v.tensor_copy(topfb[:, :], topib[:, :, 0]).then_inc(s_topfb, 1)
                dve.wait_ge(s_topfb, c + 1)
                v.tensor_tensor(mask[:, :, :], cst[:, C_IOTA:C_IOTA + E].rearrange("p (o e) -> p o e", o=1).broadcast_to([P, NT, E]),
                                topfb[:, :].rearrange("p (t o) -> p t o", o=1).broadcast_to([P, NT, E]), ALU.is_equal).then_inc(s_mask, 1)

            def l_prod(c, n):
                t, half = n // 2, n % 2
                dve.wait_ge(s_ex, c * 2 * NT + n + 1)
                if n == 0:
                    dve.wait_ge(s_mask, c + 1)
                if half == 0:
                    if t >= 2:
                        if positive(c * NT + t - 1):
                            dve.wait_ge(s_sum4, c * NT + t - 1)
                    else:
                        if positive(c * NT):
                            dve.wait_ge(s_sum4, c * NT)
                v.tensor_tensor(prod[t % 2][:, half], [L0, L1][n % 2][:, :].rearrange("p (e d) -> p e d", d=C),
                                mask[:, t, half * 4:half * 4 + 4].rearrange("p (e o) -> p e o", o=1).broadcast_to([P, 4, C]),
                                ALU.mult).then_inc(s_prod, 1)

            def l_sg(c):
                dve.wait_ge(s_s1, c + 1)
                dve.wait_ge(s_g1, c + 1)
                if positive(c):
                    dve.wait_ge(s_fin, c)
                v.tensor_tensor(sg[:, :, :], L1[:, :].rearrange("p (t d) -> p t d", t=NT), g1[:, :, :], ALU.mult).then_inc(s_sg, 1)

            def split(h, l, w):
                v.tensor_copy(h[:, :], w[:, :]).then_inc(s_w_split, 1)
                nsplit[0] += 1
                dve.wait_ge(s_w_split, nsplit[0])
                return v.tensor_tensor(l[:, :], w[:, :], h[:, :].bitcast(F32), ALU.subtract)

            def stack(s, r, w, m):
                v.tensor_copy(r[:, :], w[:, :]).then_inc(s_w_split, 1)
                nsplit[0] += 1
                dve.wait_ge(s_w_split, nsplit[0])
                v.scalar_tensor_tensor(s[:, :], r[:, :].bitcast(F32), m, w[:, :], ALU.mult, ALU.add).then_inc(s_w_split, 1)
                nsplit[0] += 1

            nsplit = [0]

            def first():
                dve.wait_ge(s_x0_in, 16)
                a_stats(0)
                a_aggr(0)
                dve.wait_ge(s_early_in, 16 * 8)
                split(wpr_h, wpr_l, wpr)
                a_norm(0)
                split(wup_h, wup_l, wup)
                a_xl(0)
                dve.wait_ge(s_consts_ready, 2)
                stack(wsum_s, wsum_r, wsum, cst[0:V3, C_MW:C_MW + 1])
                a_kvg(0)
                a_wm(0)
                a_top8(0)
                a_topi(0)
                a_onehot(0)
                a_ohs(0)
                a_tot(0)
                a_den(0)
                stack(bdn_s, bdn_r, bdn, cst[0:3 * E, C_M24:C_M24 + 1])
                split(wdn_h, wdn_l, wdn).then_inc(s_wdn_ready, 1)
                dve.wait_ge(s_late_in, 16 * 5)
                stack(row_s, row_r, row, cst[0:2, C_M2:C_M2 + 1])
                v.memset(vv[:, :, C:C + 1], 1.0)
                v.memset(hT[F1:F1 + 1, :], 1.0)
                split(wqkv_h, wqkv_l, wqkv)
                split(wr1_h, wr1_l, wr1)
                split(wex_h, wex_l, wex).then_inc(s_l1_ready, 1)
                dve.wait_ge(s_x_in, 16)

            def iteration(i, has_m, has_l1, has_next):
                if has_next:
                    a_stats(i + 1)
                    a_aggr(i + 1)
                if has_m:
                    m_scale(i, 1)
                    m_scale(i, 2)
                if has_l1:
                    l_top8(i - 1)
                if has_m:
                    m_scale(i, 3)
                if has_next:
                    a_norm(i + 1)
                if has_m:
                    m_scale(i, 4)
                    m_scale(i, 5)
                if has_l1:
                    l_max(i - 1, 0)
                    l_topi(i - 1)
                if has_m:
                    m_scale(i, 6)
                    m_scale(i, 7)
                if has_l1:
                    l_subtract(i - 1, 0)
                    l_max(i - 1, 1)
                    l_mask(i - 1)
                    l_subtract(i - 1, 1)
                if has_m:
                    m_scale(i, 8)
                if has_l1:
                    l_max(i - 1, 2)
                    l_subtract(i - 1, 2)
                    l_max(i - 1, 3)
                    l_subtract(i - 1, 3)
                if has_next:
                    a_xl(i + 1)
                if has_l1:
                    l_total(i - 1)
                    l_recip(i - 1)
                    l_softmax(i - 1)
                if has_m:
                    m_pT(i)
                if has_l1:
                    l_ctx(i - 1)
                if has_next:
                    a_kvg(i + 1)
                    a_top8(i + 1)
                if has_l1:
                    l_dinv(i - 1)
                    l_attm(i - 1)
                    l_addq(i - 1)
                if has_m:
                    m_x1(i)
                    l_stats(i)
                    l_aggr(i)
                if has_l1:
                    l_prod(i - 1, 0)
                    l_prod(i - 1, 1)
                if has_next:
                    a_wm(i + 1)
                if has_l1:
                    l_prod(i - 1, 2)
                    l_prod(i - 1, 3)
                if has_next:
                    a_topi(i + 1)
                if has_l1:
                    l_prod(i - 1, 4)
                if has_m:
                    l_norm(i)
                if has_l1:
                    l_prod(i - 1, 5)
                    l_prod(i - 1, 6)
                if has_next:
                    a_onehot(i + 1)
                    a_ohs(i + 1)
                    a_tot(i + 1)
                    a_den(i + 1)
                if has_l1:
                    l_prod(i - 1, 7)
                if has_m:
                    l_xl(i)
                if has_l1:
                    l_sg(i - 1)

            schedule(dve, first, iteration)

        @block.gpsimd
        def _(pool):
            g = nc.gpsimd


            def passed():
                pool.sem_inc(s_pool_passed, 1)

            def rstd(c, s_stats, s_ve, s_xn, s_rstd, mv, ve, rs):
                pool.wait_ge(s_stats, c + 1)
                passed()
                g.tensor_scalar(ve[:, :], mv[:, :, 1], EPS, 1.0, ALU.add, ALU.mult).then_inc(s_ve, 1)
                pool.wait_ge(s_ve, c + 1)
                if positive(c):
                    pool.wait_ge(s_xn, c)
                g.tensor_tensor(rs[:, :], ve[:, :], mhalf[:, :], ALU.pow).then_inc(s_rstd, 1)

            def a_rstd(c):
                rstd(c, s_stats0, s_ve0, s_xn0, s_rstd0, mv0, ve0, rs0)

            def l_rstd(c):
                rstd(c, s_stats1, s_ve1, s_xn1, s_rstd1, mv1, ve1, rs1)

            def a_lsh(c):
                pool.wait_ge(s_top8, c + 1)
                if positive(c):
                    pool.wait_ge(s_esh, c)
                g.tensor_tensor(lsh[:, :, :], top8[:, :, :], top8[:, :, 0:1].broadcast_to([P, NT, E]), ALU.subtract).then_inc(s_lsh, 1)

            def a_e12(c):
                pool.wait_ge(s_esh, c + 1)
                if positive(c):
                    pool.wait_ge(s_den, c)
                g.tensor_tensor(e12[:, :], esh[:, :, 0], esh[:, :, 1], ALU.add).then_inc(s_e12, 1)

            def a_w12(c):
                pool.wait_ge(s_rden, c + 1)
                g.tensor_tensor(w12[:, :, :], esh[:, :, 0:2], rden[:, :].rearrange("p (t o) -> p t o", o=1).broadcast_to([P, NT, 2]),
                                ALU.mult).then_inc(s_w12, 1)
                pool.wait_ge(s_w12, c + 1)
                pool.wait_ge(s_onehot, c + 1)
                g.tensor_tensor(ohw[:, :, :, :].rearrange("p t k e -> p (t k) e"), onehot[:, :, :, :].rearrange("p t k e -> p (t k) e"),
                                w12[:, :, :].rearrange("p t (k o) -> p (t k) o", o=1).broadcast_to([P, NT * 2, E]),
                                ALU.mult).then_inc(s_ohw, 1)

            def a_comb(c):
                pool.wait_ge(s_ohw, c + 1)
                g.tensor_tensor(comb[:, :, :], ohw[:, :, 0, :], ohw[:, :, 1, :], ALU.add).then_inc(s_comb, 1)
                pool.wait_ge(s_comb, c + 1)
                if positive(c):
                    pool.wait_ge(s_combT_ps, c)
                passed()
                g.tensor_copy(comb3[:, :, 0:E], comb[:, :, :])
                g.tensor_copy(comb3[:, :, 2 * E:3 * E], comb[:, :, :]).then_inc(s_combh, 1)
                pool.wait_ge(s_combh, c + 1)
                g.tensor_tensor(comb3[:, :, E:2 * E], comb[:, :, :], comb3[:, :, 0:E].bitcast(F32), ALU.subtract).then_inc(s_comb3, 1)

            def m_low(c, k):
                pool.wait_ge(s_act_h, c * EX + k + 1)
                if k >= 4:
                    if positive(c * EX + k - 3):
                        pool.wait_ge(s_down, c * EX + k - 3)
                else:
                    if positive(c * EX):
                        pool.wait_ge(s_down, c * EX)
                src = act_s[0] if k == 0 else act_c[k % 2]
                g.tensor_tensor(act_l[k % 4][:, :], src[:, :], act_h[k % 4][:, :].bitcast(F32), ALU.subtract).then_inc(s_act_l, 1)

            def l_sum(c, t):
                pool.wait_ge(s_prod, c * 2 * NT + 2 * t + 2)
                b = t % 2
                if t >= 1:
                    if positive(c * NT + t - 1):
                        pool.wait_ge(s_sum2, c * NT + t - 1)
                g.tensor_tensor(sum4[b][:, :, :], prod[b][:, 0], prod[b][:, 1], ALU.add).then_inc(s_sum4, 1)
                pool.wait_ge(s_sum4, c * NT + t + 1)
                if t >= 1:
                    if positive(c * NT + t - 1):
                        pool.wait_ge(s_sel1, c * NT + t - 1)
                g.tensor_tensor(sum2[b][:, :, :], sum4[b][:, 0:2, :], sum4[b][:, 2:4, :], ALU.add).then_inc(s_sum2, 1)
                pool.wait_ge(s_sum2, c * NT + t + 1)
                if t == 0:
                    if positive(c):
                        pool.wait_ge(s_g1, c)
                g.tensor_tensor(sel1[:, t, :], sum2[b][:, 0, :], sum2[b][:, 1, :], ALU.add).then_inc(s_sel1, 1)

            def l_fin(c):
                pool.wait_ge(s_sg, c + 1)
                x_c = xs[:, c] if isinstance(c, int) else xs[:, bass.ds(c, 1)].rearrange("p o t d -> p (o t) d")
                g.tensor_tensor(x_c, x_c, sg[:, :, :], ALU.add).then_inc(s_fin, 1)

            def first():
                g.memset(mhalf[:, :], -0.5).then_inc(s_memset_ready, 1)
                pool.wait_ge(s_memset_ready, 1)
                a_rstd(0)
                a_lsh(0)
                a_e12(0)
                a_w12(0)
                a_comb(0)

            def iteration(i, has_m, has_l1, has_next):
                if has_m:
                    m_low(i, 0)
                if has_next:
                    a_rstd(i + 1)
                if has_m:
                    m_low(i, 1)
                    m_low(i, 2)
                    m_low(i, 3)
                    m_low(i, 4)
                    m_low(i, 5)
                    m_low(i, 6)
                    m_low(i, 7)
                    m_low(i, 8)
                if has_next:
                    a_lsh(i + 1)
                if has_m:
                    l_rstd(i)
                if has_next:
                    a_e12(i + 1)
                if has_l1:
                    l_sum(i - 1, 0)
                    l_sum(i - 1, 1)
                    l_sum(i - 1, 2)
                if has_next:
                    a_w12(i + 1)
                if has_l1:
                    l_sum(i - 1, 3)
                if has_next:
                    a_comb(i + 1)
                if has_l1:
                    l_fin(i - 1)

            schedule(pool, first, iteration)


def constants():
    c = np.zeros((P, NCONST), np.float32)
    r = np.arange(P)
    c[:, C_ID:C_ID + P] = np.eye(P)
    c[:, C_TRI:C_TRI + P] = r[:, None] <= r[None, :]
    c[:, C_BLK:C_BLK + C] = r[:, None] // HS == r[None, :] // HS
    c[:, C_IND:C_IND + NH] = r[:, None] // HS == np.arange(NH)[None, :]
    c[:, C_FOLD:C_FOLD + V3] = r[:, None] % HS == np.arange(V3)[None, :] % HS
    c[:, C_IOTA:C_IOTA + E] = np.arange(E)[None, :]
    c[0, C_M2] = 0.0
    c[1, C_M2] = -1.0
    c[2 * E:3 * E, C_M24] = -1.0
    c[HS:2 * HS, C_MW] = -1.0
    c[:, C_ONE:C_ONE + P] = 1.0
    for e in range(E):
        c[[e, E + e], C_SEL + e * C:C_SEL + (e + 1) * C] = 1.0
    return c


def kernel(**inputs):
    import concourse.bacc as bacc
    from concourse.bass_utils import run_bass_kernel_spmd

    a = {k: np.asarray(v) for k, v in inputs.items()}
    z = lambda *s: np.zeros(s, np.float32)

    w_pr, b_pr = z(C, PR), z(P)
    for i, at in ((0, Q_ROW), (1, K_ROW), (2, V_ROW), (2, V_ROW + HS), (2, V_ROW + 2 * HS)):
        w_pr[:, at:at + HS] = a["L0_attn_qkv_w"][i * HS:(i + 1) * HS].T
        b_pr[at:at + HS] = a["L0_attn_qkv_b"][i * HS:(i + 1) * HS]
    w_pr[:, G_ROW:G_ROW + E] = a["L0_ffn_gate_w"].T

    def side_by_side(stack, shared):
        return np.concatenate([stack.transpose(1, 0, 2).reshape(C, -1), shared], axis=1)

    vecs = z(P, NVEC)
    vecs[:, V_UP:V_UP + E] = a["L0_ffn_up_b"].T
    vecs[:, V_UP + E] = a["L0_ffn_sh_up_b"]
    vecs[:, V_PR] = b_pr
    vecs[:, V_PROJ] = a["L0_attn_proj_b"]
    vecs[:, V_SHD] = a["L0_ffn_sh_down_b"]
    vecs[0:F1, V_B1] = a["L1_ffn_b1"]
    rows1 = np.concatenate([a["L1_attn_bq"], a["L1_attn_bk"], a["L1_attn_bv"], a["L1_ffn_expert_b"].reshape(-1)]
                           + [a["L1_attn_bp"]] * NT)
    arrays = {
        "x": a["L0_attn_ids"], "consts": constants(), "w_pr": w_pr,
        "w_up": side_by_side(a["L0_ffn_up_w"], a["L0_ffn_sh_up_w"]),
        "w_dn": side_by_side(a["L0_ffn_down_w"], a["L0_ffn_sh_down_w"]),
        "w_pj": a["L0_attn_proj_w"].T, "b_dn": np.concatenate([a["L0_ffn_down_b"]] * 3),
        "vecs": vecs, "rows": np.stack([rows1, rows1]),
        "w_qkv": np.concatenate([a["L1_attn_Wq"].T, a["L1_attn_Wk"].T, a["L1_attn_Wv"].T], axis=1),
        "w_ex": a["L1_ffn_expert_W"].transpose(1, 0, 2).reshape(C, -1),
        "w_p1": a["L1_attn_Wp"].T, "w_r1": a["L1_ffn_W1"],
        "w_r2": np.concatenate([a["L1_ffn_W2"], a["L1_ffn_b2"][None]]),
    }
    arrays = {k: np.ascontiguousarray(v) for k, v in arrays.items()}
    nc = bacc.Bacc("TRN2", target_bir_lowering=False, num_devices=1)
    aps = {k: nc.dram_tensor(k, v.shape, mybir.dt.from_np(v.dtype), kind="ExternalInput").ap() for k, v in arrays.items()}
    out = nc.dram_tensor("out", (B, T, C), F32, kind="ExternalOutput").ap()
    build_program(nc, out=out, **aps)
    r = run_bass_kernel_spmd(nc, [arrays], core_ids=[0])
    return r.results[0]["out"]
```

```python
from contextlib import ExitStack

import numpy as np

import concourse.bass as bass
from concourse import mybir

ALU = mybir.AluOpType
ACT = mybir.ActivationFunctionType
AX_X = mybir.AxisListType.X
F32 = mybir.dt.float32
FR = mybir.dt.float32r
U32 = mybir.dt.uint32

P = 128
C = 128
B, T = 8, 512
NT = T // P
E = 8
EX = E + 1
HS = 8
V3 = 3 * HS
NH = C // HS
F1 = C // 2
NC, NR = 3, 3
EPS = 1e-5
TINY = 1e-20

Q_ROW, K_ROW, V_ROW, G_ROW = 0, 32, 64, 96
PR = G_ROW + E
KVG = PR - K_ROW
K_COL, V_COL, G_COL = 0, V_ROW - K_ROW, G_ROW - K_ROW

C_ID, C_TRI, C_BLK, C_IND, C_FOLD, C_IOTA, C_M2, C_M24, C_MW, C_ONE = 0, 128, 256, 384, 400, 424, 432, 433, 434, 435
NCONST = C_ONE + 128
V_UP, V_PR, V_PROJ, V_SHD, V_B1 = 0, EX, EX + 1, EX + 2, EX + 3
NVEC = EX + 4
R_QKV, R_EXP, R_PROJ = 0, 3 * C, 3 * C + E * C
NROW = R_PROJ + NT * C


def build_program(nc, x, consts, sels, w_pr, w_up, w_dn, w_pj, b_dn, vecs, rows, w_qkv, w_ex, w_p1, w_r1, w_r2, out):
    with ExitStack() as ctx:
        def sb(name, shape, dt=F32):
            return ctx.enter_context(nc.sbuf_tensor(name, shape, dt))

        def sem(name):
            return ctx.enter_context(nc.semaphore(name))

        cst = sb("cst", [P, NCONST])
        sel = sb("sel", [2 * E, E * C])
        vec = sb("vec", [P, NVEC])
        row = sb("row", [2, NROW])
        row_r = sb("row_r", [2, NROW], FR)
        row_s = sb("row_s", [2, NROW], FR)
        bdn = sb("bdn", [3 * E, C])
        bdn_r = sb("bdn_r", [3 * E, C], FR)
        bdn_s = sb("bdn_s", [3 * E, C], FR)
        ones_s = sb("ones_s", [2, P], FR)
        sel_s = sb("sel_s", [2 * E, E * C], FR)
        wpr, wpr_h, wpr_l = sb("wpr", [P, PR]), sb("wpr_h", [P, PR], FR), sb("wpr_l", [P, PR], FR)
        wup, wup_h, wup_l = sb("wup", [P, EX * C]), sb("wup_h", [P, EX * C], FR), sb("wup_l", [P, EX * C], FR)
        wdn, wdn_h, wdn_l = sb("wdn", [P, EX * C]), sb("wdn_h", [P, EX * C], FR), sb("wdn_l", [P, EX * C], FR)
        wqkv, wqkv_h, wqkv_l = sb("wqkv", [P, 3 * C]), sb("wqkv_h", [P, 3 * C], FR), sb("wqkv_l", [P, 3 * C], FR)
        wex, wex_h, wex_l = sb("wex", [P, E * C]), sb("wex_h", [P, E * C], FR), sb("wex_l", [P, E * C], FR)
        wr1, wr1_h, wr1_l = sb("wr1", [P, F1]), sb("wr1_h", [P, F1], FR), sb("wr1_l", [P, F1], FR)
        wpj = sb("wpj", [P, C])
        wsum, wsum_r, wsum_s = sb("wsum", [V3, C]), sb("wsum_r", [V3, C], FR), sb("wsum_s", [V3, C], FR)
        ident_r = sb("ident_r", [P, P], FR)
        wp1 = sb("wp1", [P, C])
        wr2 = sb("wr2", [F1 + 1, E])
        mhalf = sb("mhalf", [P, NT])

        xs = sb("xs", [P, B, NT, C])
        st0, mv0, ve0, rs0 = sb("st0", [P, NT, 6]), sb("mv0", [P, NT, 2]), sb("ve0", [P, NT]), sb("rs0", [P, NT])
        xn0 = sb("xn0", [P, NT, C])
        xh0, xl0 = sb("xh0", [P, T], FR), sb("xl0", [P, T], FR)
        prj, kT = sb("prj", [PR, T]), sb("kT", [HS, T])
        kvg = sb("kvg", [P, NT, KVG])
        wm = sb("wm", [P, T])
        st_sum = sb("st_sum", [HS, (NT - 1) * V3])
        oh_r, oh_s = sb("oh_r", [V3, T], FR), sb("oh_s", [V3, T], FR)
        sTb = sb("sTb", [P, T])
        top8, topi = sb("top8", [P, NT, E]), sb("topi", [P, NT, E], U32)
        topf = sb("topf", [P, NT, 2])
        lsh, esh = sb("lsh", [P, NT, E]), sb("esh", [P, NT, E])
        onehot = sb("onehot", [P, NT, 2, E])
        tot, e12, den, rden = sb("tot", [P, NT]), sb("e12", [P, NT]), sb("den", [P, NT]), sb("rden", [P, NT])
        w12 = sb("w12", [P, NT, 2])
        ohw = sb("ohw", [P, NT, 2, E])
        comb = sb("comb", [P, NT, E])
        comb3 = sb("comb3", [P, NT, 3 * E], FR)
        combT = sb("combT", [3 * E, T], FR)
        act_s = [sb(f"act_s{i}", [P, T]) for i in range(EX)]
        act_c = [sb(f"act_c{i}", [P, T]) for i in range(NC)]
        act_h = [sb(f"act_h{i}", [P, T], FR) for i in range(NR)]
        act_l = [sb(f"act_l{i}", [P, T], FR) for i in range(NR)]
        g0T, pT = sb("g0T", [P, T]), sb("pT", [P, T])
        st1, mv1, ve1, rs1 = sb("st1", [P, NT, 6]), sb("mv1", [P, NT, 2]), sb("ve1", [P, NT]), sb("rs1", [P, NT])
        xn1 = sb("xn1", [P, NT, C])
        xh1, xl1 = sb("xh1", [P, T], FR), sb("xl1", [P, T], FR)
        qk_max = sb("qk_max", [P, NT, 2 * NH])
        qk = sb("qk", [P, NT, 2 * C])
        vv = sb("vv", [P, NT, C + 1])
        qk_sum, qk_rs = sb("qk_sum", [P, NT * 2 * NH]), sb("qk_rs", [P, NT * 2 * NH])
        ctxn = sb("ctxn", [P, C + NH])
        qT = sb("qT", [P, T])
        dinv = sb("dinv", [P, NT, NH])
        att = sb("att", [P, NT, C])
        attT = sb("attT", [P, T])
        hT = sb("hT", [F1 + 1, T])
        top8b, topib = sb("top8b", [P, NT, E]), sb("topib", [P, NT, E], U32)
        topfb = sb("topfb", [P, NT])
        mask = sb("mask", [P, NT, E])
        prod = [sb(f"prod{i}", [P, 2, NT, C]) for i in range(2)]
        sum4 = [sb(f"sum4{i}", [P, NT, C]) for i in range(2)]
        sum2 = [sb(f"sum2{i}", [P, 2, C]) for i in range(2)]
        sel1 = sb("sel1", [P, NT, C])
        g1, sg = sb("g1", [P, NT, C]), sb("sg", [P, NT, C])

        ps = [ctx.enter_context(nc.psum_tensor(f"bank{i}", [P, 512], F32)) for i in range(8)]
        UP = ps[0:2]
        CB, Y = ps[2], ps[3]
        A0, A1 = ps[4:6]
        L0, L1 = ps[6:8]

        ident = cst[:, C_ID:C_ID + P]
        tri = cst[:, C_TRI:C_TRI + P]
        ones2 = cst[0:2, C_ONE:C_ONE + P]

        s_dve_passed = sem("s_dve_passed")
        s_pool_passed = sem("s_pool_passed")
        s_proj_in = sem("s_proj_in")
        s_up_in = sem("s_up_in")
        s_down_in = sem("s_down_in")
        s_late_in = sem("s_late_in")
        s_x0_in = sem("s_x0_in")
        s_x_in = sem("s_x_in")
        s_out_done = sem("s_out_done")
        s_w_split = sem("s_w_split")
        s_fold_done = sem("s_fold_done")
        s_wup_high = sem("s_wup_high")
        s_wup_ready = sem("s_wup_ready")
        s_wdn_ready = sem("s_wdn_ready")
        s_l1_ready = sem("s_l1_ready")
        s_consts_ready = sem("s_consts_ready")
        s_memset_ready = sem("s_memset_ready")
        s_bn0 = sem("s_bn0")
        s_stats0 = sem("s_stats0")
        s_ve0 = sem("s_ve0")
        s_rstd0 = sem("s_rstd0")
        s_xn0 = sem("s_xn0")
        s_xT0 = sem("s_xT0")
        s_xh0 = sem("s_xh0")
        s_xl0 = sem("s_xl0")
        s_prj0 = sem("s_prj0")
        s_prj_sb = sem("s_prj_sb")
        s_kvg_ps = sem("s_kvg_ps")
        s_kvg_sb = sem("s_kvg_sb")
        s_wei = sem("s_wei")
        s_wm = sem("s_wm")
        s_stp = sem("s_stp")
        s_st_sb = sem("s_st_sb")
        s_oh_ps = sem("s_oh_ps")
        s_oh_r = sem("s_oh_r")
        s_oh_s = sem("s_oh_s")
        s_sT_ps = sem("s_sT_ps")
        s_sT_sb = sem("s_sT_sb")
        s_top8 = sem("s_top8")
        s_topi = sem("s_topi")
        s_topf = sem("s_topf")
        s_lsh = sem("s_lsh")
        s_esh = sem("s_esh")
        s_onehot = sem("s_onehot")
        s_tot = sem("s_tot")
        s_e12 = sem("s_e12")
        s_den = sem("s_den")
        s_rden = sem("s_rden")
        s_w12 = sem("s_w12")
        s_ohw = sem("s_ohw")
        s_comb = sem("s_comb")
        s_combh = sem("s_combh")
        s_comb3 = sem("s_comb3")
        s_combT_ps = sem("s_combT_ps")
        s_combT = sem("s_combT")
        s_up = sem("s_up")
        s_silu = sem("s_silu")
        s_cbc = sem("s_cbc")
        s_scaled = sem("s_scaled")
        s_act_h = sem("s_act_h")
        s_act_l = sem("s_act_l")
        s_down = sem("s_down")
        s_g0 = sem("s_g0")
        s_pT = sem("s_pT")
        s_pTT = sem("s_pTT")
        s_x1 = sem("s_x1")
        s_bn1 = sem("s_bn1")
        s_stats1 = sem("s_stats1")
        s_ve1 = sem("s_ve1")
        s_rstd1 = sem("s_rstd1")
        s_xn1 = sem("s_xn1")
        s_xT1 = sem("s_xT1")
        s_xh1 = sem("s_xh1")
        s_xl1 = sem("s_xl1")
        s_qkv = sem("s_qkv")
        s_v_sb = sem("s_v_sb")
        s_qk_max = sem("s_qk_max")
        s_qk_sub = sem("s_qk_sub")
        s_qk_exp = sem("s_qk_exp")
        s_qk_sum = sem("s_qk_sum")
        s_qk_rs = sem("s_qk_rs")
        s_qk_sm = sem("s_qk_sm")
        s_ctx = sem("s_ctx")
        s_ctx_sb = sem("s_ctx_sb")
        s_qT_ps = sem("s_qT_ps")
        s_qT = sem("s_qT")
        s_nd = sem("s_nd")
        s_dinv = sem("s_dinv")
        s_att_m = sem("s_att_m")
        s_att = sem("s_att")
        s_attT_ps = sem("s_attT_ps")
        s_attT = sem("s_attT")
        s_s1 = sem("s_s1")
        s_hT_ps = sem("s_hT_ps")
        s_hT = sem("s_hT")
        s_lg = sem("s_lg")
        s_top8b = sem("s_top8b")
        s_topib = sem("s_topib")
        s_topfb = sem("s_topfb")
        s_mask = sem("s_mask")
        s_ex = sem("s_ex")
        s_prod = sem("s_prod")
        s_sum4 = sem("s_sum4")
        s_sum2 = sem("s_sum2")
        s_sel1 = sem("s_sel1")
        s_g1 = sem("s_g1")
        s_sg = sem("s_sg")
        s_fin = sem("s_fin")

        block = ctx.enter_context(nc.Block())

        def positive(n):
            return not isinstance(n, int) or n > 0

        def after_next(c):
            return min(c + 2, B) if isinstance(c, int) else c + 2

        def schedule(eng, head, iteration, tail):
            head()
            iteration(1)
            with eng.Fori(2, B - 1) as i:
                iteration(i)
            tail()

        @block.sync
        def _(sp):
            def x_dram(a, c, n=1):
                return a[c:c + n].rearrange("b (t p) d -> p (b t) d", p=P)

            sp.dma_start(xs[:, 0], x_dram(x, 0)).then_inc(s_x0_in, 16)
            for dst, src in ((cst, consts), (wpr, w_pr), (vec, vecs), (wpj, w_pj)):
                sp.dma_start(dst[:, :], src).then_inc(s_proj_in, 16)
            for dst, src in ((wup, w_up), (sel, sels)):
                sp.dma_start(dst[:, :], src).then_inc(s_up_in, 16)
            for dst, src in ((wdn, w_dn), (bdn, b_dn)):
                sp.dma_start(dst[:, :], src).then_inc(s_down_in, 16)
            sp.dma_start(xs[:, 1:B].rearrange("p b t d -> p (b t) d"), x_dram(x, 1, B - 1)).then_inc(s_x_in, 16)
            for dst, src in ((row, rows), (wqkv, w_qkv), (wex, w_ex), (wp1, w_p1), (wr1, w_r1), (wr2, w_r2)):
                sp.dma_start(dst[:, :], src).then_inc(s_late_in, 16)

            def store(c):
                sp.wait_ge(s_fin, c + 1)
                sp.dma_start(out[bass.ds(c, 1)].rearrange("b (t p) d -> p (b t) d", p=P),
                             xs[:, bass.ds(c, 1)].rearrange("p b t d -> p (b t) d")).then_inc(s_out_done, 16)

            with sp.Fori(0, B) as c:
                store(c)
            sp.wait_ge(s_out_done, 16 * B)

        @block.tensor
        def _(pe):

            def mm(o, l, r, start=True, stop=True):
                return nc.tensor.matmul(o, l, r, start=start, stop=stop, skip_group_check=True)

            def mm3(o, lh, ll, rh, rl, start=True, stop=True):
                mm(o, lh, rh, start, False)
                mm(o, lh, rl, False, False)
                return mm(o, ll, rh, False, stop)

            def transpose_tiles(o, src, w, n):
                for t in range(NT):
                    last = nc.tensor.transpose(o(t), src(t), ident[0:n, 0:n])
                return last

            def a_xT(c):
                pe.wait_ge(s_xn0, c + 1)
                if positive(c):
                    pe.wait_ge(s_combT, c)
                transpose_tiles(lambda t: A0[:, t * P:(t + 1) * P], lambda t: xn0[:, t, :], P, P).then_inc(s_xT0, 1)

            def a_prj(c):
                pe.wait_ge(s_xl0, c + 1)
                pe.wait_ge(s_consts_ready, 2)
                if positive(c):
                    pe.wait_ge(s_sT_sb, c)
                mm3(A1[0:PR, :], wpr_h[:, :], wpr_l[:, :], xh0[:, :], xl0[:, :]).then_inc(s_prj0, 1)

            def a_kvg(c):
                pe.wait_ge(s_prj_sb, c + 1)
                transpose_tiles(lambda t: A0[:, t * PR:(t + 1) * PR], lambda t: prj[:, t * P:(t + 1) * P],
                                PR, PR).then_inc(s_kvg_ps, 1)

            def a_wei(c):
                pe.wait_ge(s_prj_sb, c + 1)
                for t in range(NT):
                    s = slice(t * P, (t + 1) * P)
                    last = mm(A1[:, s], kT[:, s], prj[Q_ROW:Q_ROW + HS, s])
                last.then_inc(s_wei, 1)

            def a_state(c):
                pe.wait_ge(s_kvg_sb, c + 1)
                for t in range(NT - 1):
                    n = NT - 1 - t
                    v = kvg[:, t, V_COL:V_COL + V3].rearrange("p (o d) -> p o d", o=1).broadcast_to([P, n, V3])
                    last = mm(A0[0:HS, t * V3:(NT - 1) * V3].rearrange("p (j d) -> p j d", d=V3),
                              kvg[:, t, K_COL:K_COL + HS], v, start=(t == 0), stop=(t == NT - 2))
                last.then_inc(s_stp, 1)

            def a_out(c):
                pe.wait_ge(s_wm, c + 1)
                pe.wait_ge(s_st_sb, c + 1)
                for t in range(NT):
                    s = slice(t * P, (t + 1) * P)
                    last = mm(A0[0:V3, s], kvg[:, t, V_COL:V_COL + V3], wm[:, s], stop=(t == 0))
                    if t:
                        last = mm(A0[0:V3, s], st_sum[:, (t - 1) * V3:t * V3], prj[Q_ROW:Q_ROW + HS, s], start=False)
                last.then_inc(s_oh_ps, 1)

            def a_sT(c):
                pe.wait_ge(s_oh_s, c + 1)
                mm(A1[:, :], wsum_s[:, :], oh_s[:, :]).then_inc(s_sT_ps, 1)

            def a_comb(c):
                pe.wait_ge(s_comb3, c + 1)
                pe.wait_ge(s_oh_s, c + 1)
                for t in range(NT):
                    last = nc.tensor.transpose(A0[0:3 * E, t * P:(t + 1) * P].bitcast(FR), comb3[:, t, :], ident_r[:, :])
                last.then_inc(s_combT_ps, 1)

            def which(k):
                return E if k == 0 else k - 1

            def m_up(c, k):
                if k >= 2:
                    pe.wait_ge(s_silu, c * EX + k - 1)
                elif positive(c - 1):
                    pe.wait_ge(s_prod, (c - 1) * 2 * NT)
                if k == 0:
                    if positive(c):
                        pe.wait_ge(s_silu, c * EX)
                    pe.wait_ge(s_xl0, c + 1)
                    pe.wait_ge(s_wup_ready, 1)
                e = which(k)
                mm3(UP[k % 2][:, :], wup_h[:, e * C:(e + 1) * C], wup_l[:, e * C:(e + 1) * C],
                    xh0[:, :], xl0[:, :]).then_inc(s_up, 1)

            def m_bcast(c, k):
                if positive(c * E + k - 1):
                    pe.wait_ge(s_scaled, c * E + k - 1)
                if k == 1:
                    pe.wait_ge(s_combT, c + 1)
                mm(CB[:, :], sel_s[:, (k - 1) * C:k * C], combT[0:2 * E, :]).then_inc(s_cbc, 1)

            def m_down(c, k):
                if k == 0:
                    if positive(c):
                        pe.wait_ge(s_x1, c)
                    pe.wait_ge(s_combT, c + 1)
                    pe.wait_ge(s_wdn_ready, 1)
                    mm(Y[:, :], bdn_s[:, :], combT[:, :], stop=False)
                pe.wait_ge(s_act_h, c * EX + k + 1)
                pe.wait_ge(s_act_l, c * EX + k + 1)
                e = which(k)
                mm3(Y[:, :], wdn_h[:, e * C:(e + 1) * C], wdn_l[:, e * C:(e + 1) * C],
                    act_h[k % NR][:, :], act_l[k % NR][:, :], start=False, stop=(k == E)).then_inc(s_down, 1)

            def m_pT(c):
                pe.wait_ge(s_pT, c + 1)
                pe.wait_ge(s_g0, c + 1)
                transpose_tiles(lambda t: Y[:, t * P:(t + 1) * P], lambda t: pT[:, t * P:(t + 1) * P],
                                P, P).then_inc(s_pTT, 1)

            def l_xT(c):
                pe.wait_ge(s_xn1, c + 1)
                if positive(c):
                    pe.wait_ge(s_att, c)
                transpose_tiles(lambda t: L0[:, t * P:(t + 1) * P], lambda t: xn1[:, t, :], P, P).then_inc(s_xT1, 1)

            def l_hid(c):
                pe.wait_ge(s_l1_ready, 1)
                pe.wait_ge(s_xl1, c + 1)
                if positive(c):
                    pe.wait_ge(s_sg, c)
                mm3(L1[0:F1, :], wr1_h[:, :], wr1_l[:, :], xh1[:, :], xl1[:, :]).then_inc(s_hT_ps, 1)

            QB = [L0, L1]

            def l_qkv(c, t):
                if t == 0:
                    pe.wait_ge(s_xl1, c + 1)
                if t == 1:
                    pe.wait_ge(s_topib, c + 1)
                if t >= 2:
                    pe.wait_ge(s_qk_sub, c * NT + t - 1)
                s = slice(t * P, (t + 1) * P)
                o = QB[t % 2][:, 0:3 * C]
                mm(o, ones_s[:, :], row_s[:, R_QKV:R_QKV + 3 * C], stop=False)
                mm(o, xh1[:, s], wqkv_h[:, :], False, False)
                mm(o, xl1[:, s], wqkv_h[:, :], False, False)
                mm(o, xh1[:, s], wqkv_l[:, :], False, True).then_inc(s_qkv, 1)

            def l_logits(c):
                pe.wait_ge(s_hT, c + 1)
                for t in range(NT):
                    last = mm(L1[:, t * E:(t + 1) * E], hT[:, t * P:(t + 1) * P], wr2[:, :])
                last.then_inc(s_lg, 1)

            def l_ctx(c):
                pe.wait_ge(s_qk_sm, c + 1)
                pe.wait_ge(s_v_sb, c * NT + NT)
                for t in range(NT):
                    last = mm(L0[:, 0:C + 1], qk[:, t, C:2 * C], vv[:, t, :], start=(t == 0), stop=(t == NT - 1))
                last.then_inc(s_ctx, 1)

            def l_qT(c):
                pe.wait_ge(s_qk_sm, c + 1)
                transpose_tiles(lambda t: L1[:, t * P:(t + 1) * P], lambda t: qk[:, t, 0:C], P, P).then_inc(s_qT_ps, 1)

            def l_nd(c):
                pe.wait_ge(s_qT, c + 1)
                pe.wait_ge(s_ctx_sb, c + 1)
                for t in range(NT):
                    o = QB[t // 2][:, (t % 2) * (C + NH):(t % 2 + 1) * (C + NH)]
                    last = mm(o, qT[:, t * P:(t + 1) * P], ctxn[:, :])
                last.then_inc(s_nd, 1)

            def l_attT(c):
                pe.wait_ge(s_att, c + 1)
                transpose_tiles(lambda t: L1[:, t * P:(t + 1) * P], lambda t: att[:, t, :], P, P).then_inc(s_attT_ps, 1)

            def l_expert(c, n):
                t, half = n // 2, n % 2
                if n < 2:
                    pe.wait_ge(s_silu, after_next(c) * EX)
                    pe.wait_ge(s_l1_ready, 1)
                    pe.wait_ge(s_xl1, c + 1)
                else:
                    pe.wait_ge(s_prod, c * 2 * NT + n - 1)
                s = slice(t * P, (t + 1) * P)
                h = slice(half * 4 * C, (half + 1) * 4 * C)
                o = UP[n % 2][:, :]
                mm(o, ones_s[:, :], row_s[:, R_EXP + half * 4 * C:R_EXP + (half + 1) * 4 * C], stop=False)
                mm(o, xh1[:, s], wex_h[:, h], False, False)
                mm(o, xl1[:, s], wex_h[:, h], False, False)
                mm(o, xh1[:, s], wex_l[:, h], False, True).then_inc(s_ex, 1)

            def l_proj(c):
                pe.wait_ge(s_attT, c + 1)
                mm(L1[:, :], ones_s[:, :], row_s[:, R_PROJ:R_PROJ + T], stop=False)
                for t in range(NT):
                    s = slice(t * P, (t + 1) * P)
                    last = mm(L1[:, s], attT[:, s], wp1[:, :], start=False, stop=(t == NT - 1))
                last.then_inc(s_s1, 1)

            def fold():
                pe.wait_ge(s_consts_ready, 1)
                mm(A1[0:V3, 0:C], cst[:, C_FOLD:C_FOLD + V3], wpj[:, :]).then_inc(s_fold_done, 1)


            def head():
                fold()
                a_xT(0)
                a_prj(0)
                m_up(0, 0)
                a_kvg(0)
                a_wei(0)
                m_up(0, 1)
                a_state(0)
                a_out(0)
                m_up(0, 2)
                a_sT(0)
                m_up(0, 3)
                m_up(0, 4)
                a_comb(0)
                m_up(0, 5)
                m_bcast(0, 1)
                m_up(0, 6)
                m_up(0, 7)
                m_bcast(0, 2)
                m_up(0, 8)
                a_xT(1)
                m_bcast(0, 3)
                m_down(0, 0)
                m_bcast(0, 4)
                m_down(0, 1)
                a_prj(1)
                m_bcast(0, 5)
                m_down(0, 2)
                m_bcast(0, 6)
                m_down(0, 3)
                a_kvg(1)
                m_bcast(0, 7)
                m_down(0, 4)
                a_wei(1)
                m_bcast(0, 8)
                m_down(0, 5)
                m_down(0, 6)
                a_state(1)
                m_down(0, 7)
                m_down(0, 8)
                a_out(1)
                m_pT(0)
                a_sT(1)
                l_xT(0)
                a_comb(1)

            def iteration(i):
                m_up(i, 0)
                m_up(i, 1)
                m_bcast(i, 1)
                m_up(i, 2)
                l_hid(i - 1)
                l_qkv(i - 1, 0)
                m_bcast(i, 2)
                m_up(i, 3)
                m_up(i, 4)
                l_logits(i - 1)
                m_up(i, 5)
                m_up(i, 6)
                m_bcast(i, 3)
                a_xT(i + 1)
                m_up(i, 7)
                m_up(i, 8)
                m_down(i, 0)
                l_qkv(i - 1, 1)
                m_bcast(i, 4)
                m_down(i, 1)
                l_qkv(i - 1, 2)
                l_expert(i - 1, 0)
                m_bcast(i, 5)
                a_prj(i + 1)
                m_down(i, 2)
                l_qkv(i - 1, 3)
                m_bcast(i, 6)
                m_down(i, 3)
                a_kvg(i + 1)
                m_bcast(i, 7)
                l_expert(i - 1, 1)
                m_down(i, 4)
                m_bcast(i, 8)
                a_wei(i + 1)
                m_down(i, 5)
                l_expert(i - 1, 2)
                m_down(i, 6)
                a_state(i + 1)
                m_down(i, 7)
                m_down(i, 8)
                l_expert(i - 1, 3)
                a_out(i + 1)
                l_expert(i - 1, 4)
                m_pT(i)
                l_qT(i - 1)
                l_ctx(i - 1)
                a_sT(i + 1)
                l_expert(i - 1, 5)
                l_nd(i - 1)
                a_comb(i + 1)
                l_expert(i - 1, 6)
                l_expert(i - 1, 7)
                l_attT(i - 1)
                l_proj(i - 1)
                l_xT(i)

            def tail():
                m_up(B - 1, 0)
                m_up(B - 1, 1)
                m_bcast(B - 1, 1)
                m_up(B - 1, 2)
                l_hid(B - 2)
                l_qkv(B - 2, 0)
                m_up(B - 1, 3)
                m_bcast(B - 1, 2)
                m_up(B - 1, 4)
                l_logits(B - 2)
                m_bcast(B - 1, 3)
                m_up(B - 1, 5)
                m_up(B - 1, 6)
                m_down(B - 1, 0)
                l_qkv(B - 2, 1)
                m_bcast(B - 1, 4)
                m_down(B - 1, 1)
                m_up(B - 1, 7)
                m_bcast(B - 1, 5)
                m_up(B - 1, 8)
                l_qkv(B - 2, 2)
                m_down(B - 1, 2)
                m_bcast(B - 1, 6)
                l_expert(B - 2, 0)
                l_qkv(B - 2, 3)
                m_down(B - 1, 3)
                m_bcast(B - 1, 7)
                m_down(B - 1, 4)
                l_expert(B - 2, 1)
                m_bcast(B - 1, 8)
                m_down(B - 1, 5)
                l_expert(B - 2, 2)
                m_down(B - 1, 6)
                m_down(B - 1, 7)
                l_expert(B - 2, 3)
                m_down(B - 1, 8)
                l_expert(B - 2, 4)
                l_expert(B - 2, 5)
                l_qT(B - 2)
                l_ctx(B - 2)
                m_pT(B - 1)
                l_nd(B - 2)
                l_expert(B - 2, 6)
                l_expert(B - 2, 7)
                l_attT(B - 2)
                l_xT(B - 1)
                l_proj(B - 2)
                l_hid(B - 1)
                l_qkv(B - 1, 0)
                l_logits(B - 1)
                l_expert(B - 1, 0)
                l_qkv(B - 1, 1)
                l_qkv(B - 1, 2)
                l_expert(B - 1, 1)
                l_qkv(B - 1, 3)
                l_expert(B - 1, 2)
                l_expert(B - 1, 3)
                l_expert(B - 1, 4)
                l_expert(B - 1, 5)
                l_expert(B - 1, 6)
                l_qT(B - 1)
                l_ctx(B - 1)
                l_expert(B - 1, 7)
                l_nd(B - 1)
                l_attT(B - 1)
                l_proj(B - 1)

            schedule(pe, head, iteration, tail)

        @block.scalar
        def _(act):

            def identity(o, i, **kw):
                return nc.scalar.activation(o, i, ACT.Identity, **kw)

            def a_xh(c):
                act.wait_ge(s_xT0, c + 1)
                if positive(c * EX):
                    act.wait_ge(s_up, c * EX)
                identity(xh0[:, :], A0[:, :]).then_inc(s_xh0, 1)

            def a_prj(c):
                act.wait_ge(s_prj0, c + 1)
                if positive(c):
                    act.wait_ge(s_oh_ps, c)
                identity(prj[:, :], A1[0:PR, :], bias=vec[0:PR, V_PR:V_PR + 1])
                identity(kT[:, :], A1[K_ROW:K_ROW + HS, :], bias=vec[K_ROW:K_ROW + HS, V_PR:V_PR + 1]).then_inc(s_prj_sb, 1)

            def a_state(c):
                act.wait_ge(s_stp, c + 1)
                identity(st_sum[:, :], A0[0:HS, 0:(NT - 1) * V3]).then_inc(s_st_sb, 1)

            def a_exp(c):
                act.wait_ge(s_lsh, c + 1)
                if positive(c):
                    act.wait_ge(s_w12, c)
                nc.scalar.activation(esh[:, :, :], lsh[:, :, :], ACT.Exp).then_inc(s_esh, 1)

            def a_oh(c):
                act.wait_ge(s_oh_ps, c + 1)
                if positive(c):
                    act.wait_ge(s_oh_s, c)
                identity(oh_r[:, :], A0[0:V3, :]).then_inc(s_oh_r, 1)

            def a_sTb(c):
                act.wait_ge(s_sT_ps, c + 1)
                if positive(c):
                    act.wait_ge(s_pT, c)
                identity(sTb[:, :], A1[:, :], bias=vec[:, V_PROJ:V_PROJ + 1]).then_inc(s_sT_sb, 1)

            def a_combT(c):
                act.wait_ge(s_combT_ps, c + 1)
                if positive(c * EX):
                    act.wait_ge(s_down, c * EX)
                identity(combT[:, :], A0[0:3 * E, :]).then_inc(s_combT, 1)

            def m_silu(c, k):
                e = E if k == 0 else k - 1
                act.wait_ge(s_up, c * EX + k + 1)
                if k == 0:
                    if positive(c):
                        act.wait_ge(s_act_l, (c - 1) * EX + 1)
                        act.wait_ge(s_act_h, (c - 1) * EX + 1)
                else:
                    if positive(c):
                        act.wait_ge(s_scaled, (c - 1) * E + k)
                nc.scalar.activation(act_s[k][:, :], UP[k % 2][:, :], ACT.Silu, bias=vec[:, V_UP + e:V_UP + e + 1]).then_inc(s_silu, 1)

            def m_high(c, k):
                if k == 0:
                    act.wait_ge(s_silu, c * EX + 1)
                    src = act_s[0]
                else:
                    act.wait_ge(s_scaled, c * E + k)
                    src = act_c[k % NC]
                if positive(c * EX + k - NR + 1):
                    act.wait_ge(s_down, c * EX + k - NR + 1)
                identity(act_h[k % NR][:, :], src[:, :]).then_inc(s_act_h, 1)

            def m_gate(c):
                act.wait_ge(s_down, c * EX + EX)
                if positive(c):
                    act.wait_ge(s_pT, c)
                nc.scalar.activation(g0T[:, :], Y[:, :], ACT.Silu, bias=vec[:, V_SHD:V_SHD + 1]).then_inc(s_g0, 1)

            def l_xh(c):
                act.wait_ge(s_xT1, c + 1)
                if positive(c * 2 * NT):
                    act.wait_ge(s_ex, c * 2 * NT)
                identity(xh1[:, :], L0[:, :]).then_inc(s_xh1, 1)

            def l_v(c, t):
                act.wait_ge(s_qkv, c * NT + t + 1)
                if t == 0:
                    if positive(c):
                        act.wait_ge(s_ctx, c)
                identity(vv[:, t, 0:C], [L0, L1][t % 2][:, 2 * C:3 * C]).then_inc(s_v_sb, 1)

            def l_exp(c, t):
                act.wait_ge(s_qk_sub, c * NT + t + 1)
                nc.scalar.activation(qk[:, t, :], qk[:, t, :], ACT.Exp).then_inc(s_qk_exp, 1)

            def l_relu(c):
                act.wait_ge(s_hT_ps, c + 1)
                if positive(c):
                    act.wait_ge(s_lg, c)
                nc.scalar.activation(hT[0:F1, :], L1[0:F1, :], ACT.Relu, bias=vec[0:F1, V_B1:V_B1 + 1]).then_inc(s_hT, 1)

            def l_qT(c):
                act.wait_ge(s_qT_ps, c + 1)
                if positive(c):
                    act.wait_ge(s_nd, c)
                identity(qT[:, :], L1[:, :]).then_inc(s_qT, 1)

            def l_attT(c):
                act.wait_ge(s_attT_ps, c + 1)
                if positive(c):
                    act.wait_ge(s_s1, c)
                identity(attT[:, :], L1[:, :]).then_inc(s_attT, 1)

            def l_gate(c):
                act.wait_ge(s_sel1, c * NT + NT)
                if positive(c):
                    act.wait_ge(s_sg, c)
                nc.scalar.activation(g1[:, :, :], sel1[:, :, :], ACT.Silu).then_inc(s_g1, 1)

            def consts_parts():
                act.wait_ge(s_proj_in, 16 * 4)
                identity(ident_r[:, :], ident)
                identity(ones_s[:, :], ones2).then_inc(s_consts_ready, 1)

            def fold():
                act.wait_ge(s_fold_done, 1)
                identity(wsum[:, :], A1[0:V3, 0:C]).then_inc(s_consts_ready, 1)

            def wup_high():
                act.wait_ge(s_up_in, 16 * 2)
                identity(wup_h[:, :], wup[:, :]).then_inc(s_wup_high, 1)

            def selectors_part():
                act.wait_ge(s_up_in, 16 * 2)
                identity(sel_s[:, :], sel[:, :])


            def head():
                consts_parts()
                fold()
                wup_high()
                a_xh(0)
                a_prj(0)
                selectors_part()
                m_silu(0, 0)
                a_state(0)
                m_silu(0, 1)
                a_exp(0)
                a_oh(0)
                m_silu(0, 2)
                m_silu(0, 3)
                a_sTb(0)
                m_silu(0, 4)
                a_combT(0)
                m_silu(0, 5)
                m_high(0, 0)
                m_silu(0, 6)
                m_high(0, 1)
                m_high(0, 2)
                a_xh(1)
                m_silu(0, 7)
                m_high(0, 3)
                m_high(0, 4)
                a_prj(1)
                m_high(0, 5)
                m_silu(0, 8)
                m_high(0, 6)
                m_high(0, 7)
                a_state(1)
                m_high(0, 8)
                a_exp(1)
                m_gate(0)
                a_oh(1)
                a_sTb(1)
                l_xh(0)
                a_combT(1)

            def iteration(i):
                m_silu(i, 0)
                m_silu(i, 1)
                m_high(i, 0)
                m_silu(i, 2)
                l_relu(i - 1)
                m_high(i, 1)
                m_silu(i, 3)
                l_v(i - 1, 0)
                m_silu(i, 4)
                m_silu(i, 5)
                m_silu(i, 6)
                m_silu(i, 7)
                m_silu(i, 8)
                a_xh(i + 1)
                m_high(i, 2)
                l_v(i - 1, 1)
                l_exp(i - 1, 0)
                m_high(i, 3)
                l_v(i - 1, 2)
                l_exp(i - 1, 1)
                m_high(i, 4)
                a_prj(i + 1)
                l_v(i - 1, 3)
                l_exp(i - 1, 2)
                m_high(i, 5)
                m_high(i, 6)
                m_high(i, 7)
                l_exp(i - 1, 3)
                m_high(i, 8)
                a_state(i + 1)
                a_exp(i + 1)
                m_gate(i)
                a_oh(i + 1)
                l_qT(i - 1)
                a_sTb(i + 1)
                l_attT(i - 1)
                a_combT(i + 1)
                l_xh(i)
                l_gate(i - 1)

            def tail():
                m_silu(B - 1, 0)
                m_silu(B - 1, 1)
                m_silu(B - 1, 2)
                l_relu(B - 2)
                l_v(B - 2, 0)
                m_high(B - 1, 0)
                m_silu(B - 1, 3)
                m_silu(B - 1, 4)
                m_high(B - 1, 1)
                m_silu(B - 1, 5)
                m_silu(B - 1, 6)
                m_high(B - 1, 2)
                m_high(B - 1, 3)
                m_silu(B - 1, 7)
                m_high(B - 1, 4)
                l_v(B - 2, 1)
                m_silu(B - 1, 8)
                l_exp(B - 2, 0)
                l_v(B - 2, 2)
                l_exp(B - 2, 1)
                m_high(B - 1, 5)
                m_high(B - 1, 6)
                l_v(B - 2, 3)
                l_exp(B - 2, 2)
                m_high(B - 1, 7)
                l_exp(B - 2, 3)
                m_high(B - 1, 8)
                m_gate(B - 1)
                l_qT(B - 2)
                l_attT(B - 2)
                l_xh(B - 1)
                l_gate(B - 2)
                l_relu(B - 1)
                l_v(B - 1, 0)
                l_v(B - 1, 1)
                l_exp(B - 1, 0)
                l_v(B - 1, 2)
                l_exp(B - 1, 1)
                l_v(B - 1, 3)
                l_exp(B - 1, 2)
                l_exp(B - 1, 3)
                l_qT(B - 1)
                l_attT(B - 1)
                l_gate(B - 1)

            schedule(act, head, iteration, tail)

        @block.vector
        def _(dve):
            v = nc.vector


            def passed():
                dve.sem_inc(s_dve_passed, 1)

            def stats(st, src):
                for t in range(NT):
                    last = v.bn_stats(st[:, t, :], src(t))
                return last

            def aggregate(mv, st):
                for t in range(NT):
                    last = v.bn_aggr(mv[:, t, :], st[:, t, :])
                return last

            def normalise(c, s_rstd, s_xT, s_xn, xn, src, mv, rs):
                dve.wait_ge(s_rstd, c + 1)
                if positive(c):
                    dve.wait_ge(s_xT, c)
                for t in range(NT):
                    last = v.tensor_scalar(xn[:, t, :], src(t), mv[:, t, 0:1], rs[:, t:t + 1], ALU.subtract, ALU.mult)
                last.then_inc(s_xn, 1)

            def x_of(c):
                if isinstance(c, int):
                    return lambda t: xs[:, c, t, :]
                return lambda t: xs[:, bass.ds(c, 1), t, :].rearrange("p o d -> p (o d)")

            def a_stats(c):
                if isinstance(c, int) and c == 0:
                    dve.wait_ge(s_x0_in, 16)
                if isinstance(c, int) and c == 1:
                    dve.wait_ge(s_x_in, 16)
                passed()
                stats(st0, x_of(c)).then_inc(s_bn0, 1)

            def a_aggr(c):
                dve.wait_ge(s_bn0, c + 1)
                if positive(c):
                    dve.wait_ge(s_rstd0, c)
                    dve.wait_ge(s_xn0, c)
                passed()
                aggregate(mv0, st0).then_inc(s_stats0, 1)

            def a_norm(c):
                normalise(c, s_rstd0, s_xT0, s_xn0, xn0, x_of(c), mv0, rs0)

            def a_xl(c):
                dve.wait_ge(s_xh0, c + 1)
                if positive(c * EX):
                    dve.wait_ge(s_up, c * EX)
                v.tensor_tensor(xl0[:, :], A0[:, :], xh0[:, :].bitcast(F32), ALU.subtract).then_inc(s_xl0, 1)

            def a_kvg(c):
                dve.wait_ge(s_kvg_ps, c + 1)
                if positive(c):
                    dve.wait_ge(s_oh_ps, c)
                v.tensor_copy(kvg[:, :, :], A0[:, 0:NT * PR].rearrange("p (t n) -> p t n", t=NT)[:, :, K_ROW:PR]).then_inc(s_kvg_sb, 1)

            def a_wm(c):
                dve.wait_ge(s_wei, c + 1)
                v.tensor_tensor(wm[:, :].rearrange("p (t n) -> p t n", t=NT), A1[:, :].rearrange("p (t n) -> p t n", t=NT),
                                tri.rearrange("p (o n) -> p o n", o=1).broadcast_to([P, NT, P]), ALU.mult).then_inc(s_wm, 1)

            def a_top8(c):
                dve.wait_ge(s_kvg_sb, c + 1)
                if positive(c):
                    dve.wait_ge(s_lsh, c)
                passed()
                for t in range(NT):
                    last = v.max(top8[:, t, :], kvg[:, t, G_COL:G_COL + E])
                last.then_inc(s_top8, 1)

            def a_topi(c):
                dve.wait_ge(s_top8, c + 1)
                if positive(c):
                    dve.wait_ge(s_topf, c)
                passed()
                for t in range(NT):
                    last = v.max_index(topi[:, t, :], top8[:, t, :], kvg[:, t, G_COL:G_COL + E])
                last.then_inc(s_topi, 1)

            def a_onehot(c):
                dve.wait_ge(s_topi, c + 1)
                v.tensor_copy(topf[:, :, :], topi[:, :, 0:2]).then_inc(s_topf, 1)
                dve.wait_ge(s_topf, c + 1)
                if positive(c):
                    dve.wait_ge(s_ohw, c)
                v.tensor_tensor(onehot[:, :, :, :].rearrange("p t k e -> p (t k) e"),
                                cst[:, C_IOTA:C_IOTA + E].rearrange("p (o e) -> p o e", o=1).broadcast_to([P, NT * 2, E]),
                                topf[:, :, :].rearrange("p t (k o) -> p (t k) o", o=1).broadcast_to([P, NT * 2, E]),
                                ALU.is_equal).then_inc(s_onehot, 1)

            def a_tot(c):
                dve.wait_ge(s_esh, c + 1)
                v.tensor_reduce(tot[:, :], esh[:, :, :], AX_X, ALU.add).then_inc(s_tot, 1)

            def a_den(c):
                dve.wait_ge(s_e12, c + 1)
                dve.wait_ge(s_tot, c + 1)
                v.scalar_tensor_tensor(den[:, :], tot[:, :], TINY, e12[:, :], ALU.mult, ALU.add).then_inc(s_den, 1)
                dve.wait_ge(s_den, c + 1)
                if positive(c):
                    dve.wait_ge(s_w12, c)
                v.reciprocal(rden[:, :], den[:, :]).then_inc(s_rden, 1)

            def a_ohs(c):
                dve.wait_ge(s_oh_r, c + 1)
                if positive(c):
                    dve.wait_ge(s_sT_ps, c)
                v.scalar_tensor_tensor(oh_s[:, :], oh_r[:, :].bitcast(F32), cst[0:V3, C_M24:C_M24 + 1], A0[0:V3, :],
                                       ALU.mult, ALU.add).then_inc(s_oh_s, 1)

            def m_scale(c, k):
                dve.wait_ge(s_silu, c * EX + k + 1)
                dve.wait_ge(s_cbc, c * E + k)
                if positive(c * EX + k - NC + 1):
                    dve.wait_ge(s_act_l, c * EX + k - NC + 1)
                    dve.wait_ge(s_act_h, c * EX + k - NC + 1)
                v.tensor_tensor(act_c[k % NC][:, :], act_s[k][:, :], CB[:, :], ALU.mult).then_inc(s_scaled, 1)

            def m_pT(c):
                dve.wait_ge(s_g0, c + 1)
                dve.wait_ge(s_sT_sb, c + 1)
                if positive(c):
                    dve.wait_ge(s_pTT, c)
                v.tensor_tensor(pT[:, :], g0T[:, :], sTb[:, :], ALU.mult).then_inc(s_pT, 1)

            def m_x1(c):
                dve.wait_ge(s_pTT, c + 1)
                x_c = xs[:, c] if isinstance(c, int) else xs[:, bass.ds(c, 1)].rearrange("p o t d -> p (o t) d")
                v.tensor_tensor(x_c, Y[:, :].rearrange("p (t d) -> p t d", t=NT), x_c, ALU.add).then_inc(s_x1, 1)

            def l_stats(c):
                dve.wait_ge(s_x1, c + 1)
                passed()
                stats(st1, x_of(c)).then_inc(s_bn1, 1)

            def l_aggr(c):
                dve.wait_ge(s_bn1, c + 1)
                if positive(c):
                    dve.wait_ge(s_rstd1, c)
                    dve.wait_ge(s_xn1, c)
                passed()
                aggregate(mv1, st1).then_inc(s_stats1, 1)

            def l_norm(c):
                normalise(c, s_rstd1, s_xT1, s_xn1, xn1, x_of(c), mv1, rs1)

            def l_xl(c):
                dve.wait_ge(s_xh1, c + 1)
                v.tensor_tensor(xl1[:, :], L0[:, :], xh1[:, :].bitcast(F32), ALU.subtract).then_inc(s_xl1, 1)

            def l_max(c, t):
                dve.wait_ge(s_v_sb, c * NT + t + 1)
                z = [L0, L1][t % 2][:, 0:2 * C].rearrange("p (h d) -> p h d", d=HS)
                if t == 0:
                    if positive(c):
                        dve.wait_ge(s_qT_ps, c)
                    if positive(c):
                        dve.wait_ge(s_att, c)
                v.tensor_reduce(qk_max[:, t, :], z, AX_X, ALU.max).then_inc(s_qk_max, 1)

            def l_subtract(c, t):
                z = [L0, L1][t % 2][:, 0:2 * C].rearrange("p (h d) -> p h d", d=HS)
                dve.wait_ge(s_qk_max, c * NT + t + 1)
                v.tensor_tensor(qk[:, t, :].rearrange("p (h d) -> p h d", d=HS), z,
                                qk_max[:, t, :].rearrange("p (h o) -> p h o", o=1).broadcast_to([P, 2 * NH, HS]),
                                ALU.subtract).then_inc(s_qk_sub, 1)

            def l_total(c):
                dve.wait_ge(s_qk_exp, c * NT + NT)
                a = qk[:, :, :].rearrange("p t (h d) -> p (t h) d", d=HS)
                v.tensor_reduce(qk_sum[:, :], a, AX_X, ALU.add).then_inc(s_qk_sum, 1)

            def l_recip(c):
                dve.wait_ge(s_qk_sum, c + 1)
                v.reciprocal(qk_rs[:, :], qk_sum[:, :]).then_inc(s_qk_rs, 1)

            def l_softmax(c):
                a = qk[:, :, :].rearrange("p t (h d) -> p (t h) d", d=HS)
                dve.wait_ge(s_qk_rs, c + 1)
                v.tensor_tensor(a, a, qk_rs[:, :].rearrange("p (h o) -> p h o", o=1).broadcast_to([P, NT * 2 * NH, HS]),
                                ALU.mult).then_inc(s_qk_sm, 1)

            def l_ctx(c):
                dve.wait_ge(s_ctx, c + 1)
                if positive(c):
                    dve.wait_ge(s_nd, c)
                v.tensor_tensor(ctxn[:, 0:C], L0[:, 0:C], cst[:, C_BLK:C_BLK + C], ALU.mult)
                v.tensor_scalar(ctxn[:, C:C + NH], cst[:, C_IND:C_IND + NH], L0[:, C:C + 1], None, ALU.mult).then_inc(s_ctx_sb, 1)

            def l_dinv(c):
                dve.wait_ge(s_nd, c + 1)
                if positive(c):
                    dve.wait_ge(s_attT_ps, c)
                for b, z in enumerate((L0, L1)):
                    zz = z[:, 0:2 * (C + NH)].rearrange("p (t n) -> p t n", t=2)
                    last = v.reciprocal(dinv[:, 2 * b:2 * b + 2, :], zz[:, :, C:C + NH])
                last.then_inc(s_dinv, 1)

            def l_attm(c):
                dve.wait_ge(s_dinv, c + 1)
                for b, z in enumerate((L0, L1)):
                    for u in range(2):
                        t = 2 * b + u
                        o = u * (C + NH)
                        last = v.tensor_tensor(att[:, t, :].rearrange("p (h d) -> p h d", d=HS),
                                               z[:, o:o + C].rearrange("p (h d) -> p h d", d=HS),
                                               dinv[:, t, :].rearrange("p (h o) -> p h o", o=1).broadcast_to([P, NH, HS]), ALU.mult)
                last.then_inc(s_att_m, 1)

            def l_addq(c):
                dve.wait_ge(s_att_m, c + 1)
                v.tensor_tensor(att[:, :, :], att[:, :, :], qk[:, :, 0:C], ALU.add).then_inc(s_att, 1)

            def l_top8(c):
                dve.wait_ge(s_lg, c + 1)
                passed()
                for t in range(NT):
                    last = v.max(top8b[:, t, :], L1[:, t * E:(t + 1) * E])
                last.then_inc(s_top8b, 1)

            def l_topi(c):
                dve.wait_ge(s_top8b, c + 1)
                passed()
                for t in range(NT):
                    last = v.max_index(topib[:, t, :], top8b[:, t, :], L1[:, t * E:(t + 1) * E])
                last.then_inc(s_topib, 1)

            def l_mask(c):
                dve.wait_ge(s_topib, c + 1)
                if positive(c):
                    dve.wait_ge(s_mask, c)
                v.tensor_copy(topfb[:, :], topib[:, :, 0]).then_inc(s_topfb, 1)
                dve.wait_ge(s_topfb, c + 1)
                v.tensor_tensor(mask[:, :, :], cst[:, C_IOTA:C_IOTA + E].rearrange("p (o e) -> p o e", o=1).broadcast_to([P, NT, E]),
                                topfb[:, :].rearrange("p (t o) -> p t o", o=1).broadcast_to([P, NT, E]), ALU.is_equal).then_inc(s_mask, 1)

            def l_prod(c, n):
                t, half = n // 2, n % 2
                dve.wait_ge(s_ex, c * 2 * NT + n + 1)
                if n == 0:
                    dve.wait_ge(s_mask, c + 1)
                if half == 0:
                    if t >= 2:
                        if positive(c * NT + t - 1):
                            dve.wait_ge(s_sum4, c * NT + t - 1)
                    else:
                        if positive(c * NT):
                            dve.wait_ge(s_sum4, c * NT)
                v.tensor_tensor(prod[t % 2][:, half], UP[n % 2][:, :].rearrange("p (e d) -> p e d", d=C),
                                mask[:, t, half * 4:half * 4 + 4].rearrange("p (e o) -> p e o", o=1).broadcast_to([P, 4, C]),
                                ALU.mult).then_inc(s_prod, 1)

            def l_sg(c):
                dve.wait_ge(s_s1, c + 1)
                dve.wait_ge(s_g1, c + 1)
                if positive(c):
                    dve.wait_ge(s_fin, c)
                v.tensor_tensor(sg[:, :, :], L1[:, :].rearrange("p (t d) -> p t d", t=NT), g1[:, :, :], ALU.mult).then_inc(s_sg, 1)

            def split(h, l, w):
                v.tensor_copy(h[:, :], w[:, :]).then_inc(s_w_split, 1)
                nsplit[0] += 1
                dve.wait_ge(s_w_split, nsplit[0])
                return v.tensor_tensor(l[:, :], w[:, :], h[:, :].bitcast(F32), ALU.subtract)

            def stack(s, r, w, m):
                v.tensor_copy(r[:, :], w[:, :]).then_inc(s_w_split, 1)
                nsplit[0] += 1
                dve.wait_ge(s_w_split, nsplit[0])
                v.scalar_tensor_tensor(s[:, :], r[:, :].bitcast(F32), m, w[:, :], ALU.mult, ALU.add).then_inc(s_w_split, 1)
                nsplit[0] += 1

            nsplit = [0]

            def wpr_parts():
                dve.wait_ge(s_proj_in, 16 * 4)
                split(wpr_h, wpr_l, wpr)

            def wsum_parts():
                dve.wait_ge(s_consts_ready, 2)
                stack(wsum_s, wsum_r, wsum, cst[0:V3, C_MW:C_MW + 1])

            def wdn_parts():
                dve.wait_ge(s_down_in, 16 * 2)
                stack(bdn_s, bdn_r, bdn, cst[0:3 * E, C_M24:C_M24 + 1])
                split(wdn_h, wdn_l, wdn).then_inc(s_wdn_ready, 1)

            def late_parts():
                dve.wait_ge(s_late_in, 16 * 6)
                stack(row_s, row_r, row, cst[0:2, C_M2:C_M2 + 1])
                v.memset(vv[:, :, C:C + 1], 1.0)
                v.memset(hT[F1:F1 + 1, :], 1.0)
                split(wqkv_h, wqkv_l, wqkv)
                split(wr1_h, wr1_l, wr1)
                split(wex_h, wex_l, wex).then_inc(s_l1_ready, 1)

            def head():
                a_stats(0)
                a_aggr(0)
                wpr_parts()
                a_norm(0)
                a_xl(0)
                wdn_parts()
                wsum_parts()
                a_kvg(0)
                a_wm(0)
                a_top8(0)
                a_topi(0)
                a_onehot(0)
                a_ohs(0)
                a_tot(0)
                a_den(0)
                a_stats(1)
                a_aggr(1)
                m_scale(0, 1)
                a_norm(1)
                m_scale(0, 2)
                m_scale(0, 3)
                a_xl(1)
                m_scale(0, 4)
                m_scale(0, 5)
                m_scale(0, 6)
                a_kvg(1)
                m_scale(0, 7)
                a_top8(1)
                a_wm(1)
                m_scale(0, 8)
                late_parts()
                m_pT(0)
                a_topi(1)
                a_onehot(1)
                m_x1(0)
                l_stats(0)
                l_aggr(0)
                a_ohs(1)
                a_tot(1)
                a_den(1)
                l_norm(0)
                l_xl(0)

            def iteration(i):
                m_scale(i, 1)
                a_stats(i + 1)
                a_aggr(i + 1)
                m_scale(i, 2)
                a_norm(i + 1)
                l_top8(i - 1)
                l_max(i - 1, 0)
                m_scale(i, 3)
                l_topi(i - 1)
                l_subtract(i - 1, 0)
                l_max(i - 1, 1)
                m_scale(i, 4)
                l_mask(i - 1)
                a_xl(i + 1)
                l_subtract(i - 1, 1)
                l_max(i - 1, 2)
                m_scale(i, 5)
                l_prod(i - 1, 0)
                l_subtract(i - 1, 2)
                m_scale(i, 6)
                l_max(i - 1, 3)
                m_scale(i, 7)
                a_kvg(i + 1)
                a_top8(i + 1)
                l_subtract(i - 1, 3)
                m_scale(i, 8)
                l_prod(i - 1, 1)
                l_total(i - 1)
                a_wm(i + 1)
                l_recip(i - 1)
                a_topi(i + 1)
                l_prod(i - 1, 2)
                l_softmax(i - 1)
                a_onehot(i + 1)
                l_prod(i - 1, 3)
                m_pT(i)
                a_ohs(i + 1)
                a_tot(i + 1)
                l_prod(i - 1, 4)
                a_den(i + 1)
                m_x1(i)
                l_ctx(i - 1)
                l_stats(i)
                l_prod(i - 1, 5)
                l_dinv(i - 1)
                l_attm(i - 1)
                l_addq(i - 1)
                l_aggr(i)
                l_prod(i - 1, 6)
                l_prod(i - 1, 7)
                l_norm(i)
                l_xl(i)
                l_sg(i - 1)

            def tail():
                m_scale(B - 1, 1)
                m_scale(B - 1, 2)
                l_top8(B - 2)
                l_max(B - 2, 0)
                l_topi(B - 2)
                l_subtract(B - 2, 0)
                m_scale(B - 1, 3)
                m_scale(B - 1, 4)
                m_scale(B - 1, 5)
                l_max(B - 2, 1)
                l_mask(B - 2)
                l_subtract(B - 2, 1)
                m_scale(B - 1, 6)
                l_prod(B - 2, 0)
                l_max(B - 2, 2)
                m_scale(B - 1, 7)
                l_subtract(B - 2, 2)
                l_max(B - 2, 3)
                l_subtract(B - 2, 3)
                m_scale(B - 1, 8)
                l_prod(B - 2, 1)
                l_total(B - 2)
                l_recip(B - 2)
                l_prod(B - 2, 2)
                l_prod(B - 2, 3)
                l_softmax(B - 2)
                l_prod(B - 2, 4)
                m_pT(B - 1)
                l_prod(B - 2, 5)
                l_ctx(B - 2)
                m_x1(B - 1)
                l_stats(B - 1)
                l_dinv(B - 2)
                l_aggr(B - 1)
                l_attm(B - 2)
                l_prod(B - 2, 6)
                l_addq(B - 2)
                l_prod(B - 2, 7)
                l_norm(B - 1)
                l_xl(B - 1)
                l_sg(B - 2)
                l_top8(B - 1)
                l_max(B - 1, 0)
                l_topi(B - 1)
                l_subtract(B - 1, 0)
                l_max(B - 1, 1)
                l_mask(B - 1)
                l_subtract(B - 1, 1)
                l_prod(B - 1, 0)
                l_max(B - 1, 2)
                l_prod(B - 1, 1)
                l_subtract(B - 1, 2)
                l_max(B - 1, 3)
                l_prod(B - 1, 2)
                l_subtract(B - 1, 3)
                l_prod(B - 1, 3)
                l_total(B - 1)
                l_prod(B - 1, 4)
                l_recip(B - 1)
                l_softmax(B - 1)
                l_prod(B - 1, 5)
                l_prod(B - 1, 6)
                l_ctx(B - 1)
                l_prod(B - 1, 7)
                l_dinv(B - 1)
                l_attm(B - 1)
                l_addq(B - 1)
                l_sg(B - 1)

            schedule(dve, head, iteration, tail)

        @block.gpsimd
        def _(pool):
            g = nc.gpsimd


            def passed():
                pool.sem_inc(s_pool_passed, 1)

            def rstd(c, s_stats, s_ve, s_xn, s_rstd, mv, ve, rs):
                pool.wait_ge(s_stats, c + 1)
                passed()
                g.tensor_scalar(ve[:, :], mv[:, :, 1], EPS, 1.0, ALU.add, ALU.mult).then_inc(s_ve, 1)
                pool.wait_ge(s_ve, c + 1)
                if positive(c):
                    pool.wait_ge(s_xn, c)
                g.tensor_tensor(rs[:, :], ve[:, :], mhalf[:, :], ALU.pow).then_inc(s_rstd, 1)

            def a_rstd(c):
                rstd(c, s_stats0, s_ve0, s_xn0, s_rstd0, mv0, ve0, rs0)

            def l_rstd(c):
                rstd(c, s_stats1, s_ve1, s_xn1, s_rstd1, mv1, ve1, rs1)

            def a_lsh(c):
                pool.wait_ge(s_top8, c + 1)
                if positive(c):
                    pool.wait_ge(s_esh, c)
                g.tensor_tensor(lsh[:, :, :], top8[:, :, :], top8[:, :, 0:1].broadcast_to([P, NT, E]), ALU.subtract).then_inc(s_lsh, 1)

            def a_e12(c):
                pool.wait_ge(s_esh, c + 1)
                if positive(c):
                    pool.wait_ge(s_den, c)
                g.tensor_tensor(e12[:, :], esh[:, :, 0], esh[:, :, 1], ALU.add).then_inc(s_e12, 1)

            def a_w12(c):
                pool.wait_ge(s_rden, c + 1)
                g.tensor_tensor(w12[:, :, :], esh[:, :, 0:2], rden[:, :].rearrange("p (t o) -> p t o", o=1).broadcast_to([P, NT, 2]),
                                ALU.mult).then_inc(s_w12, 1)
                pool.wait_ge(s_w12, c + 1)
                pool.wait_ge(s_onehot, c + 1)
                g.tensor_tensor(ohw[:, :, :, :].rearrange("p t k e -> p (t k) e"), onehot[:, :, :, :].rearrange("p t k e -> p (t k) e"),
                                w12[:, :, :].rearrange("p t (k o) -> p (t k) o", o=1).broadcast_to([P, NT * 2, E]),
                                ALU.mult).then_inc(s_ohw, 1)

            def a_comb(c):
                pool.wait_ge(s_ohw, c + 1)
                g.tensor_tensor(comb[:, :, :], ohw[:, :, 0, :], ohw[:, :, 1, :], ALU.add).then_inc(s_comb, 1)
                pool.wait_ge(s_comb, c + 1)
                if positive(c):
                    pool.wait_ge(s_combT_ps, c)
                passed()
                g.tensor_copy(comb3[:, :, 0:E], comb[:, :, :])
                g.tensor_copy(comb3[:, :, 2 * E:3 * E], comb[:, :, :]).then_inc(s_combh, 1)
                pool.wait_ge(s_combh, c + 1)
                g.tensor_tensor(comb3[:, :, E:2 * E], comb[:, :, :], comb3[:, :, 0:E].bitcast(F32), ALU.subtract).then_inc(s_comb3, 1)

            def m_low(c, k):
                pool.wait_ge(s_act_h, c * EX + k + 1)
                if positive(c * EX + k - NR + 1):
                    pool.wait_ge(s_down, c * EX + k - NR + 1)
                src = act_s[0] if k == 0 else act_c[k % NC]
                g.tensor_tensor(act_l[k % NR][:, :], src[:, :], act_h[k % NR][:, :].bitcast(F32), ALU.subtract).then_inc(s_act_l, 1)

            def l_sum(c, t):
                pool.wait_ge(s_prod, c * 2 * NT + 2 * t + 2)
                b = t % 2
                if t >= 1:
                    if positive(c * NT + t - 1):
                        pool.wait_ge(s_sum2, c * NT + t - 1)
                g.tensor_tensor(sum4[b][:, :, :], prod[b][:, 0], prod[b][:, 1], ALU.add).then_inc(s_sum4, 1)
                pool.wait_ge(s_sum4, c * NT + t + 1)
                if t >= 1:
                    if positive(c * NT + t - 1):
                        pool.wait_ge(s_sel1, c * NT + t - 1)
                g.tensor_tensor(sum2[b][:, :, :], sum4[b][:, 0:2, :], sum4[b][:, 2:4, :], ALU.add).then_inc(s_sum2, 1)
                pool.wait_ge(s_sum2, c * NT + t + 1)
                if t == 0:
                    if positive(c):
                        pool.wait_ge(s_g1, c)
                g.tensor_tensor(sel1[:, t, :], sum2[b][:, 0, :], sum2[b][:, 1, :], ALU.add).then_inc(s_sel1, 1)

            def l_fin(c):
                pool.wait_ge(s_sg, c + 1)
                x_c = xs[:, c] if isinstance(c, int) else xs[:, bass.ds(c, 1)].rearrange("p o t d -> p (o t) d")
                g.tensor_tensor(x_c, x_c, sg[:, :, :], ALU.add).then_inc(s_fin, 1)

            def half_power():
                g.memset(mhalf[:, :], -0.5).then_inc(s_memset_ready, 1)
                pool.wait_ge(s_memset_ready, 1)

            def wup_low():
                pool.wait_ge(s_wup_high, 1)
                g.tensor_tensor(wup_l[:, :], wup[:, :], wup_h[:, :].bitcast(F32), ALU.subtract).then_inc(s_wup_ready, 1)


            def head():
                half_power()
                a_rstd(0)
                wup_low()
                a_lsh(0)
                a_e12(0)
                a_w12(0)
                a_comb(0)
                a_rstd(1)
                m_low(0, 0)
                m_low(0, 1)
                m_low(0, 2)
                m_low(0, 3)
                m_low(0, 4)
                m_low(0, 5)
                m_low(0, 6)
                a_lsh(1)
                m_low(0, 7)
                m_low(0, 8)
                a_e12(1)
                l_rstd(0)
                a_w12(1)
                a_comb(1)

            def iteration(i):
                a_rstd(i + 1)
                m_low(i, 0)
                m_low(i, 1)
                m_low(i, 2)
                m_low(i, 3)
                m_low(i, 4)
                m_low(i, 5)
                m_low(i, 6)
                m_low(i, 7)
                a_lsh(i + 1)
                m_low(i, 8)
                l_sum(i - 1, 0)
                a_e12(i + 1)
                l_sum(i - 1, 1)
                a_w12(i + 1)
                a_comb(i + 1)
                l_sum(i - 1, 2)
                l_rstd(i)
                l_sum(i - 1, 3)
                l_fin(i - 1)

            def tail():
                m_low(B - 1, 0)
                m_low(B - 1, 1)
                m_low(B - 1, 2)
                m_low(B - 1, 3)
                m_low(B - 1, 4)
                m_low(B - 1, 5)
                m_low(B - 1, 6)
                m_low(B - 1, 7)
                m_low(B - 1, 8)
                l_sum(B - 2, 0)
                l_sum(B - 2, 1)
                l_sum(B - 2, 2)
                l_rstd(B - 1)
                l_sum(B - 2, 3)
                l_sum(B - 1, 0)
                l_sum(B - 1, 1)
                l_fin(B - 2)
                l_sum(B - 1, 2)
                l_sum(B - 1, 3)
                l_fin(B - 1)

            schedule(pool, head, iteration, tail)


def constants():
    c = np.zeros((P, NCONST), np.float32)
    r = np.arange(P)
    c[:, C_ID:C_ID + P] = np.eye(P)
    c[:, C_TRI:C_TRI + P] = r[:, None] <= r[None, :]
    c[:, C_BLK:C_BLK + C] = r[:, None] // HS == r[None, :] // HS
    c[:, C_IND:C_IND + NH] = r[:, None] // HS == np.arange(NH)[None, :]
    c[:, C_FOLD:C_FOLD + V3] = r[:, None] % HS == np.arange(V3)[None, :] % HS
    c[:, C_IOTA:C_IOTA + E] = np.arange(E)[None, :]
    c[0, C_M2] = 0.0
    c[1, C_M2] = -1.0
    c[2 * E:3 * E, C_M24] = -1.0
    c[HS:2 * HS, C_MW] = -1.0
    c[:, C_ONE:C_ONE + P] = 1.0
    return c


def selectors():
    s = np.zeros((2 * E, E * C), np.float32)
    for e in range(E):
        s[[e, E + e], e * C:(e + 1) * C] = 1.0
    return s


def kernel(**inputs):
    import concourse.bacc as bacc
    from concourse.bass_utils import run_bass_kernel_spmd

    a = {k: np.asarray(v) for k, v in inputs.items()}
    z = lambda *s: np.zeros(s, np.float32)

    w_pr, b_pr = z(C, PR), z(P)
    for i, at in ((0, Q_ROW), (1, K_ROW), (2, V_ROW), (2, V_ROW + HS), (2, V_ROW + 2 * HS)):
        w_pr[:, at:at + HS] = a["L0_attn_qkv_w"][i * HS:(i + 1) * HS].T
        b_pr[at:at + HS] = a["L0_attn_qkv_b"][i * HS:(i + 1) * HS]
    w_pr[:, G_ROW:G_ROW + E] = a["L0_ffn_gate_w"].T

    def side_by_side(stack, shared):
        return np.concatenate([stack.transpose(1, 0, 2).reshape(C, -1), shared], axis=1)

    vecs = z(P, NVEC)
    vecs[:, V_UP:V_UP + E] = a["L0_ffn_up_b"].T
    vecs[:, V_UP + E] = a["L0_ffn_sh_up_b"]
    vecs[:, V_PR] = b_pr
    vecs[:, V_PROJ] = a["L0_attn_proj_b"]
    vecs[:, V_SHD] = a["L0_ffn_sh_down_b"]
    vecs[0:F1, V_B1] = a["L1_ffn_b1"]
    rows1 = np.concatenate([a["L1_attn_bq"], a["L1_attn_bk"], a["L1_attn_bv"], a["L1_ffn_expert_b"].reshape(-1)]
                           + [a["L1_attn_bp"]] * NT)
    arrays = {
        "x": a["L0_attn_ids"], "consts": constants(), "sels": selectors(), "w_pr": w_pr,
        "w_up": side_by_side(a["L0_ffn_up_w"], a["L0_ffn_sh_up_w"]),
        "w_dn": side_by_side(a["L0_ffn_down_w"], a["L0_ffn_sh_down_w"]),
        "w_pj": a["L0_attn_proj_w"].T, "b_dn": np.concatenate([a["L0_ffn_down_b"]] * 3),
        "vecs": vecs, "rows": np.stack([rows1, rows1]),
        "w_qkv": np.concatenate([a["L1_attn_Wq"].T, a["L1_attn_Wk"].T, a["L1_attn_Wv"].T], axis=1),
        "w_ex": a["L1_ffn_expert_W"].transpose(1, 0, 2).reshape(C, -1),
        "w_p1": a["L1_attn_Wp"].T, "w_r1": a["L1_ffn_W1"],
        "w_r2": np.concatenate([a["L1_ffn_W2"], a["L1_ffn_b2"][None]]),
    }
    arrays = {k: np.ascontiguousarray(v) for k, v in arrays.items()}
    nc = bacc.Bacc("TRN2", target_bir_lowering=False, num_devices=1)
    aps = {k: nc.dram_tensor(k, v.shape, mybir.dt.from_np(v.dtype), kind="ExternalInput").ap() for k, v in arrays.items()}
    out = nc.dram_tensor("out", (B, T, C), F32, kind="ExternalOutput").ap()
    build_program(nc, out=out, **aps)
    r = run_bass_kernel_spmd(nc, [arrays], core_ids=[0])
    return r.results[0]["out"]
```
